# Optimizing a Trainium2 kernel written in Bass

```python
import numpy as np
import jax
import jax.numpy as jnp

def _softmax(x, axis=-1):
    return jax.nn.softmax(x, axis=axis)

def _gelu(x):
    return jax.nn.gelu(x, approximate=True)

def _silu(x):
    return jax.nn.silu(x)

def _sigmoid(x):
    return jax.nn.sigmoid(x)

def _layernorm(x, axis=-1, eps=1e-05):
    m = jnp.mean(x, axis=axis, keepdims=True)
    v = jnp.var(x, axis=axis, keepdims=True)
    return (x - m) / jnp.sqrt(v + eps)

def _scatter_add(tgt, idx, src, axis=0):
    return tgt.at[idx].add(src)

def _segment_sum(src, seg, n):
    return jax.ops.segment_sum(src, seg, n)
kernel_name = 'mk_adaln_d1_jaxref_r4_999bcd'

def setup_inputs(seed: int=0):
    np.random.seed(seed)
    _w = jnp.asarray

    def _L0_attn_setup():
        import jax, jax.numpy as jnp
        import numpy as np
        E = 256
        H = 16
        D = E // H
        WIN = 64
        STRIDE = 128
        G = 1
        B = 2
        L = 4097
        key = jax.random.key(seed)
        ks = jax.random.split(key, 9)
        s = 0.02
        return {'hidden_states': jax.random.normal(ks[0], (B, L, E), jnp.float32), 'Wq': jax.random.normal(ks[1], (E, E), jnp.float32) * s, 'bq': jnp.zeros((E,), jnp.float32), 'Wk': jax.random.normal(ks[2], (E, E), jnp.float32) * s, 'bk': jnp.zeros((E,), jnp.float32), 'Wv': jax.random.normal(ks[3], (E, E), jnp.float32) * s, 'bv': jnp.zeros((E,), jnp.float32), 'Wo': jax.random.normal(ks[4], (E, E), jnp.float32) * s, 'bo': jnp.zeros((E,), jnp.float32)}
    _L0_attn_in = _L0_attn_setup()

    def _L0_ffn_setup():
        import jax, jax.numpy as jnp
        import numpy as np

        def _binarize(w):
            alpha = jax.lax.stop_gradient(jnp.mean(jnp.abs(w), axis=1, keepdims=True))
            bw = alpha * jnp.sign(w)
            return w + jax.lax.stop_gradient(bw - w)
        key = jax.random.key(seed)
        k1, k2, k3, k4, k5 = jax.random.split(key, 5)
        D, H = (256, 1024)
        x = jax.random.normal(k1, (64, 196, D), dtype=jnp.float32)
        w1 = jax.random.normal(k2, (H, D), dtype=jnp.float32) * 0.02
        b1 = jax.random.normal(k3, (H,), dtype=jnp.float32) * 0.02
        w2 = jax.random.normal(k4, (D, H), dtype=jnp.float32) * 0.02
        b2 = jax.random.normal(k5, (D,), dtype=jnp.float32) * 0.02
        return {'x': x, 'w1': w1, 'b1': b1, 'w2': w2, 'b2': b2}
    _L0_ffn_in = _L0_ffn_setup()
    _L0_c = _w((lambda *s: np.random.randn(*s).astype(np.float32) * 0.05)(8, 256))
    _L0_wmod = _w((lambda *s: np.random.randn(*s).astype(np.float32) * 0.05)(256, 6 * 256) * 256 ** (-0.5))
    _d = {'L0_attn_hidden_states': _L0_attn_in['hidden_states'], 'L0_attn_Wq': _L0_attn_in['Wq'], 'L0_attn_bq': _L0_attn_in['bq'], 'L0_attn_Wk': _L0_attn_in['Wk'], 'L0_attn_bk': _L0_attn_in['bk'], 'L0_attn_Wv': _L0_attn_in['Wv'], 'L0_attn_bv': _L0_attn_in['bv'], 'L0_attn_Wo': _L0_attn_in['Wo'], 'L0_attn_bo': _L0_attn_in['bo'], 'L0_ffn_w1': _L0_ffn_in['w1'], 'L0_ffn_b1': _L0_ffn_in['b1'], 'L0_ffn_w2': _L0_ffn_in['w2'], 'L0_ffn_b2': _L0_ffn_in['b2'], 'L0_c': _L0_c, 'L0_wmod': _L0_wmod}
    _x0 = _d['L0_attn_hidden_states']
    _d['L0_attn_hidden_states'] = jax.random.normal(jax.random.fold_in(jax.random.key(seed), 1), (8, 1024, 256), dtype=_x0.dtype)
    del _x0
    return _d

def reference(L0_attn_hidden_states, L0_attn_Wq, L0_attn_bq, L0_attn_Wk, L0_attn_bk, L0_attn_Wv, L0_attn_bv, L0_attn_Wo, L0_attn_bo, L0_ffn_w1, L0_ffn_b1, L0_ffn_w2, L0_ffn_b2, L0_c, L0_wmod):

    def _L0_attn_ref(hidden_states, Wq, bq, Wk, bk, Wv, bv, Wo, bo):
        import jax, jax.numpy as jnp
        import numpy as np
        E = 256
        H = 16
        D = E // H
        WIN = 64
        STRIDE = 128
        G = 1
        B = 2
        L = 4097
        b, seq_len, e = hidden_states.shape
        scale = 1.0 / jnp.sqrt(jnp.asarray(D, hidden_states.dtype))
        q = (hidden_states @ Wq + bq).reshape(b, seq_len, H, D)
        k = (hidden_states @ Wk + bk).reshape(b, seq_len, H, D)
        v = (hidden_states @ Wv + bv).reshape(b, seq_len, H, D)
        qg = q[:, :G]
        gw = jnp.einsum('bghd,bshd->bhgs', qg, k) * scale
        gp = jax.nn.softmax(gw, axis=-1)
        gctx = jnp.einsum('bhgs,bshd->bghd', gp, v).reshape(b, G, e)
        ql, kl, vl = (q[:, G:], k[:, G:], v[:, G:])
        Lc = seq_len - G
        num_windows = max(1, (Lc - WIN) // STRIDE + 1)
        starts = jnp.arange(num_windows) * STRIDE
        widx = starts[:, None] + jnp.arange(WIN)
        qw = ql[:, widx]
        kw = kl[:, widx]
        vw = vl[:, widx]
        aw = jnp.einsum('bwqhd,bwkhd->bwhqk', qw, kw) * scale
        ap = jax.nn.softmax(aw, axis=-1)
        ctx = jnp.einsum('bwhqk,bwkhd->bwqhd', ap, vw)
        ctx = ctx.reshape(b, num_windows * WIN, e)
        flat = widx.reshape(-1)
        local = jnp.zeros((b, Lc, e), hidden_states.dtype).at[:, flat].add(ctx)
        counts = jnp.zeros((Lc,), hidden_states.dtype).at[flat].add(1.0)
        counts = jnp.maximum(counts, 1.0)
        local = local / counts[None, :, None]
        out = jnp.concatenate([gctx, local], axis=1)
        return out @ Wo + bo

    def _L0_ffn_ref(x, w1, b1, w2, b2):
        import jax, jax.numpy as jnp
        import numpy as np

        def _binarize(w):
            alpha = jax.lax.stop_gradient(jnp.mean(jnp.abs(w), axis=1, keepdims=True))
            bw = alpha * jnp.sign(w)
            return w + jax.lax.stop_gradient(bw - w)
        bw1 = _binarize(w1)
        h = jnp.einsum('bsd,hd->bsh', x, bw1) + b1
        h = jax.nn.gelu(h, approximate=False)
        bw2 = _binarize(w2)
        out = jnp.einsum('bsh,dh->bsd', h, bw2) + b2
        return out
    x = L0_attn_hidden_states
    mod = (_silu(L0_c) @ L0_wmod).reshape(L0_c.shape[0], 6, 1, -1)
    sa, ca, ga, sb, cb, gb = (mod[:, 0], mod[:, 1], mod[:, 2], mod[:, 3], mod[:, 4], mod[:, 5])
    ga = (2 * (ga >= 0) - 1) * jnp.maximum(jnp.abs(ga), 0.25)
    gb = (2 * (gb >= 0) - 1) * jnp.maximum(jnp.abs(gb), 0.25)
    h = _layernorm(x, axis=-1) * (1 + ca) + sa
    x = x + ga * _L0_attn_ref(h, L0_attn_Wq, L0_attn_bq, L0_attn_Wk, L0_attn_bk, L0_attn_Wv, L0_attn_bv, L0_attn_Wo, L0_attn_bo)
    h = _layernorm(x, axis=-1) * (1 + cb) + sb
    x = x + gb * _L0_ffn_ref(h, L0_ffn_w1, L0_ffn_b1, L0_ffn_w2, L0_ffn_b2)
    return x

_drawn_inputs = setup_inputs


def setup_inputs(seed=0):
    import zlib

    import numpy as np

    out = dict(_drawn_inputs(seed))
    spreads = {'L0_attn_bq': (0.0, 0.8),
     'L0_attn_bk': (0.0, 0.8),
     'L0_attn_bv': (0.0, 0.8),
     'L0_attn_bo': (0.0, 0.331)}
    factors = {'L0_attn_Wq': 8.0,
     'L0_attn_Wk': 8.0,
     'L0_attn_Wv': 8.0,
     'L0_attn_Wo': 8.0,
     'L0_ffn_w1': 3.301,
     'L0_ffn_b1': 8.0,
     'L0_ffn_w2': 3.201,
     'L0_ffn_b2': 8.0}
    for name, (base, spread) in spreads.items():
        noise = np.random.default_rng([zlib.crc32(name.encode()), seed]).standard_normal(out[name].shape)
        drawn = base * np.exp(spread * noise) if base else spread * noise
        out[name] = jnp.asarray(drawn.astype(out[name].dtype))
    for name, factor in factors.items():
        out[name] = (out[name] * factor).astype(out[name].dtype)
    return out
```

```python
from contextlib import ExitStack

import concourse.bass as bass
from concourse import mybir

ALU = mybir.AluOpType
ACT = mybir.ActivationFunctionType
AX = mybir.AxisListType.X
F32 = mybir.dt.float32
F32R = mybir.dt.float32r

P = 128
NB = 8
L = 1024
E = 256
EC = E // P
H = 16
D = E // H
WIN = 64
PAIRS = 4
HALF = L // 2
F = 1024
FC = F // P
ITEMS = 8
SCALE = float(D) ** -0.5
EPS = 1e-5
DVE_BEFORE, DVE_FIRST, DVE_STEPS = 16, 28, 29
F_BEFORE, F_STEPS = 4, 6
SA, CA, SB, CB = range(4)
MOD_BLOCKS = (0, 1, 3, 4)
TOK = 512
TT = TOK // P


def positive(value):
    return not isinstance(value, int) or value > 0


def known_below(value, limit):
    return not isinstance(value, int) or value < limit


def known_from(value, limit):
    return not isinstance(value, int) or value >= limit


def batches(engine, iteration):
    iteration(0, 0)
    with engine.Fori(0, 2) as it:
        iteration(it * 2 + 1, 1)
        iteration(it * 2 + 2, 0)
    for b in range(5, NB + 1):
        iteration(b, b % 2)


def stage_count(b, k):
    return 12 * b + k


def small_count(name, b):
    order, at = {"turn": (0, 0), "out": (1, 1), "mix": (2, 0), "values": (3, 0), "wo0": (4, 1), "wo1": (5, 1),
                 "query": (6, -1), "direction": (7, -1)}[name]
    b = b + at
    if isinstance(b, int) and b < 1:
        return {-1: {"query": 1, "direction": 2},
                0: {"turn": 3, "mix": 4, "values": 5, "query": 6, "direction": 7}}[b][name]
    if isinstance(b, int) and b == NB:
        return 8 * b - 1 - 2 + {"out": 1, "wo0": 2, "wo1": 3}[name]
    if isinstance(b, int) and b == NB - 1:
        return 8 * b - 1 + order + 1
    return 8 * b - 1 + order + 1


def adaln_block(nc, x, wq, bq, wk, bk, wv, bv, wo, bo, w1, w1t, b1, w2t, b2, ct, wmod, wkt, ident_in, hmask_in, out):
    x1 = nc.dram_tensor("x1_between", (NB, L, E), F32).ap()
    gates = nc.dram_tensor("gates_between", (NB, 2 * E), F32).ap()

    with ExitStack() as ctx:
        def sb(name, shape, dt=F32, stack=ctx):
            return stack.enter_context(nc.sbuf_tensor(name, shape, dt))

        def sem(name, stack=ctx):
            return stack.enter_context(nc.semaphore(name))

        ident = sb("ident", [P, P])
        modt = sb("modt", [P, 4, EC, NB])
        neg_half = sb("neg_half", [P, 4])
        psum = [ctx.enter_context(nc.psum_tensor(f"bank{i}", [P, 512], F32)) for i in range(8)]

        phase_a(nc, psum, ident, modt, neg_half, x, wq, bq, wk, bk, wv, bv, wo, bo, ct, wmod, wkt, ident_in,
                hmask_in, gates, x1)
        phase_b(nc, psum, ident, modt, neg_half, w1, w1t, b1, w2t, b2, gates, x1, out)


def phase_a(nc, psum, ident, modt, neg_half, x, wq, bq, wk, bk, wv, bv, wo, bo, ct, wmod, wkt, ident_in, hmask_in,
            gates, x1):
    with ExitStack() as ctx:
        def sb(name, shape, dt=F32):
            return ctx.enter_context(nc.sbuf_tensor(name, shape, dt))

        def sem(name):
            return ctx.enter_context(nc.semaphore(name))

        WQ, WK, WV, WO = range(4)
        w_q = sb("w_q", [P, EC, E])
        w_v = sb("w_v", [P, EC, E])
        w_kt = sb("w_kt", [P, EC, E])
        w_hi = sb("w_hi", [P, 4, EC, E], F32R)
        w_lo = sb("w_lo", [P, 4, EC, E], F32R)
        bias_q = sb("bias_q", [P, EC])
        bias_k = sb("bias_k", [P, EC])
        bias_v = sb("bias_v", [P, EC])
        bias_o = sb("bias_o", [P, E])
        hmask = sb("hmask", [P, EC, H])
        c_t = sb("c_t", [P, EC, NB])
        c_e = sb("c_e", [P, EC, NB])
        c_s = sb("c_s", [P, EC, NB])

        x_ln = sb("x_ln", [P, 8, E])
        x_res = sb("x_res", [P, 8, E])
        x_n = sb("x_n", [P, 8, E])
        stats = sb("stats", [P, 8, 6])
        mean_var = sb("mean_var", [P, 8, 2])
        var_eps = sb("var_eps", [P, 8])
        rstd = sb("rstd", [P, 8])
        mod_now = sb("mod_now", [P, 2, 2, EC])
        h_full = sb("h_full", [P, 2, 512])
        h_hi = sb("h_hi", [P, EC, L], F32R)
        h_lo = sb("h_lo", [P, EC, L], F32R)
        k_full = sb("k_full", [P, HALF])
        k_parts = sb("k_parts", [P, 2, EC, HALF], F32R)
        k_diag = [sb(f"k_diag{c}", [P, 2, 2, 4, HALF], F32R) for c in range(EC)]
        q_full = sb("q_full", [P, HALF])
        q_stack = sb("q_stack", [P, 4, PAIRS, 3, WIN], F32R)
        v_diag = sb("v_diag", [P, 2, 2 * PAIRS, H // 2, 2 * D])
        prob = sb("prob", [P, 4, 512])
        row_max = sb("row_max", [P, 2, 8])
        row_sum = sb("row_sum", [P, 2, 8])
        row_inv = sb("row_inv", [P, 2, 8])
        prob_t = sb("prob_t", [P, 2, 512])
        ctx_full = sb("ctx_full", [P, HALF])
        ctx_hi = sb("ctx_hi", [P, EC, HALF], F32R)
        ctx_lo = sb("ctx_lo", [P, EC, HALF], F32R)
        attn_tmp = sb("attn_tmp", [P, 512])
        gate_now = sb("gate_now", [P, E])
        gated_bias = sb("gated_bias", [P, E])
        h_tok = sb("h_tok", [P, EC])
        q_tok = sb("q_tok", [P, EC])
        q_heads = sb("q_heads", [P, EC, H])
        key_hi = sb("key_hi", [P, EC, H], F32R)
        key_lo = sb("key_lo", [P, EC, H], F32R)
        key_bias = sb("key_bias", [H, 1])
        g_score = sb("g_score", [H, L])
        g_max = sb("g_max", [H, 1])
        g_shift = sb("g_shift", [H, 1])
        g_sum = sb("g_sum", [H, 1])
        g_inv = sb("g_inv", [H, 1])
        g_prob_t = sb("g_prob_t", [P, 8, H])
        g_mix = sb("g_mix", [P, EC, H])
        g_all = sb("g_all", [P, EC, H])
        g_ctx = sb("g_ctx", [P, EC])
        g_ctx2 = sb("g_ctx2", [P, EC])
        g_hi = sb("g_hi", [P, EC, P], F32R)
        g_lo = sb("g_lo", [P, EC, P], F32R)

        gate_rows = attn_tmp[0:NB, :]
        gate_sign = ctx_full[0:NB, :]
        wmod_sb = v_diag[:, :, :, :, :].rearrange("p a w j d -> p (a w j d)")[:, 0:EC * 6 * E].rearrange(
            "p (c n) -> p c n", c=EC)
        w_k = x_res[:, 0:2, :]
        w_o = x_res[:, 2:4, :]

        stage = psum[0:2]
        score = psum[2:4]
        turned = psum[4:6]
        mixed = psum[6]
        small = psum[7]

        x_ln_loaded = sem("x_ln_loaded")
        x_res_loaded = sem("x_res_loaded")
        gate_loaded = sem("gate_loaded")
        x1_stored = sem("x1_stored")
        setup_loaded = sem("setup_loaded")
        gates_stored = sem("gates_stored")
        gates_ready = sem("gates_ready")
        silu_exp = sem("silu_exp")
        silu_ready = sem("silu_ready")
        mod_full = sem("mod_full")
        weights_ready = sem("weights_ready")
        zeroed = sem("zeroed")
        v_zeroed = sem("v_zeroed")
        dve_step = sem("dve_step")
        stats_ready = sem("stats_ready")
        rstd_ready = sem("rstd_ready")
        xn_ready = sem("xn_ready")
        mod_now_ready = sem("mod_now_ready")
        stage_full = sem("stage_full")
        stage_free = sem("stage_free")
        h_lo_ready = sem("h_lo_ready")
        k_lo_ready = sem("k_lo_ready")
        k_diag_loaded = [sem(f"k_diag_loaded{c}") for c in range(EC)]
        q_lo_ready = sem("q_lo_ready")
        score_full = sem("score_full")
        shifted = sem("shifted")
        exp_done = sem("exp_done")
        inv_ready = sem("inv_ready")
        prob_ready = sem("prob_ready")
        turned_full = sem("turned_full")
        turned_copied = sem("turned_copied")
        mix_done = sem("mix_done")
        ctx_hi_ready = sem("ctx_hi_ready")
        ctx_lo_ready = sem("ctx_lo_ready")
        small_full = sem("small_full")
        small_free = sem("small_free")
        g_shift_ready = sem("g_shift_ready")
        g_exp_done = sem("g_exp_done")
        g_prob_ready = sem("g_prob_ready")
        res_added = sem("res_added")
        bias_added = sem("bias_added")
        mod_loaded = sem("mod_loaded")
        h_tok_ready = sem("h_tok_ready")
        stack_zeroed = sem("stack_zeroed")

        N_ROLLED = 6

        def transfers(batch, tile):
            view = batch.rearrange("(p r) e -> r p e", r=256)
            yield view[1:65, :, :], tile[0:64, 0:4, :]
            yield view[65:129, :, :], tile[0:64, 4:8, :]
            yield view[129:193, :, :], tile[64:128, 0:4, :]
            yield view[193:256, :, :], tile[64:127, 4:8, :]
            yield view[0:1, 1:4, :], tile[127:128, 4:7, :]
            yield view[0:1, 0:1, :], tile[127:128, 7:8, :]

        def lagging(b, i, lag):
            n, j = (b, i - lag) if i >= lag else (b - 1, i - lag + ITEMS)
            return (n, j) if known_from(n, 0) and known_below(n, NB) else None

        block = ctx.enter_context(nc.Block())

        @block.sync
        def _(sp):
            def load_x(dst, loaded, b):
                for dram, tile in transfers(x[b], dst):
                    sp.dma_start(tile, dram).then_inc(loaded, 16)

            def load_gate(b):
                row = gates[b:b + 1, 0:E] if isinstance(b, int) else gates[bass.ds(b, 1), 0:E]
                sp.dma_start(gate_now[:], row.broadcast_to([P, E])).then_inc(gate_loaded, 16)

            def spread_keys(b, c):
                if positive(ITEMS * b - ITEMS + 4 + 4 * c):
                    sp.wait_ge(score_full, ITEMS * b - ITEMS + 4 + 4 * c)
                sp.wait_ge(k_lo_ready, (b + 1) * 2 + c - 1)
                for head in range(8):
                    for dup in range(2):
                        to = 64 * dup + D * (head % 4)
                        sp.dma_start(k_diag[c][to:to + D, :, head // 4, head % 4, :].bitcast(F32),
                                     k_parts[D * head:D * head + D, :, c, :].bitcast(F32)).then_inc(k_diag_loaded[c], 16)

            load_x(x_ln, x_ln_loaded, 0)
            sp.dma_start(c_t[:], ct.rearrange("(c p) b -> p c b", p=P)).then_inc(mod_loaded, 16)
            sp.dma_start(wmod_sb, wmod.rearrange("(c p) n -> p c n", p=P)).then_inc(mod_loaded, 16)
            for dst, src in (
                (ident[:], ident_in),
                (w_k, wk.rearrange("(c p) n -> p c n", p=P)),
                (w_q[:], wq.rearrange("(c p) n -> p c n", p=P)),
                (w_v[:], wv.rearrange("(c p) n -> p c n", p=P)),
                (w_o, wo.rearrange("(c p) n -> p c n", p=P)),
                (w_kt[:], wkt.rearrange("(c p) n -> p c n", p=P)),
                (hmask[:], hmask_in),
                (bias_q[:], bq),
                (bias_k[:], bk),
                (bias_v[:], bv),
                (bias_o[:], bo.rearrange("(a n) -> a n", a=1).broadcast_to([P, E])),
            ):
                sp.dma_start(dst, src).then_inc(setup_loaded, 16)
            sp.wait_ge(gates_ready, 1)
            sp.dma_start(gates, gate_rows).then_inc(gates_stored, 16)
            sp.wait_ge(xn_ready, 2)
            load_x(x_ln, x_ln_loaded, 1)
            sp.wait_ge(zeroed, 2)
            spread_keys(0, 0)
            sp.wait_ge(weights_ready, 1)
            load_x(x_res, x_res_loaded, 0)
            sp.wait_ge(gates_stored, 16)
            load_gate(0)

            def iteration(b, par):
                if known_below(b, NB):
                    spread_keys(b, 1)
                if known_below(b, NB - 1):
                    spread_keys(b + 1, 0)
                if known_below(b, NB - 2):
                    sp.wait_ge(xn_ready, 2 * b + 4)
                    load_x(x_ln, x_ln_loaded, b + 2)
                if known_from(b, 1):
                    sp.wait_ge(res_added, 4 * b)
                    for dram, tile in transfers(x1[b - 1], x_res):
                        sp.dma_start(dram, tile).then_inc(x1_stored, 16)
                    if known_below(b, NB):
                        sp.wait_ge(x1_stored, 16 * N_ROLLED * b)
                        load_x(x_res, x_res_loaded, b)
                        load_gate(b)

            batches(sp, iteration)
            sp.wait_ge(x1_stored, 16 * N_ROLLED * NB)

        @block.tensor
        def _(pe):
            def exact(dst, stationary, moving):
                n = len(stationary)
                for k in range(n):
                    (s_hi, s_lo), (m_hi, m_lo) = stationary[k], moving[k]
                    nc.tensor.matmul(dst, s_hi, m_hi, start=k == 0, stop=False)
                    nc.tensor.matmul(dst, s_hi, m_lo, start=False, stop=False)
                    done = nc.tensor.matmul(dst, s_lo, m_hi, start=False, stop=k == n - 1)
                return done

            def stage_bank(b, k):
                if positive(stage_count(b, k) - 2):
                    pe.wait_ge(stage_free, stage_count(b, k) - 2)
                return stage[k % 2]

            def small_bank(name, b):
                if positive(small_count(name, b) - 1):
                    pe.wait_ge(small_free, small_count(name, b) - 1)
                return small

            def turn_x(b, half, c, k):
                if c == 0:
                    pe.wait_ge(xn_ready, 2 * b + half + 1)
                bank = stage_bank(b, k)
                for p in range(4):
                    done = nc.tensor.transpose(bank[:, p * P:(p + 1) * P],
                                               x_n[:, 4 * half + p, c * P:(c + 1) * P], ident[:])
                done.then_inc(stage_full, 1)

            def project(b, which, c, k):
                pe.wait_ge(stage_free, stage_count(b, 2))
                pe.wait_ge(h_lo_ready, 4 * b + 2)
                bank = stage_bank(b, k)
                cols = slice(c * P, (c + 1) * P)
                exact(bank[:], [(w_hi[:, which, e, cols], w_lo[:, which, e, cols]) for e in range(EC)],
                      [(h_hi[:, e, 0:HALF], h_lo[:, e, 0:HALF]) for e in range(EC)]).then_inc(stage_full, 1)

            def project_v(b, two, k):
                bank = stage_bank(b, k)
                for p in (2 * two, 2 * two + 1):
                    tok = slice(p * P, (p + 1) * P)
                    done = exact(bank[:, (p % 2) * E:(p % 2 + 1) * E],
                                 [(h_hi[:, e, tok], h_lo[:, e, tok]) for e in range(EC)],
                                 [(w_hi[:, WV, e, :], w_lo[:, WV, e, :]) for e in range(EC)])
                done.then_inc(stage_full, 1)

            def global_query(b):
                pe.wait_ge(h_tok_ready, b + 1)
                bank = small_bank("query", b)
                for c in range(EC):
                    for e in range(EC):
                        done = nc.tensor.matmul(bank[:, c:c + 1], w_q[:, e, c * P:(c + 1) * P], h_tok[:, e:e + 1],
                                                start=e == 0, stop=e == EC - 1)
                done.then_inc(small_full, 1)

            def global_direction(b):
                bank = small_bank("direction", b)
                for e in range(EC):
                    for c in range(EC):
                        nc.tensor.matmul(bank[:, e * H:(e + 1) * H], w_kt[:, c, e * P:(e + 1) * P],
                                         q_heads[:, c, :], start=c == 0, stop=c == EC - 1)
                for c in range(EC):
                    done = nc.tensor.matmul(bank[0:H, 2 * H:2 * H + 1], q_heads[:, c, :], bias_k[:, c:c + 1],
                                            start=c == 0, stop=c == EC - 1)
                done.then_inc(small_full, 1)

            def global_scores(b, half, k):
                pe.wait_ge(small_free, small_count("direction", b))
                pe.wait_ge(stage_free, stage_count(b, 5))
                pe.wait_ge(h_lo_ready, 4 * b + 4)
                bank = stage_bank(b, k)
                tok = slice(half * HALF, (half + 1) * HALF)
                exact(bank[0:H, :], [(key_hi[:, e, :], key_lo[:, e, :]) for e in range(EC)],
                      [(h_hi[:, e, tok], h_lo[:, e, tok]) for e in range(EC)]).then_inc(stage_full, 1)

            def global_turn(b):
                pe.wait_ge(g_prob_ready, b + 1)
                bank = small_bank("turn", b)
                for t in range(8):
                    done = nc.tensor.matmul(bank[:, t * H:(t + 1) * H], g_score[:, t * P:(t + 1) * P],
                                            ident[0:H, 0:H], start=True, stop=True)
                done.then_inc(small_full, 1)

            def global_mix(b):
                pe.wait_ge(small_free, small_count("turn", b))
                bank = small_bank("mix", b)
                for e in range(EC):
                    for t in range(8):
                        done = nc.tensor.matmul(bank[:, e * H:(e + 1) * H], x_n[:, t, e * P:(e + 1) * P],
                                                g_prob_t[:, t, :], start=t == 0, stop=t == 7)
                done.then_inc(small_full, 1)

            def global_values(b):
                bank = small_bank("values", b)
                for c in range(EC):
                    for e in range(EC):
                        done = nc.tensor.matmul(bank[:, c * H:(c + 1) * H], w_v[:, e, c * P:(c + 1) * P],
                                                g_mix[:, e, :], start=e == 0, stop=e == EC - 1)
                done.then_inc(small_full, 1)

            def global_out(b):
                bank = small_bank("out", b)
                exact(bank[:, 0:E], [(g_hi[:, c, :], g_lo[:, c, :]) for c in range(EC)],
                      [(w_hi[:, WO, c, :], w_lo[:, WO, c, :]) for c in range(EC)]).then_inc(small_full, 1)

            def window_out(b, two):
                pe.wait_ge(ctx_hi_ready, 2 * b + 2)
                pe.wait_ge(ctx_lo_ready, 2 * b + 2)
                bank = small_bank(f"wo{two}", b)
                for p in (2 * two, 2 * two + 1):
                    tok = slice(p * P, (p + 1) * P)
                    done = exact(bank[:, (p % 2) * E:(p % 2 + 1) * E],
                                 [(ctx_hi[:, c, tok], ctx_lo[:, c, tok]) for c in range(EC)],
                                 [(w_hi[:, WO, c, :], w_lo[:, WO, c, :]) for c in range(EC)])
                done.then_inc(small_full, 1)

            def scores(b, i):
                c, p = divmod(i, 4)
                if p == 0:
                    pe.wait_ge(k_diag_loaded[c], 256 * b + 256)
                    pe.wait_ge(stage_free, stage_count(b, 7 + 5 * c))
                    pe.wait_ge(q_lo_ready, 2 * b + c + 1)
                if positive(ITEMS * b + i - 1):
                    pe.wait_ge(shifted, ITEMS * b + i - 1)
                bank = score[i % 2]
                for g in range(2):
                    for par in range(2):
                        for part in range(2):
                            done = nc.tensor.matmul(
                                bank[:, g * E:(g + 1) * E],
                                q_stack[:, 2 * c + g, p, par:par + 2, :],
                                k_diag[c][:, part, g, :, p * P + par * WIN:p * P + (par + 1) * WIN],
                                start=par + part == 0, stop=par + part == 2)
                done.then_inc(score_full, 1)

            def turn_probs(b, i):
                pe.wait_ge(prob_ready, ITEMS * b + i + 1)
                if positive(ITEMS * b + i - 1):
                    pe.wait_ge(turned_copied, ITEMS * b + i - 1)
                for j in range(4):
                    done = nc.tensor.transpose(turned[i % 2][:, j * P:(j + 1) * P],
                                               prob[:, i % 4, j * P:(j + 1) * P], ident[:])
                done.then_inc(turned_full, 1)

            def mix(b, i, par_b):
                c, p = divmod(i, 4)
                pe.wait_ge(turned_copied, ITEMS * b + i + 1)
                if i == 0:
                    pe.wait_ge(stage_free, stage_count(b, 11))
                if p == 0:
                    if positive(2 * b + c):
                        pe.wait_ge(ctx_hi_ready, 2 * b + c)
                for j in range(4):
                    for par in range(2):
                        done = nc.tensor.matmul(
                            mixed[32 * j:32 * j + 32, p * P + par * WIN:p * P + (par + 1) * WIN],
                            v_diag[:, par_b, 2 * p + par, 4 * c + j, :],
                            prob_t[:, i % 2, j * P + par * WIN:j * P + (par + 1) * WIN],
                            start=True, stop=True)
                done.then_inc(mix_done, 1)

            def stage_one(b, i):
                if i == 2:
                    turn_x(b, 0, 0, 1)
                    turn_x(b, 0, 1, 2)
                if i == 3:
                    project(b, WK, 0, 3)
                if i == 4:
                    turn_x(b, 1, 0, 4)
                    turn_x(b, 1, 1, 5)
                if i == 5:
                    project(b, WK, 1, 6)
                    project(b, WQ, 0, 7)
                if i == 6:
                    global_query(b)
                    project_v(b, 0, 8)
                    global_direction(b)
                if i == 7:
                    global_scores(b, 0, 9)
                    global_scores(b, 1, 10)
                    project_v(b, 1, 11)

            def rest(b, i):
                cur, prev = known_below(b, NB), known_from(b, 1)
                if i == 0 and cur:
                    project(b, WQ, 1, 12)
                    global_turn(b)
                if i == 1 and prev:
                    global_out(b - 1)
                if i == 1 and cur:
                    global_mix(b)
                if i == 2 and cur:
                    global_values(b)
                if i == 4 and prev:
                    window_out(b - 1, 0)
                if i == 5 and prev:
                    window_out(b - 1, 1)

            def iteration(b, par):
                for i in range(ITEMS):
                    if known_below(b, NB):
                        scores(b, i)
                    if (at := lagging(b, i, 2)) is not None:
                        turn_probs(*at)
                    if (at := lagging(b, i, 3)) is not None:
                        mix(*at, par if i >= 3 else 1 - par)
                    rest(b, i)
                    if known_below(b, NB - 1):
                        stage_one(b + 1, i)

            pe.wait_ge(mod_loaded, 32)
            pe.wait_ge(silu_ready, 1)
            for j, blk in enumerate(MOD_BLOCKS):
                for c in range(EC):
                    col = (j * EC + c) * NB
                    for e in range(EC):
                        nc.tensor.matmul(turned[0][:, col:col + NB],
                                         wmod_sb[:, e, blk * E + c * P:blk * E + (c + 1) * P], c_s[:, e, :],
                                         start=e == 0, stop=e == EC - 1)
            for j, blk in enumerate((2, 5)):
                for e in range(EC):
                    done = nc.tensor.matmul(turned[1][0:NB, j * E:(j + 1) * E], c_s[:, e, :],
                                            wmod_sb[:, e, blk * E:(blk + 1) * E], start=e == 0, stop=e == EC - 1)
            done.then_inc(mod_full, 1)
            pe.wait_ge(setup_loaded, 16 * 11)
            pe.wait_ge(weights_ready, 1)
            for i in range(ITEMS):
                stage_one(0, i)
            batches(pe, iteration)

        @block.scalar
        def _(act):
            def filled(b, k):
                act.wait_ge(stage_full, stage_count(b, k))
                return stage[k % 2]

            def modulate(b, par, half, c, k):
                bank = filled(b, k)
                act.wait_ge(mod_now_ready, b + 1)
                if positive(4 * b + 2 * half + c - 1):
                    act.wait_ge(h_lo_ready, 4 * b + 2 * half + c - 1)
                cols = slice(half * HALF, (half + 1) * HALF)
                shift, scale = mod_now[:, par, 0, c:c + 1], mod_now[:, par, 1, c:c + 1]
                nc.scalar.activation(h_full[:, c, :], bank[:], ACT.Identity, scale=scale, bias=shift)
                nc.scalar.activation(h_hi[:, c, cols], bank[:], ACT.Identity, scale=scale,
                                     bias=shift).then_inc(stage_free, 1)

            def take_keys(b, c, k):
                bank = filled(b, k)
                if positive(2 * b + c):
                    act.wait_ge(k_lo_ready, 2 * b + c)
                if positive(256 * b):
                    act.wait_ge(k_diag_loaded[c], 256 * b)
                nc.scalar.activation(k_full[:], bank[:], ACT.Identity, bias=bias_k[:, c:c + 1])
                nc.scalar.activation(k_parts[:, 0, c, :], bank[:], ACT.Identity,
                                     bias=bias_k[:, c:c + 1]).then_inc(stage_free, 1)

            def take_queries(b, c, k):
                bank = filled(b, k)
                if positive(2 * b + c):
                    act.wait_ge(q_lo_ready, 2 * b + c)
                if positive(ITEMS * b - ITEMS + 4 * c + 4):
                    act.wait_ge(score_full, ITEMS * b - ITEMS + 4 * c + 4)
                nc.scalar.activation(q_full[:], bank[:], ACT.Identity, bias=bias_q[:, c:c + 1])
                for g in range(2):
                    rows = slice(64 * g, 64 * g + 64)
                    done = nc.scalar.activation(q_stack[rows, 2 * c + g, :, 0:3:2, :],
                                                bank[rows, :].rearrange("r (p a q) -> r p a q", a=2, q=WIN),
                                                ACT.Identity, bias=bias_q[rows, c:c + 1])
                done.then_inc(stage_free, 1)

            def take_values(b, par_b, two, k):
                bank = filled(b, k)
                if isinstance(b, int) and b == 0:
                    act.wait_ge(v_zeroed, 1)
                if positive(ITEMS * b - ITEMS):
                    act.wait_ge(mix_done, ITEMS * b - ITEMS)
                for par in range(2):
                    src = bank[64 * par:64 * par + 64, :].rearrange("k (p j h d) -> k p j h d", p=2, j=H // 2, h=2)
                    for h2 in range(2):
                        dst = v_diag[64 * h2:64 * h2 + 64, par_b, 4 * two + par:4 * two + par + 3:2, :,
                                     D * h2:D * h2 + D]
                        done = nc.scalar.copy(dst, src[:, :, :, h2, :])
                done.then_inc(stage_free, 1)

            def take_global_scores(b, half, k):
                bank = filled(b, k)
                act.wait_ge(small_free, small_count("direction", b))
                if known_from(b, 1):
                    act.wait_ge(small_full, small_count("turn", b - 1))
                nc.scalar.activation(g_score[:, half * HALF:(half + 1) * HALF], bank[0:H, :], ACT.Identity,
                                     bias=key_bias[:, 0:1]).then_inc(stage_free, 1)

            def global_exp(b):
                act.wait_ge(g_shift_ready, b + 1)
                nc.scalar.activation(g_score[:], g_score[:], ACT.Exp, scale=SCALE,
                                     bias=g_shift[:, 0:1]).then_inc(g_exp_done, 1)

            def exponentials(b, i):
                act.wait_ge(shifted, ITEMS * b + i + 1)
                nc.scalar.activation(prob[:, i % 4, :], prob[:, i % 4, :], ACT.Exp, scale=SCALE).then_inc(exp_done, 1)

            def copy_turned(b, i):
                act.wait_ge(turned_full, ITEMS * b + i + 1)
                if positive(ITEMS * b + i - 1):
                    act.wait_ge(mix_done, ITEMS * b + i - 1)
                nc.scalar.copy(prob_t[:, i % 2, :], turned[i % 2][:]).then_inc(turned_copied, 1)

            def take_context(b, c):
                act.wait_ge(mix_done, ITEMS * b + 4 * c + 4)
                if positive(2 * b + c):
                    act.wait_ge(ctx_lo_ready, 2 * b + c)
                if known_from(b, 1):
                    act.wait_ge(small_full, small_count("wo1", b - 1))
                nc.scalar.activation(ctx_full[:], mixed[:], ACT.Identity, bias=bias_v[:, c:c + 1])
                nc.scalar.activation(ctx_hi[:, c, :], mixed[:], ACT.Identity,
                                     bias=bias_v[:, c:c + 1]).then_inc(ctx_hi_ready, 1)

            def stage_one(b, par, i):
                if i == 2:
                    modulate(b, par, 0, 0, 1)
                    modulate(b, par, 0, 1, 2)
                if i == 3:
                    take_keys(b, 0, 3)
                if i == 4:
                    modulate(b, par, 1, 0, 4)
                    modulate(b, par, 1, 1, 5)
                if i == 5:
                    take_keys(b, 1, 6)
                    take_queries(b, 0, 7)
                if i == 6:
                    take_values(b, par, 0, 8)
                if i == 7:
                    take_global_scores(b, 0, 9)
                    take_global_scores(b, 1, 10)
                    take_values(b, par, 1, 11)

            def iteration(b, par):
                cur = known_below(b, NB)
                for i in range(ITEMS):
                    if cur:
                        if i == 0:
                            global_exp(b)
                        exponentials(b, i)
                    if (at := lagging(b, i, 2)) is not None:
                        copy_turned(*at)
                    if i == 0 and cur:
                        take_queries(b, 1, 12)
                    if i == 2 and known_from(b, 1):
                        take_context(b - 1, 1)
                    if i == 6 and cur:
                        take_context(b, 0)
                    if known_below(b, NB - 1):
                        stage_one(b + 1, 1 - par, i)

            act.wait_ge(mod_loaded, 32)
            nc.scalar.activation(c_e[:], c_t[:], ACT.Exp, scale=-1.0).then_inc(silu_exp, 1)
            act.wait_ge(setup_loaded, 16 * 11)
            for i in range(ITEMS):
                stage_one(0, 0, i)
            batches(act, iteration)

        @block.vector
        def _(dve):
            steps = {"at": 0}

            def step():
                steps["at"] = steps["at"] + 1
                return steps["at"]

            def shift_scores(b, i):
                rows = score[i % 2][:].rearrange("q (h k) -> q h k", k=WIN)
                dve.wait_ge(score_full, ITEMS * b + i + 1)
                nc.vector.reduce_max(row_max[:, i % 2, :], rows, AX).then_inc(dve_step, 1)
                dve.wait_ge(dve_step, step())
                if positive(ITEMS * b + i - 3):
                    dve.wait_ge(turned_full, ITEMS * b + i - 3)
                nc.vector.tensor_tensor(prob[:, i % 4, :].rearrange("q (h k) -> q h k", k=WIN), rows,
                                        row_max[:, i % 2, :].unsqueeze(2).broadcast_to([P, 8, WIN]),
                                        ALU.subtract).then_inc(shifted, 1)

            def invert_sums(b, i):
                dve.wait_ge(exp_done, ITEMS * b + i + 1)
                nc.vector.reduce_sum(row_sum[:, i % 2, :], prob[:, i % 4, :].rearrange("q (h k) -> q h k", k=WIN), AX).then_inc(dve_step, 1)
                dve.wait_ge(dve_step, step())
                if positive(ITEMS * b + i - 1):
                    dve.wait_ge(prob_ready, ITEMS * b + i - 1)
                nc.vector.reciprocal(row_inv[:, i % 2, :], row_sum[:, i % 2, :]).then_inc(inv_ready, 1)

            def statistics(b, tiles, half=None):
                for t in tiles:
                    dve.wait_ge(x_ln_loaded, 16 * N_ROLLED * (b + 1))
                    done = nc.vector.bn_stats(stats[:, t, :], x_ln[:, t, :])
                if half is None:
                    return
                done.then_inc(dve_step, 1)
                dve.wait_ge(dve_step, step())
                if positive(2 * b + half):
                    dve.wait_ge(rstd_ready, 2 * b + half)
                nc.vector.memset(var_eps[:, 4 * half:4 * half + 4], EPS)
                for t in range(4 * half, 4 * half + 4):
                    done = nc.vector.bn_aggr(mean_var[:, t, :], stats[:, t, :])
                done.then_inc(dve_step, 1)
                dve.wait_ge(dve_step, step())
                part = var_eps[:, 4 * half:4 * half + 4]
                nc.vector.tensor_tensor(part, part, mean_var[:, 4 * half:4 * half + 4, 1],
                                        ALU.add).then_inc(stats_ready, 1)

            def normalise(b, half):
                dve.wait_ge(rstd_ready, 2 * b + half + 1)
                if known_from(b, 1):
                    dve.wait_ge(small_full, small_count("mix", b - 1))
                for t in range(4 * half, 4 * half + 4):
                    done = nc.vector.tensor_scalar(x_n[:, t, :], x_ln[:, t, :], mean_var[:, t, 0:1],
                                                   rstd[:, t:t + 1], ALU.subtract, ALU.mult)
                done.then_inc(xn_ready, 1)

            def pick_modulation(b, par):
                src = modt[:, SA:CA + 1, :, b:b + 1] if isinstance(b, int) else modt[:, SA:CA + 1, :, bass.ds(b, 1)]
                nc.vector.tensor_copy(mod_now[:, par, :, :],
                                      src.rearrange("p j c b -> p j (c b)")).then_inc(mod_now_ready, 1)

            def low_queries(b, c):
                dve.wait_ge(stage_free, stage_count(b, 7 + 5 * c))
                for g in range(2):
                    rows, other = slice(64 * g, 64 * g + 64), slice(64 - 64 * g, 128 - 64 * g)
                    done = nc.vector.tensor_tensor(
                        q_stack[other, 2 * c + g, :, 0:3:2, :],
                        q_full[rows, :].rearrange("r (p a q) -> r p a q", a=2, q=WIN),
                        q_stack[rows, 2 * c + g, :, 0:3:2, :].bitcast(F32), ALU.subtract)
                done.then_inc(q_lo_ready, 1)

            def token_h(b):
                dve.wait_ge(stage_free, stage_count(b, 5))
                dve.wait_ge(h_lo_ready, 4 * b + 4)
                if known_from(b, 1):
                    dve.wait_ge(small_full, small_count("query", b - 1))
                nc.vector.tensor_tensor(h_tok[:].unsqueeze(2), h_hi[:, :, L - 1:L].bitcast(F32),
                                        h_lo[:, :, L - 1:L].bitcast(F32), ALU.add).then_inc(h_tok_ready, 1)

            def take_query(b):
                dve.wait_ge(small_full, small_count("query", b))
                nc.vector.tensor_tensor(q_tok[:], small[:, 0:EC], bias_q[:], ALU.add).then_inc(dve_step, 1)
                dve.wait_ge(dve_step, step())
                nc.vector.tensor_tensor(q_heads[:], hmask[:], q_tok[:].unsqueeze(2).broadcast_to([P, EC, H]),
                                        ALU.mult).then_inc(small_free, 1)

            def take_direction(b):
                dve.wait_ge(small_full, small_count("direction", b))
                nc.vector.tensor_copy(key_bias[:], small[0:H, 2 * H:2 * H + 1])
                both = small[:, 0:2 * H].rearrange("p (e h) -> p e h", e=EC)
                nc.vector.tensor_copy(key_hi[:], both).then_inc(dve_step, 1)
                dve.wait_ge(dve_step, step())
                nc.vector.tensor_tensor(key_lo[:], both, key_hi[:].bitcast(F32), ALU.subtract).then_inc(small_free, 1)

            def global_shift(b):
                dve.wait_ge(stage_free, stage_count(b, 10))
                nc.vector.reduce_max(g_max[:], g_score[:], AX).then_inc(dve_step, 1)
                dve.wait_ge(dve_step, step())
                nc.vector.tensor_scalar_mul(g_shift[:], g_max[:], -SCALE).then_inc(g_shift_ready, 1)

            def global_probs(b):
                dve.wait_ge(g_exp_done, b + 1)
                nc.vector.reduce_sum(g_sum[:], g_score[:], AX).then_inc(dve_step, 1)
                dve.wait_ge(dve_step, step())
                nc.vector.reciprocal(g_inv[:], g_sum[:]).then_inc(dve_step, 1)
                dve.wait_ge(dve_step, step())
                nc.vector.tensor_scalar_mul(g_score[:], g_score[:], g_inv[:, 0:1]).then_inc(g_prob_ready, 1)

            def take_turn(b):
                dve.wait_ge(small_full, small_count("turn", b))
                nc.vector.tensor_copy(g_prob_t[:].rearrange("p t h -> p (t h)"),
                                      small[:, 0:8 * H]).then_inc(small_free, 1)

            def take_mix(b, par):
                dve.wait_ge(small_full, small_count("mix", b))
                for e in range(EC):
                    done = nc.vector.tensor_scalar(g_mix[:, e, :], small[:, e * H:(e + 1) * H],
                                                   mod_now[:, par, 1, e:e + 1], mod_now[:, par, 0, e:e + 1],
                                                   ALU.mult, ALU.add)
                done.then_inc(small_free, 1)

            def take_global_values(b):
                dve.wait_ge(small_full, small_count("values", b))
                nc.vector.tensor_tensor(g_all[:], small[:, 0:2 * H].rearrange("p (c h) -> p c h", c=EC),
                                        hmask[:], ALU.mult).then_inc(dve_step, 1)
                dve.wait_ge(dve_step, step())
                nc.vector.reduce_sum(g_ctx[:], g_all[:], AX).then_inc(dve_step, 1)
                dve.wait_ge(dve_step, step())
                nc.vector.tensor_tensor(g_ctx2[:], g_ctx[:], bias_v[:], ALU.add).then_inc(dve_step, 1)
                dve.wait_ge(dve_step, step())
                nc.vector.tensor_copy(g_hi[:, :, P - 1:P], g_ctx2[:].unsqueeze(2)).then_inc(dve_step, 1)
                dve.wait_ge(dve_step, step())
                nc.vector.tensor_tensor(g_lo[:, :, P - 1:P], g_ctx2[:].unsqueeze(2),
                                        g_hi[:, :, P - 1:P].bitcast(F32), ALU.subtract).then_inc(small_free, 1)

            def gate_out(name, b, tiles):
                dve.wait_ge(small_full, small_count(name, b))
                dve.wait_ge(gate_loaded, 16 * b + 16)
                dve.wait_ge(res_added, 4 * b + {"out": 1, "wo0": 2, "wo1": 3}[name])
                nc.vector.tensor_tensor(attn_tmp[:, 0:tiles * E].rearrange("p (t e) -> p t e", e=E),
                                        small[:, 0:tiles * E].rearrange("p (t e) -> p t e", e=E),
                                        gate_now[:].unsqueeze(1).broadcast_to([P, tiles, E]),
                                        ALU.mult).then_inc(small_free, 1)

            def slot_steps(b, par, i):
                cur, prev, nxt = known_below(b, NB), known_from(b, 1), known_below(b, NB - 1)
                if i == 0 and nxt:
                    pick_modulation(b + 1, 1 - par)
                    statistics(b + 1, (0, 1))
                if i == 0 and cur:
                    low_queries(b, 1)
                    take_turn(b)
                if i == 1:
                    if nxt:
                        statistics(b + 1, (2, 3), 0)
                    if prev:
                        gate_out("out", b - 1, 1)
                    if cur:
                        take_mix(b, par)
                if i == 2:
                    if nxt:
                        normalise(b + 1, 0)
                    if cur:
                        take_global_values(b)
                if i == 3 and nxt:
                    statistics(b + 1, (4, 5, 6, 7), 1)
                if i == 4:
                    if nxt:
                        normalise(b + 1, 1)
                    if prev:
                        gate_out("wo0", b - 1, 2)
                if i == 5 and prev:
                    gate_out("wo1", b - 1, 2)
                if nxt:
                    if i == 5:
                        low_queries(b + 1, 0)
                    if i == 6:
                        token_h(b + 1)
                        take_query(b + 1)
                        take_direction(b + 1)
                    if i == 7:
                        global_shift(b + 1)

            def iteration(b, par):
                if not isinstance(b, int) or 1 <= b < NB:
                    steps["at"] = DVE_BEFORE + DVE_FIRST + DVE_STEPS * (b - 1)
                for i in range(ITEMS):
                    if known_below(b, NB):
                        shift_scores(b, i)
                        if i == 0:
                            global_probs(b)
                    if (at := lagging(b, i, 1)) is not None:
                        invert_sums(*at)
                    slot_steps(b, par, i)

            nc.vector.memset(q_stack[:].bitcast(F32), 0.0)
            nc.vector.memset(g_hi[:].bitcast(F32), 0.0)
            nc.vector.memset(g_lo[:].bitcast(F32), 0.0)
            nc.vector.memset(neg_half[:], -0.5).then_inc(stack_zeroed, 1)
            statistics(0, (0, 1, 2, 3), 0)
            dve.wait_ge(silu_exp, 1)
            nc.vector.tensor_scalar_add(c_e[:], c_e[:], 1.0).then_inc(dve_step, 1)
            dve.wait_ge(dve_step, step())
            nc.vector.reciprocal(c_e[:], c_e[:]).then_inc(dve_step, 1)
            dve.wait_ge(dve_step, step())
            nc.vector.tensor_tensor(c_s[:], c_e[:], c_t[:], ALU.mult).then_inc(silu_ready, 1)
            statistics(0, (4, 5, 6, 7), 1)
            normalise(0, 0)
            dve.wait_ge(setup_loaded, 16 * 11)
            for which, src in ((WK, w_k), (WQ, w_q[:]), (WV, w_v[:]), (WO, w_o)):
                nc.vector.tensor_copy(w_hi[:, which, :, :], src).then_inc(dve_step, 1)
                dve.wait_ge(dve_step, step())
                done = nc.vector.tensor_tensor(w_lo[:, which, :, :], src, w_hi[:, which, :, :].bitcast(F32),
                                               ALU.subtract)
            done.then_inc(weights_ready, 1)
            dve.wait_ge(mod_full, 1)
            mods = turned[0][:, 0:4 * EC * NB].rearrange("p (j n) -> p j n", j=4)
            flat = modt[:].rearrange("p j c b -> p j (c b)")
            nc.vector.tensor_copy(flat[:, SA:CB:2, :], mods[:, SA:CB:2, :])
            nc.vector.tensor_scalar_add(flat[:, CA:CB + 1:2, :], mods[:, CA:CB + 1:2, :], 1.0).then_inc(dve_step, 1)
            dve.wait_ge(dve_step, step())
            pick_modulation(0, 0)
            normalise(0, 1)
            raw = turned[1][0:NB, :]
            nc.vector.tensor_scalar(gate_sign, raw, 0.0, 2.0, ALU.is_ge, ALU.mult)
            nc.vector.tensor_scalar_mul(gate_rows, raw, -1.0).then_inc(dve_step, 1)
            dve.wait_ge(dve_step, step())
            nc.vector.scalar_tensor_tensor(gate_rows, gate_rows, 0.25, raw, ALU.max, ALU.max).then_inc(dve_step, 1)
            dve.wait_ge(dve_step, step())
            nc.vector.scalar_tensor_tensor(gate_rows, gate_sign, 1.0, gate_rows, ALU.subtract,
                                           ALU.mult).then_inc(gates_ready, 1)
            low_queries(0, 0)
            token_h(0)
            take_query(0)
            take_direction(0)
            global_shift(0)
            assert steps["at"] == DVE_BEFORE, steps
            batches(dve, iteration)

        @block.gpsimd
        def _(pool):
            def power(b, half):
                pool.wait_ge(stats_ready, 2 * b + half + 1)
                if positive(2 * b - 1 + half):
                    pool.wait_ge(xn_ready, 2 * b - 1 + half)
                cols = slice(4 * half, 4 * half + 4)
                nc.gpsimd.tensor_tensor(rstd[:, cols], var_eps[:, cols], neg_half[:],
                                        ALU.pow).then_inc(rstd_ready, 1)

            def low_h(b, half, c):
                pool.wait_ge(stage_free, stage_count(b, (1 if half == 0 else 4) + c))
                cols = slice(half * HALF, (half + 1) * HALF)
                nc.gpsimd.tensor_tensor(h_lo[:, c, cols], h_full[:, c, :], h_hi[:, c, cols].bitcast(F32),
                                        ALU.subtract).then_inc(h_lo_ready, 1)

            def low_keys(b, c):
                pool.wait_ge(stage_free, stage_count(b, 3 + 3 * c))
                nc.gpsimd.tensor_tensor(k_parts[:, 1, c, :], k_full[:], k_parts[:, 0, c, :].bitcast(F32),
                                        ALU.subtract).then_inc(k_lo_ready, 1)

            def low_context(b, c):
                pool.wait_ge(ctx_hi_ready, 2 * b + c + 1)
                nc.gpsimd.tensor_tensor(ctx_lo[:, c, :], ctx_full[:], ctx_hi[:, c, :].bitcast(F32),
                                        ALU.subtract).then_inc(ctx_lo_ready, 1)

            def normalise_probs(b, i):
                pool.wait_ge(inv_ready, ITEMS * b + i + 1)
                rows = prob[:, i % 4, :].rearrange("q (h k) -> q h k", k=WIN)
                nc.gpsimd.tensor_tensor(rows, rows, row_inv[:, i % 2, :].unsqueeze(2).broadcast_to([P, 8, WIN]),
                                        ALU.mult).then_inc(prob_ready, 1)

            def gate_bias(b):
                pool.wait_ge(gate_loaded, 16 * b + 16)
                nc.gpsimd.tensor_tensor(gated_bias[:], bias_o[:], gate_now[:], ALU.mult).then_inc(res_added, 1)

            def add_bias(b):
                nc.gpsimd.tensor_tensor(x_res[:], x_res[:], gated_bias[:].unsqueeze(1).broadcast_to([P, 8, E]),
                                        ALU.add).then_inc(bias_added, 1)
                pool.wait_ge(bias_added, b + 1)

            def add_out(name, b, first, tiles):
                pool.wait_ge(small_free, small_count(name, b))
                pool.wait_ge(x_res_loaded, 16 * N_ROLLED * (b + 1))
                part = x_res[:, first:first + tiles, :].rearrange("p t e -> p (t e)")
                nc.gpsimd.tensor_tensor(part, part, attn_tmp[:, 0:tiles * E], ALU.add).then_inc(res_added, 1)

            def slot_steps(b, i):
                cur, prev, nxt = known_below(b, NB), known_from(b, 1), known_below(b, NB - 1)
                if i == 1 and nxt:
                    power(b + 1, 0)
                if i == 1 and prev:
                    gate_bias(b - 1)
                    add_out("out", b - 1, 7, 1)
                if i == 2 and nxt:
                    low_h(b + 1, 0, 0)
                    low_h(b + 1, 0, 1)
                if i == 2 and prev:
                    pool.wait_ge(res_added, 4 * b - 2)
                    add_bias(b - 1)
                if i == 3 and prev:
                    low_context(b - 1, 1)
                if i == 3 and nxt:
                    low_keys(b + 1, 0)
                    power(b + 1, 1)
                if i == 4:
                    if nxt:
                        low_h(b + 1, 1, 0)
                        low_h(b + 1, 1, 1)
                    if prev:
                        add_out("wo0", b - 1, 0, 2)
                if i == 5:
                    if nxt:
                        low_keys(b + 1, 1)
                    if prev:
                        add_out("wo1", b - 1, 2, 2)
                if i == 7 and cur:
                    low_context(b, 0)

            def iteration(b, par):
                for i in range(ITEMS):
                    if (at := lagging(b, i, 1)) is not None:
                        normalise_probs(*at)
                    slot_steps(b, i)

            nc.gpsimd.memset(k_diag[0][:].bitcast(F32), 0.0).then_inc(zeroed, 1)
            pool.wait_ge(stack_zeroed, 1)
            power(0, 0)
            power(0, 1)
            pool.wait_ge(mod_full, 1)
            nc.gpsimd.memset(v_diag[:], 0.0).then_inc(v_zeroed, 1)
            low_h(0, 0, 0)
            low_h(0, 0, 1)
            low_keys(0, 0)
            nc.gpsimd.memset(k_diag[1][:].bitcast(F32), 0.0).then_inc(zeroed, 1)
            low_h(0, 1, 0)
            low_h(0, 1, 1)
            low_keys(0, 1)
            batches(pool, iteration)


def phase_b(nc, psum, ident, modt, neg_half, w1, w1t, b1, w2t, b2, gates, x1, out):
    units = NB * L // TOK
    x1_units = x1.rearrange("b (u t p) e -> (b u) p t e", p=P, t=TT)
    out_units = out.rearrange("b (u t p) e -> (b u) p t e", p=P, t=TT)

    with ExitStack() as ctx:
        def sb(name, shape, dt=F32):
            return ctx.enter_context(nc.sbuf_tensor(name, shape, dt))

        def sem(name):
            return ctx.enter_context(nc.semaphore(name))

        w1_raw = sb("w1_raw", [P, FC, E])
        w1t_raw = sb("w1t_raw", [P, EC, F])
        w2t_raw = sb("w2t_raw", [P, FC, E])
        w2_abs = sb("w2_abs", [P, FC, E])
        w1_abs = sb("w1_abs", [P, FC, E])
        w1_sign = sb("w1_sign", [P, EC, F], F32R)
        w2_sign = sb("w2_sign", [P, FC, E], F32R)
        mean_ones = sb("mean_ones", [P, P])
        w1_sum = sb("w1_sum", [P, FC])
        alpha1 = sb("alpha1", [P, FC])
        bias1 = sb("bias1", [P, FC])
        alpha2 = sb("alpha2", [P, E])
        bias2 = sb("bias2", [P, E])
        x_in = sb("x_in", [P, 2, TT, E])
        stats = sb("f_stats", [P, TT, 6])
        mean_var = sb("f_mean_var", [P, TT, 2])
        var_eps = sb("f_var_eps", [P, TT])
        rstd = sb("f_rstd", [P, TT])
        x_n = sb("f_x_n", [P, TT, E])
        mod_now = sb("f_mod_now", [P, 2, 2, EC])
        gate_now = sb("f_gate_now", [P, 2, E])
        out_scale = sb("out_scale", [P, 2, E])
        out_bias = sb("out_bias", [P, E])
        h_full = sb("f_h_full", [P, EC, TOK])
        h_hi = sb("f_h_hi", [P, 2, EC, TOK], F32R)
        h_lo = sb("f_h_lo", [P, 2, EC, TOK], F32R)
        g_full = sb("g_full", [P, 2, TOK])
        act_hi = sb("act_hi", [P, 2, FC, TOK], F32R)
        act_lo = sb("act_lo", [P, 2, FC, TOK], F32R)
        y_tmp = sb("y_tmp", [P, 2, E])
        y = sb("y", [P, 2, TT, E])

        hidden = psum[0:4]
        turned = psum[4:6]
        result = psum[6:8]

        w_loaded = sem("w_loaded")
        x_in_loaded = [sem(f"x_in_loaded{i}") for i in range(2)]
        f_gate_loaded = [sem(f"f_gate_loaded{i}") for i in range(2)]
        y_stored = [sem(f"y_stored{i}") for i in range(2)]
        signs_ready = sem("signs_ready")
        abs_ready = sem("abs_ready")
        alpha2_full = sem("alpha2_full")
        alphas_ready = sem("alphas_ready")
        f_step = sem("f_step")
        f_stats_ready = sem("f_stats_ready")
        f_rstd_ready = sem("f_rstd_ready")
        f_xn_ready = sem("f_xn_ready")
        f_mod_ready = sem("f_mod_ready")
        f_turned_full = sem("f_turned_full")
        f_h_hi_ready = sem("f_h_hi_ready")
        f_h_lo_ready = sem("f_h_lo_ready")
        hidden_full = sem("hidden_full")
        gelu_done = sem("gelu_done")
        act_lo_ready = sem("act_lo_ready")
        result_full = sem("result_full")
        scaled = sem("scaled")
        y_started = sem("y_started")
        y_ready = sem("y_ready")
        scale_ready = sem("scale_ready")
        out_bias_ready = sem("out_bias_ready")

        def moved_before(v, par):
            return 8 * (v - par)

        def over_units(engine, iteration):
            iteration(0, 0, 0)
            iteration(1, 1, 0)
            with engine.Fori(1, (units - 2) // 2) as it:
                iteration(it * 2, 0, it)
                iteration(it * 2 + 1, 1, it)
            for v in range(units - 2, units + 1):
                iteration(v, v % 2, v // 2)

        block = ctx.enter_context(nc.Block())

        @block.sync
        def _(sp):
            def load(v, par, batch):
                src = x1_units[v] if isinstance(v, int) else x1_units[bass.ds(v, 1)].rearrange(
                    "u p t e -> (u p) t e")
                row = gates[batch:batch + 1, E:2 * E] if isinstance(batch, int) else gates[bass.ds(batch, 1), E:2 * E]
                sp.dma_start(x_in[:, par, :, :], src).then_inc(x_in_loaded[par], 16)
                sp.dma_start(gate_now[:, par, :], row.broadcast_to([P, E])).then_inc(f_gate_loaded[par], 16)

            load(0, 0, 0)
            for dst, src in (
                (w1t_raw[:], w1t.rearrange("(c p) n -> p c n", p=P)),
                (w1_raw[:], w1.rearrange("(c p) n -> p c n", p=P)),
                (w2t_raw[:], w2t.rearrange("(c p) n -> p c n", p=P)),
                (bias1[:], b1),
                (bias2[:], b2.rearrange("(a n) -> a n", a=1).broadcast_to([P, E])),
            ):
                sp.dma_start(dst, src).then_inc(w_loaded, 16)

            def iteration(v, par, batch):
                if known_below(v, units - 1):
                    if positive(v):
                        sp.wait_ge(y_started, v)
                    load(v + 1, 1 - par, batch + 1 if par else batch)
                if known_from(v, 1):
                    sp.wait_ge(y_ready, TT * v)
                    dst = out_units[v - 1] if isinstance(v, int) else out_units[bass.ds(v - 1, 1)].rearrange(
                        "u p t e -> (u p) t e")
                    sp.dma_start(dst, y[:, 1 - par, :, :]).then_inc(y_stored[1 - par], 16)

            over_units(sp, iteration)
            sp.wait_ge(y_stored[0], 16 * units // 2)
            sp.wait_ge(y_stored[1], 16 * units // 2)

        @block.tensor
        def _(pe):
            def turn_x(v, c):
                pe.wait_ge(f_xn_ready, v + 1)
                if positive(2 * v + c - 1):
                    pe.wait_ge(f_h_hi_ready, 2 * v + c - 1)
                for t in range(TT):
                    done = nc.tensor.transpose(turned[c][:, t * P:(t + 1) * P], x_n[:, t, c * P:(c + 1) * P],
                                               ident[:])
                done.then_inc(f_turned_full, 1)

            def up(v, par, f):
                if f == 0:
                    pe.wait_ge(f_h_hi_ready, 2 * v + 2)
                    pe.wait_ge(f_h_lo_ready, 2 * v + 2)
                if positive(FC * v + f - 3):
                    pe.wait_ge(gelu_done, FC * v + f - 3)
                for e in range(EC):
                    for h in (h_hi, h_lo):
                        done = nc.tensor.matmul(hidden[f % 4][:], w1_sign[:, e, f * P:(f + 1) * P],
                                                h[:, par, e, :], start=e == 0 and h is h_hi,
                                                stop=e == EC - 1 and h is h_lo)
                done.then_inc(hidden_full, 1)

            def down(v, par, t):
                pe.wait_ge(act_lo_ready, FC * v + FC)
                if positive(TT * v + t - 1):
                    pe.wait_ge(scaled, TT * v + t - 1)
                for f in range(FC):
                    for a in (act_hi, act_lo):
                        done = nc.tensor.matmul(result[t % 2][:, 0:E], a[:, par, f, t * P:(t + 1) * P],
                                                w2_sign[:, f, :], start=f == 0 and a is act_hi,
                                                stop=f == FC - 1 and a is act_lo)
                done.then_inc(result_full, 1)

            def iteration(v, par, batch):
                cur, prev = known_below(v, units), known_from(v, 1)
                for f in range(FC):
                    if cur:
                        up(v, par, f)
                    if f % 2 == 1 and prev:
                        down(v - 1, 1 - par, f // 2)
                    if f in (5, 6) and known_below(v, units - 1):
                        turn_x(v + 1, f - 5)

            turn_x(0, 0)
            turn_x(0, 1)
            pe.wait_ge(signs_ready, 1)
            pe.wait_ge(abs_ready, 1)
            for f in range(FC):
                done = nc.tensor.matmul(result[0][:, 0:E], mean_ones[:], w2_abs[:, f, :], start=f == 0, stop=f == FC - 1)
            done.then_inc(alpha2_full, 1)
            pe.wait_ge(alphas_ready, 1)
            over_units(pe, iteration)

        @block.scalar
        def _(act):
            def modulate(v, par, c):
                act.wait_ge(f_turned_full, 2 * v + c + 1)
                act.wait_ge(f_mod_ready, v + 1)
                if positive(2 * v + c - 1):
                    act.wait_ge(f_h_lo_ready, 2 * v + c - 1)
                shift, scale = mod_now[:, par, 0, c:c + 1], mod_now[:, par, 1, c:c + 1]
                nc.scalar.activation(h_full[:, c, :], turned[c][:], ACT.Identity, scale=scale, bias=shift)
                nc.scalar.activation(h_hi[:, par, c, :], turned[c][:], ACT.Identity, scale=scale,
                                     bias=shift).then_inc(f_h_hi_ready, 1)

            def gelu(v, par, f):
                act.wait_ge(hidden_full, FC * v + f + 1)
                if positive(FC * v + f - 1):
                    act.wait_ge(act_lo_ready, FC * v + f - 1)
                if f == 0:
                    if positive(TT * v - TT):
                        act.wait_ge(result_full, TT * v - TT)
                done = nc.scalar.activation(g_full[:, f % 2, :], hidden[f % 4][:], ACT.Gelu,
                                            scale=alpha1[:, f:f + 1], bias=bias1[:, f:f + 1])
                if f % 2 == 0:
                    done = nc.scalar.activation(act_hi[:, par, f, :], hidden[f % 4][:], ACT.Gelu,
                                                scale=alpha1[:, f:f + 1], bias=bias1[:, f:f + 1])
                done.then_inc(gelu_done, 1)

            def iteration(v, par, batch):
                for f in range(FC):
                    if known_below(v, units):
                        gelu(v, par, f)
                    if f in (6, 7) and known_below(v, units - 1):
                        modulate(v + 1, 1 - par, f - 6)

            act.wait_ge(w_loaded, 16 * 5)
            nc.scalar.activation(w1_sign[:], w1t_raw[:], ACT.Sign)
            nc.scalar.activation(w2_sign[:], w2t_raw[:], ACT.Sign).then_inc(signs_ready, 1)
            modulate(0, 0, 0)
            modulate(0, 0, 1)
            act.wait_ge(alphas_ready, 1)
            over_units(act, iteration)

        @block.vector
        def _(dve):
            steps = {"at": 0}

            def step():
                steps["at"] = steps["at"] + 1
                return steps["at"]

            def statistics(v, par):
                dve.wait_ge(x_in_loaded[par], moved_before(v, par) + 16)
                for t in range(TT):
                    done = nc.vector.bn_stats(stats[:, t, :], x_in[:, par, t, :])
                done.then_inc(f_step, 1)
                dve.wait_ge(f_step, step())
                nc.vector.memset(var_eps[:], EPS)
                for t in range(TT):
                    done = nc.vector.bn_aggr(mean_var[:, t, :], stats[:, t, :])
                done.then_inc(f_step, 1)
                dve.wait_ge(f_step, step())
                nc.vector.tensor_tensor(var_eps[:], var_eps[:], mean_var[:, :, 1], ALU.add).then_inc(f_stats_ready, 1)

            def normalise(v, par):
                dve.wait_ge(f_rstd_ready, v + 1)
                if positive(2 * v):
                    dve.wait_ge(f_turned_full, 2 * v)
                for t in range(TT):
                    done = nc.vector.tensor_scalar(x_n[:, t, :], x_in[:, par, t, :], mean_var[:, t, 0:1],
                                                   rstd[:, t:t + 1], ALU.subtract, ALU.mult)
                done.then_inc(f_xn_ready, 1)

            def pick_modulation(v, par, batch):
                src = modt[:, SB:CB + 1, :, batch:batch + 1] if isinstance(batch, int) else modt[
                    :, SB:CB + 1, :, bass.ds(batch, 1)]
                nc.vector.tensor_copy(mod_now[:, par, :, :],
                                      src.rearrange("p j c b -> p j (c b)")).then_inc(f_mod_ready, 1)

            def low_activation(v, par, f):
                dve.wait_ge(gelu_done, FC * v + f + 1)
                if f % 2 == 1:
                    nc.vector.tensor_copy(act_hi[:, par, f, :], g_full[:, f % 2, :]).then_inc(f_step, 1)
                    dve.wait_ge(f_step, step())
                nc.vector.tensor_tensor(act_lo[:, par, f, :], g_full[:, f % 2, :],
                                        act_hi[:, par, f, :].bitcast(F32), ALU.subtract).then_inc(act_lo_ready, 1)

            def scale_result(v, par, t):
                dve.wait_ge(result_full, TT * v + t + 1)
                if positive(TT * v + t - 1):
                    dve.wait_ge(y_ready, TT * v + t - 1)
                if t == 0:
                    dve.wait_ge(scale_ready, v + 1)
                nc.vector.tensor_tensor(y_tmp[:, t % 2, :], result[t % 2][:, 0:E], out_scale[:, par, :],
                                        ALU.mult).then_inc(scaled, 1)

            def iteration(v, par, batch):
                if not isinstance(v, int) or 1 <= v < units:
                    steps["at"] = F_BEFORE + F_STEPS * v
                cur, prev, nxt = known_below(v, units), known_from(v, 1), known_below(v, units - 1)
                for f in range(FC):
                    if cur:
                        low_activation(v, par, f)
                    if f % 2 == 1 and prev:
                        scale_result(v - 1, 1 - par, f // 2)
                    if f == 2 and nxt:
                        pick_modulation(v + 1, 1 - par, batch + 1 if par else batch)
                        statistics(v + 1, 1 - par)
                    if f == 4 and nxt:
                        normalise(v + 1, 1 - par)

            pick_modulation(0, 0, 0)
            statistics(0, 0)
            normalise(0, 0)
            nc.vector.memset(mean_ones[:], 1.0 / F)
            dve.wait_ge(w_loaded, 16 * 5)
            for dst, src in ((w2_abs, w2t_raw), (w1_abs, w1_raw)):
                done = nc.vector.scalar_tensor_tensor(dst[:], src[:], -1.0, src[:], ALU.mult, ALU.max)
                if dst is w2_abs:
                    done.then_inc(abs_ready, 1)
            done.then_inc(f_step, 1)
            dve.wait_ge(f_step, step())
            nc.vector.reduce_sum(w1_sum[:], w1_abs[:], AX).then_inc(f_step, 1)
            dve.wait_ge(f_step, step())
            nc.vector.tensor_scalar_mul(alpha1[:], w1_sum[:], 1.0 / E)
            dve.wait_ge(alpha2_full, 1)
            nc.vector.tensor_copy(alpha2[:], result[0][:, 0:E]).then_inc(alphas_ready, 1)
            assert steps["at"] == F_BEFORE, steps
            over_units(dve, iteration)

        @block.gpsimd
        def _(pool):
            def power(v):
                pool.wait_ge(f_stats_ready, v + 1)
                if positive(v):
                    pool.wait_ge(f_xn_ready, v)
                nc.gpsimd.tensor_tensor(rstd[:], var_eps[:], neg_half[:], ALU.pow).then_inc(f_rstd_ready, 1)

            def low_h(v, par, c):
                pool.wait_ge(f_h_hi_ready, 2 * v + c + 1)
                nc.gpsimd.tensor_tensor(h_lo[:, par, c, :], h_full[:, c, :], h_hi[:, par, c, :].bitcast(F32),
                                        ALU.subtract).then_inc(f_h_lo_ready, 1)

            def start_y(v, par):
                pool.wait_ge(f_gate_loaded[par], moved_before(v, par) + 16)
                pool.wait_ge(x_in_loaded[par], moved_before(v, par) + 16)
                if positive(TT * v - TT):
                    pool.wait_ge(scaled, TT * v - TT)
                nc.gpsimd.tensor_tensor(out_scale[:, par, :], alpha2[:], gate_now[:, par, :],
                                        ALU.mult).then_inc(scale_ready, 1)
                nc.gpsimd.tensor_tensor(out_bias[:], bias2[:], gate_now[:, par, :], ALU.mult).then_inc(
                    out_bias_ready, 1)
                pool.wait_ge(out_bias_ready, v + 1)
                if known_from(v, 2):
                    pool.wait_ge(y_stored[par], moved_before(v, par))
                nc.gpsimd.tensor_tensor(y[:, par, :, :], x_in[:, par, :, :],
                                        out_bias[:].unsqueeze(1).broadcast_to([P, TT, E]),
                                        ALU.add).then_inc(y_started, 1)

            def add_result(v, par, t):
                pool.wait_ge(scaled, TT * v + t + 1)
                pool.wait_ge(y_started, v + 1)
                nc.gpsimd.tensor_tensor(y[:, par, t, :], y[:, par, t, :], y_tmp[:, t % 2, :],
                                        ALU.add).then_inc(y_ready, 1)

            def iteration(v, par, batch):
                cur, prev, nxt = known_below(v, units), known_from(v, 1), known_below(v, units - 1)
                for f in range(FC):
                    if f == 0 and cur:
                        start_y(v, par)
                    if f % 2 == 1 and prev:
                        add_result(v - 1, 1 - par, f // 2)
                    if f == 3 and nxt:
                        power(v + 1)
                    if f in (6, 7) and nxt:
                        low_h(v + 1, 1 - par, f - 6)

            power(0)
            low_h(0, 0, 0)
            low_h(0, 0, 1)
            pool.wait_ge(w_loaded, 16 * 5)
            pool.wait_ge(alphas_ready, 1)
            over_units(pool, iteration)





_X = "L0_attn_hidden_states"


def kernel(**inputs):
    import numpy as np
    import concourse.bacc as bacc
    from concourse.bass_utils import run_bass_kernel_spmd

    a = {name: np.ascontiguousarray(value) for name, value in inputs.items()}
    heads = np.zeros((P, EC, H), np.float32)
    for c in range(EC):
        for p in range(P):
            heads[p, c, (c * P + p) // D] = 1.0
    def by_partition(v):
        return np.ascontiguousarray(v.reshape(-1, P).T)

    laid = {
        "x": a[_X], "wq": a["L0_attn_Wq"], "bq": by_partition(a["L0_attn_bq"]), "wk": a["L0_attn_Wk"], "bk": by_partition(a["L0_attn_bk"]),
        "wv": a["L0_attn_Wv"], "bv": by_partition(a["L0_attn_bv"]), "wo": a["L0_attn_Wo"], "bo": a["L0_attn_bo"],
        "w1": a["L0_ffn_w1"], "w1t": np.ascontiguousarray(a["L0_ffn_w1"].T), "b1": by_partition(a["L0_ffn_b1"]),
        "w2t": np.ascontiguousarray(a["L0_ffn_w2"].T), "b2": a["L0_ffn_b2"],
        "ct": np.ascontiguousarray(a["L0_c"].T), "wmod": a["L0_wmod"],
        "wkt": np.ascontiguousarray(a["L0_attn_Wk"].T), "ident": np.eye(P, dtype=np.float32), "heads": heads,
    }
    nc = bacc.Bacc("TRN2", target_bir_lowering=False, num_devices=1)
    args = [nc.dram_tensor(f"in_{n}", v.shape, F32, kind="ExternalInput").ap() for n, v in laid.items()]
    out = nc.dram_tensor("out", (NB, L, E), F32, kind="ExternalOutput").ap()
    adaln_block(nc, *args, out)
    result = run_bass_kernel_spmd(nc, [{f"in_{n}": v for n, v in laid.items()}], core_ids=[0])
    return result.results[0]["out"]
```

```python
from contextlib import ExitStack

import concourse.bass as bass
from concourse import mybir

ALU = mybir.AluOpType
ACT = mybir.ActivationFunctionType
AX = mybir.AxisListType.X
F32 = mybir.dt.float32
F32R = mybir.dt.float32r

P = 128
NB = 8
L = 1024
E = 256
EC = E // P
H = 16
D = E // H
WIN = 64
PAIRS = 4
HALF = L // 2
F = 1024
FC = F // P
ITEMS = 8
SCALE = float(D) ** -0.5
EPS = 1e-5
DVE_BEFORE, DVE_FIRST, DVE_STEPS = 20, 21, 22
F_BEFORE, F_STEPS = 6, 6
SA, CA, SB, CB = range(4)
MOD_BLOCKS = (0, 1, 3, 4)
TOK = 512
TT = TOK // P


def positive(value):
    return not isinstance(value, int) or value > 0


def known_below(value, limit):
    return not isinstance(value, int) or value < limit


def known_from(value, limit):
    return not isinstance(value, int) or value >= limit


def batches(engine, iteration):
    iteration(0, 0)
    with engine.Fori(0, 2) as it:
        iteration(it * 2 + 1, 1)
        iteration(it * 2 + 2, 0)
    for b in range(5, NB + 1):
        iteration(b, b % 2)


def stage_count(b, k):
    return 12 * b + k


def small_count(name, b):
    order = ("turn", "mix", "flip", "wo0", "wo1")
    n = b + 1 if name in ("wo0", "wo1") else b
    if isinstance(n, int) and n == 0:
        return 1 + order.index(name)
    at = 5 * n - 2 + 1 + order.index(name)
    if isinstance(n, int) and n == NB:
        return at - 3
    return at


def adaln_block(nc, x, wq, bq, wk, bk, wv, bv, wo, bo, w1, w1t, b1, w2t, b2, ct, wmod, wkt, ident_in, hmask_in, out):
    x1 = nc.dram_tensor("x1_between", (NB, L, E), F32).ap()
    gates = nc.dram_tensor("gates_between", (NB, 2 * E), F32).ap()

    with ExitStack() as ctx:
        def sb(name, shape, dt=F32, stack=ctx):
            return stack.enter_context(nc.sbuf_tensor(name, shape, dt))

        def sem(name, stack=ctx):
            return stack.enter_context(nc.semaphore(name))

        ident = sb("ident", [P, P])
        modt = sb("modt", [P, 4, EC, NB])
        neg_half = sb("neg_half", [P, 4])
        psum = [ctx.enter_context(nc.psum_tensor(f"bank{i}", [P, 512], F32)) for i in range(8)]

        phase_a(nc, psum, ident, modt, neg_half, x, wq, bq, wk, bk, wv, bv, wo, bo, ct, wmod, wkt, ident_in,
                hmask_in, gates, x1)
        phase_b(nc, psum, ident, modt, neg_half, w1, w1t, b1, w2t, b2, gates, x1, out)


def phase_a(nc, psum, ident, modt, neg_half, x, wq, bq, wk, bk, wv, bv, wo, bo, ct, wmod, wkt, ident_in, hmask_in,
            gates, x1):
    with ExitStack() as ctx:
        def sb(name, shape, dt=F32):
            return ctx.enter_context(nc.sbuf_tensor(name, shape, dt))

        def sem(name):
            return ctx.enter_context(nc.semaphore(name))

        WQ, WK, WV, WO = range(4)
        w_q = sb("w_q", [P, EC, E])
        w_v = sb("w_v", [P, EC, E])
        w_kt = sb("w_kt", [P, EC, E])
        w_hi = sb("w_hi", [P, 4, EC, E], F32R)
        w_lo = sb("w_lo", [P, 4, EC, E], F32R)
        bias_q = sb("bias_q", [P, EC])
        bias_k = sb("bias_k", [P, EC])
        bias_v = sb("bias_v", [P, EC])
        bias_o = sb("bias_o", [P, E])
        hmask = sb("hmask", [P, EC, H])
        c_t = sb("c_t", [P, EC, NB])
        c_e = sb("c_e", [P, EC, NB])
        c_s = sb("c_s", [P, EC, NB])

        x_ln = sb("x_ln", [P, 8, E])
        x_res = sb("x_res", [P, 8, E])
        x_n = sb("x_n", [P, 8, E])
        stats = sb("stats", [P, 8, 6])
        mean_var = sb("mean_var", [P, 8, 2])
        var_eps = sb("var_eps", [P, 8])
        rstd = sb("rstd", [P, 8])
        mod_now = sb("mod_now", [P, 2, 2, EC])
        h_full = sb("h_full", [P, 2, 512])
        h_hi = sb("h_hi", [P, EC, L], F32R)
        h_lo = sb("h_lo", [P, EC, L], F32R)
        k_parts = sb("k_parts", [P, 2, EC, HALF], F32R)
        k_diag = [sb(f"k_diag{c}", [P, 2, 2, 4, HALF], F32R) for c in range(EC)]
        q_stack = sb("q_stack", [P, 4, PAIRS, 3, WIN], F32R)
        v_diag = sb("v_diag", [P, 2, 2 * PAIRS, H // 2, 2 * D])
        prob = sb("prob", [P, 4, 512])
        row_max = sb("row_max", [P, 2, 8])
        row_sum = sb("row_sum", [P, 2, 8])
        row_inv = sb("row_inv", [P, 2, 8])
        prob_t = sb("prob_t", [P, 2, 512])
        ctx_full = sb("ctx_full", [P, HALF])
        ctx_hi = sb("ctx_hi", [P, EC, HALF], F32R)
        ctx_lo = sb("ctx_lo", [P, EC, HALF], F32R)
        attn_tmp = sb("attn_tmp", [P, 512])
        gate_now = sb("gate_now", [P, E])
        gated_bias = sb("gated_bias", [P, E])
        g_stats = sb("g_stats", [NB, 6])
        g_mean_var = sb("g_mean_var", [NB, 2])
        g_var_eps = sb("g_var_eps", [NB, 1])
        g_rstd = sb("g_rstd", [NB, 1])
        h_tok = sb("h_tok", [P, EC, NB])
        q_tok = sb("q_tok", [P, EC, NB])
        keys = sb("keys", [P, NB, 2, EC, H], F32R)
        key_bias = sb("key_bias", [H, NB])
        key_now = sb("key_now", [P, 2, 2, EC, H], F32R)
        key_bias_now = sb("key_bias_now", [H, 2])
        g_score = sb("g_score", [H, L])
        g_max = sb("g_max", [H, 1])
        g_shift = sb("g_shift", [H, 1])
        g_sum = sb("g_sum", [H, 1])
        g_inv = sb("g_inv", [H, 1])
        g_prob_t = sb("g_prob_t", [P, 8, H])
        g_mix = sb("g_mix", [P, EC, NB, H])
        g_ctx = sb("g_ctx", [P, EC, NB])
        g_parts = sb("g_parts", [P, 2, EC, NB], F32R)
        ones_r = sb("ones_r", [1, P], F32R)
        bias_parts = sb("bias_parts", [1, 2, E], F32R)

        ones_row = h_full[0:1, 0, 0:P]
        gate_rows = attn_tmp[0:NB, :]
        gate_sign = ctx_full[0:NB, :]
        wmod_sb = v_diag[:, :, :, :, :].rearrange("p a w j d -> p (a w j d)")[:, 0:EC * 6 * E].rearrange(
            "p (c n) -> p c n", c=EC)
        w_k = x_res[:, 0:2, :]
        w_o = x_res[:, 2:4, :]
        g_x = x_res[0:NB, 4, :]
        g_x_n = x_res[0:NB, 5, :]
        q_heads = g_mix
        g_rows = g_score[:, 0:E]
        g_x_again = w_q[0:NB, 0, :]
        g_gate = w_q[0:NB, 1, :]
        g_mod = w_kt[:, :, 0:P]
        g_all = w_kt[:, :, P:2 * P]

        stage = psum[0:2]
        score = psum[2:4]
        turned = psum[4:6]
        mixed = psum[6]
        small = psum[7]

        x_ln_loaded = sem("x_ln_loaded")
        x_res_loaded = sem("x_res_loaded")
        gate_loaded = sem("gate_loaded")
        x1_stored = sem("x1_stored")
        setup_loaded = sem("setup_loaded")
        gates_stored = sem("gates_stored")
        gates_ready = sem("gates_ready")
        silu_exp = sem("silu_exp")
        silu_ready = sem("silu_ready")
        mod_full = sem("mod_full")
        weights_ready = sem("weights_ready")
        zeroed = sem("zeroed")
        v_zeroed = sem("v_zeroed")
        dve_step = sem("dve_step")
        stats_ready = sem("stats_ready")
        rstd_ready = sem("rstd_ready")
        xn_ready = sem("xn_ready")
        mod_now_ready = sem("mod_now_ready")
        stage_full = sem("stage_full")
        stage_free = sem("stage_free")
        h_lo_ready = sem("h_lo_ready")
        k_lo_ready = sem("k_lo_ready")
        k_diag_loaded = [sem(f"k_diag_loaded{c}") for c in range(EC)]
        q_lo_ready = sem("q_lo_ready")
        score_full = sem("score_full")
        shifted = sem("shifted")
        exp_done = sem("exp_done")
        inv_ready = sem("inv_ready")
        prob_ready = sem("prob_ready")
        turned_full = sem("turned_full")
        turned_copied = sem("turned_copied")
        mix_done = sem("mix_done")
        ctx_hi_ready = sem("ctx_hi_ready")
        ctx_lo_ready = sem("ctx_lo_ready")
        small_full = sem("small_full")
        small_free = sem("small_free")
        g_shift_ready = sem("g_shift_ready")
        g_exp_done = sem("g_exp_done")
        g_sum_ready = sem("g_sum_ready")
        res_added = sem("res_added")
        mod_loaded = sem("mod_loaded")
        key_now_ready = sem("key_now_ready")
        g_x_loaded = sem("g_x_loaded")
        g_var_ready = sem("g_var_ready")
        g_rstd_ready = sem("g_rstd_ready")
        g_taken = sem("g_taken")
        g_product = sem("g_product")
        g_again_loaded = sem("g_again_loaded")
        g_stored = sem("g_stored")
        stack_zeroed = sem("stack_zeroed")

        N_ROLLED = 6
        N_STORED = 5
        G_NORM, G_H, G_QUERY, G_KEYS, G_MOD, G_CTX, G_OUT = range(1, 8)
        G_TURNED, G_QUERIED, G_DIRECTED, G_VALUED, G_PROJECTED = range(1, 6)

        def transfers(batch, tile):
            view = batch.rearrange("(p r) e -> r p e", r=256)
            yield view[1:65, :, :], tile[0:64, 0:4, :]
            yield view[65:129, :, :], tile[0:64, 4:8, :]
            yield view[129:193, :, :], tile[64:128, 0:4, :]
            yield view[193:256, :, :], tile[64:127, 4:8, :]
            yield view[0:1, 1:4, :], tile[127:128, 4:7, :]
            yield view[0:1, 0:1, :], tile[127:128, 7:8, :]

        def lagging(b, i, lag):
            j = i - lag
            n, j = (b - 1, j + ITEMS) if j < 0 else (b + 1, j - ITEMS) if j >= ITEMS else (b, j)
            return (n, j) if known_from(n, 0) and known_below(n, NB) else None

        block = ctx.enter_context(nc.Block())

        @block.sync
        def _(sp):
            def load_x(dst, loaded, b):
                for dram, tile in transfers(x[b], dst):
                    sp.dma_start(tile, dram).then_inc(loaded, 16)

            def load_gate(b):
                row = gates[b:b + 1, 0:E] if isinstance(b, int) else gates[bass.ds(b, 1), 0:E]
                sp.dma_start(gate_now[:], row.broadcast_to([P, E])).then_inc(gate_loaded, 16)

            def spread_keys(b, c):
                if positive(ITEMS * b - ITEMS + 4 + 4 * c):
                    sp.wait_ge(score_full, ITEMS * b - ITEMS + 4 + 4 * c)
                sp.wait_ge(k_lo_ready, (b + 1) * 2 + c - 1)
                for head in range(8):
                    for dup in range(2):
                        to = 64 * dup + D * (head % 4)
                        sp.dma_start(k_diag[c][to:to + D, :, head // 4, head % 4, :].bitcast(F32),
                                     k_parts[D * head:D * head + D, :, c, :].bitcast(F32)).then_inc(k_diag_loaded[c], 16)

            load_x(x_ln, x_ln_loaded, 0)
            sp.dma_start(g_x, x[:, 0, :]).then_inc(g_x_loaded, 16)
            sp.dma_start(c_t[:], ct.rearrange("(c p) b -> p c b", p=P)).then_inc(mod_loaded, 16)
            sp.dma_start(wmod_sb, wmod.rearrange("(c p) n -> p c n", p=P)).then_inc(mod_loaded, 16)
            for dst, src in (
                (ident[:], ident_in),
                (w_k, wk.rearrange("(c p) n -> p c n", p=P)),
                (w_q[:], wq.rearrange("(c p) n -> p c n", p=P)),
                (w_v[:], wv.rearrange("(c p) n -> p c n", p=P)),
                (w_o, wo.rearrange("(c p) n -> p c n", p=P)),
                (w_kt[:], wkt.rearrange("(c p) n -> p c n", p=P)),
                (hmask[:], hmask_in),
                (bias_q[:], bq),
                (bias_k[:], bk),
                (bias_v[:], bv),
                (bias_o[:], bo.rearrange("(a n) -> a n", a=1).broadcast_to([P, E])),
            ):
                sp.dma_start(dst, src).then_inc(setup_loaded, 16)
            sp.wait_ge(gates_ready, 1)
            sp.dma_start(gates, gate_rows).then_inc(gates_stored, 16)
            sp.wait_ge(xn_ready, 2)
            load_x(x_ln, x_ln_loaded, 1)
            sp.wait_ge(zeroed, 2)
            spread_keys(0, 0)
            sp.wait_ge(weights_ready, 1)
            sp.wait_ge(g_taken, G_KEYS)
            load_x(x_res, x_res_loaded, 0)
            sp.wait_ge(gates_stored, 16)
            load_gate(0)
            sp.dma_start(g_x_again, x[:, 0, :]).then_inc(g_again_loaded, 16)
            sp.dma_start(g_gate, gates[:, 0:E]).then_inc(g_again_loaded, 16)

            def iteration(b, par):
                if known_below(b, NB):
                    spread_keys(b, 1)
                if known_below(b, NB - 1):
                    spread_keys(b + 1, 0)
                if known_below(b, NB - 2):
                    sp.wait_ge(xn_ready, 2 * b + 4)
                    load_x(x_ln, x_ln_loaded, b + 2)
                if known_from(b, 1):
                    sp.wait_ge(res_added, 4 * b)
                    for n, (dram, tile) in enumerate(transfers(x1[b - 1], x_res)):
                        if n < N_STORED:
                            sp.dma_start(dram, tile).then_inc(x1_stored, 16)
                    if known_below(b, NB):
                        sp.wait_ge(x1_stored, 16 * N_STORED * b)
                        load_x(x_res, x_res_loaded, b)
                        load_gate(b)

            batches(sp, iteration)
            sp.wait_ge(g_taken, G_OUT)
            sp.dma_start(x1[:, 0, :], g_x_again).then_inc(g_stored, 16)
            sp.wait_ge(x1_stored, 16 * N_STORED * NB)
            sp.wait_ge(g_stored, 16)

        @block.tensor
        def _(pe):
            def exact(dst, stationary, moving, fresh=True):
                n = len(stationary)
                for k in range(n):
                    (s_hi, s_lo), (m_hi, m_lo) = stationary[k], moving[k]
                    nc.tensor.matmul(dst, s_hi, m_hi, start=fresh and k == 0, stop=False)
                    nc.tensor.matmul(dst, s_hi, m_lo, start=False, stop=False)
                    done = nc.tensor.matmul(dst, s_lo, m_hi, start=False, stop=k == n - 1)
                return done

            def stage_bank(b, k):
                if positive(stage_count(b, k) - 2):
                    pe.wait_ge(stage_free, stage_count(b, k) - 2)
                if k in (5, 8):
                    pe.wait_ge(k_lo_ready, 2 * b + (1 if k == 5 else 2))
                if k == 9:
                    pe.wait_ge(q_lo_ready, 2 * b + 1)
                if k == 2 and known_from(b, 1):
                    pe.wait_ge(q_lo_ready, 2 * b)
                return stage[k % 2]

            def small_bank(name, b):
                if positive(small_count(name, b) - 1):
                    pe.wait_ge(small_free, small_count(name, b) - 1)
                return small

            def turn_x(b, half, c, k):
                if c == 0:
                    pe.wait_ge(xn_ready, 2 * b + half + 1)
                bank = stage_bank(b, k)
                for p in range(4):
                    done = nc.tensor.transpose(bank[:, p * P:(p + 1) * P],
                                               x_n[:, 4 * half + p, c * P:(c + 1) * P], ident[:])
                done.then_inc(stage_full, 1)

            def project(b, which, c, k):
                pe.wait_ge(stage_free, stage_count(b, 2))
                pe.wait_ge(h_lo_ready, 4 * b + 2)
                bank = stage_bank(b, k)
                cols = slice(c * P, (c + 1) * P)
                exact(bank[:], [(w_hi[:, which, e, cols], w_lo[:, which, e, cols]) for e in range(EC)],
                      [(h_hi[:, e, 0:HALF], h_lo[:, e, 0:HALF]) for e in range(EC)]).then_inc(stage_full, 1)

            def project_v(b, two, k):
                bank = stage_bank(b, k)
                for p in (2 * two, 2 * two + 1):
                    tok = slice(p * P, (p + 1) * P)
                    done = exact(bank[:, (p % 2) * E:(p % 2 + 1) * E],
                                 [(h_hi[:, e, tok], h_lo[:, e, tok]) for e in range(EC)],
                                 [(w_hi[:, WV, e, :], w_lo[:, WV, e, :]) for e in range(EC)])
                done.then_inc(stage_full, 1)

            def global_tokens():
                pe.wait_ge(g_taken, G_NORM)
                for c in range(EC):
                    done = nc.tensor.transpose(small[:, c * NB:(c + 1) * NB], g_x_n[:, c * P:(c + 1) * P],
                                               ident[0:NB, 0:NB])
                done.then_inc(g_product, 1)

            def global_queries():
                pe.wait_ge(g_taken, G_H)
                for c in range(EC):
                    for e in range(EC):
                        done = nc.tensor.matmul(small[:, (2 + c) * NB:(3 + c) * NB], w_q[:, e, c * P:(c + 1) * P],
                                                h_tok[:, e, :], start=e == 0, stop=e == EC - 1)
                done.then_inc(g_product, 1)

            def global_directions():
                pe.wait_ge(g_taken, G_QUERY)
                for e in range(EC):
                    for c in range(EC):
                        nc.tensor.matmul(mixed[:, e * P:(e + 1) * P], w_kt[:, c, e * P:(e + 1) * P],
                                         q_heads[:, c, :, :], start=c == 0, stop=c == EC - 1)
                for n in range(NB):
                    for c in range(EC):
                        done = nc.tensor.matmul(small[0:H, 4 * NB + n:4 * NB + n + 1], q_heads[:, c, n, :],
                                                bias_k[:, c:c + 1], start=c == 0, stop=c == EC - 1)
                done.then_inc(g_product, 1)

            def global_values():
                pe.wait_ge(stage_free, stage_count(NB - 1, 12))
                pe.wait_ge(g_taken, G_MOD)
                for c in range(EC):
                    for e in range(EC):
                        done = nc.tensor.matmul(stage[0][:, c * P:(c + 1) * P], w_v[:, e, c * P:(c + 1) * P],
                                                g_mod[:, e, :], start=e == 0, stop=e == EC - 1)
                done.then_inc(g_product, 1)

            def global_out():
                pe.wait_ge(g_taken, G_CTX)
                exact(stage[1][0:NB, 0:E], [(g_parts[:, 0, c, :], g_parts[:, 1, c, :]) for c in range(EC)],
                      [(w_hi[:, WO, c, :], w_lo[:, WO, c, :]) for c in range(EC)]).then_inc(g_product, 1)

            def global_scores(b, par, half, k):
                if half == 0:
                    pe.wait_ge(key_now_ready, b + 1)
                    pe.wait_ge(stage_free, stage_count(b, 5))
                    pe.wait_ge(h_lo_ready, 4 * b + 4)
                bank = stage_bank(b, k)
                tok = slice(half * HALF, (half + 1) * HALF)
                exact(bank[0:H, :], [(key_now[:, par, 0, e, :], key_now[:, par, 1, e, :]) for e in range(EC)],
                      [(h_hi[:, e, tok], h_lo[:, e, tok]) for e in range(EC)]).then_inc(stage_full, 1)

            def global_turn(b):
                pe.wait_ge(g_exp_done, b + 1)
                bank = small_bank("turn", b)
                for t in range(8):
                    done = nc.tensor.matmul(bank[:, t * H:(t + 1) * H], g_score[:, t * P:(t + 1) * P],
                                            ident[0:H, 0:H], start=True, stop=True)
                done.then_inc(small_full, 1)

            def global_mix(b):
                bank = small_bank("mix", b)
                for t in range(8):
                    done = nc.tensor.matmul(bank[0:H, 0:E], g_prob_t[:, t, :], x_n[:, t, :],
                                            start=t == 0, stop=t == 7)
                done.then_inc(small_full, 1)

            def global_flip(b):
                bank = small_bank("flip", b)
                for e in range(EC):
                    done = nc.tensor.matmul(bank[:, e * H:(e + 1) * H], g_rows[:, e * P:(e + 1) * P],
                                            ident[0:H, 0:H], start=True, stop=True)
                done.then_inc(small_full, 1)

            def window_out(b, two):
                pe.wait_ge(ctx_hi_ready, 2 * b + 2)
                pe.wait_ge(ctx_lo_ready, 2 * b + 2)
                bank = small_bank(f"wo{two}", b)
                for p in (2 * two, 2 * two + 1):
                    tok = slice(p * P, (p + 1) * P)
                    part = bank[:, (p % 2) * E:(p % 2 + 1) * E]
                    nc.tensor.matmul(part, ones_r[:], bias_parts[:, 0, :], start=True, stop=False)
                    nc.tensor.matmul(part, ones_r[:], bias_parts[:, 1, :], start=False, stop=False)
                    done = exact(part, [(ctx_hi[:, c, tok], ctx_lo[:, c, tok]) for c in range(EC)],
                                 [(w_hi[:, WO, c, :], w_lo[:, WO, c, :]) for c in range(EC)], fresh=False)
                done.then_inc(small_full, 1)

            def scores(b, i):
                c, p = divmod(i, 4)
                if p == 0:
                    pe.wait_ge(k_diag_loaded[c], 256 * b + 256)
                    pe.wait_ge(stage_free, stage_count(b, 7 + 5 * c))
                    pe.wait_ge(q_lo_ready, 2 * b + c + 1)
                if positive(ITEMS * b + i - 1):
                    pe.wait_ge(shifted, ITEMS * b + i - 1)
                bank = score[i % 2]
                for g in range(2):
                    for par in range(2):
                        for part in range(2):
                            done = nc.tensor.matmul(
                                bank[:, g * E:(g + 1) * E],
                                q_stack[:, 2 * c + g, p, par:par + 2, :],
                                k_diag[c][:, part, g, :, p * P + par * WIN:p * P + (par + 1) * WIN],
                                start=par + part == 0, stop=par + part == 2)
                done.then_inc(score_full, 1)

            def turn_probs(b, i):
                pe.wait_ge(prob_ready, ITEMS * b + i + 1)
                if positive(ITEMS * b + i - 1):
                    pe.wait_ge(turned_copied, ITEMS * b + i - 1)
                for j in range(4):
                    done = nc.tensor.transpose(turned[i % 2][:, j * P:(j + 1) * P],
                                               prob[:, i % 4, j * P:(j + 1) * P], ident[:])
                done.then_inc(turned_full, 1)

            def mix(b, i, par_b):
                c, p = divmod(i, 4)
                pe.wait_ge(turned_copied, ITEMS * b + i + 1)
                if i == 0:
                    pe.wait_ge(stage_free, stage_count(b, 11))
                if p == 0:
                    if positive(2 * b + c):
                        pe.wait_ge(ctx_hi_ready, 2 * b + c)
                for j in range(4):
                    for par in range(2):
                        done = nc.tensor.matmul(
                            mixed[32 * j:32 * j + 32, p * P + par * WIN:p * P + (par + 1) * WIN],
                            v_diag[:, par_b, 2 * p + par, 4 * c + j, :],
                            prob_t[:, i % 2, j * P + par * WIN:j * P + (par + 1) * WIN],
                            start=True, stop=True)
                done.then_inc(mix_done, 1)

            def stage_one(b, par, i):
                if i == 2:
                    turn_x(b, 0, 0, 1)
                    turn_x(b, 0, 1, 2)
                if i == 3:
                    project(b, WK, 0, 3)
                if i == 4:
                    turn_x(b, 1, 0, 4)
                    turn_x(b, 1, 1, 5)
                if i == 5:
                    project(b, WK, 1, 6)
                    project(b, WQ, 0, 7)
                if i == 6:
                    project_v(b, 0, 8)
                    global_scores(b, par, 0, 9)
                if i == 7:
                    global_scores(b, par, 1, 10)
                    project_v(b, 1, 11)

            def rest(b, i):
                cur, prev = known_below(b, NB), known_from(b, 1)
                if i == 0 and cur:
                    project(b, WQ, 1, 12)
                    global_turn(b)
                if i == 1 and cur:
                    global_mix(b)
                if i == 2 and cur:
                    global_flip(b)
                if i == 4 and prev:
                    window_out(b - 1, 0)
                if i == 5 and prev:
                    window_out(b - 1, 1)

            def iteration(b, par):
                for i in range(ITEMS):
                    if (at := lagging(b, i, -1)) is not None:
                        scores(*at)
                    if (at := lagging(b, i, 2)) is not None:
                        turn_probs(*at)
                    if (at := lagging(b, i, 3)) is not None:
                        mix(*at, par if i >= 3 else 1 - par)
                    rest(b, i)
                    if known_below(b, NB - 1):
                        stage_one(b + 1, 1 - par, i)
                    if isinstance(b, int) and b == NB - 1 and i == 5:
                        global_values()
                    if isinstance(b, int) and b == NB - 1 and i == 6:
                        global_out()

            pe.wait_ge(mod_loaded, 32)
            pe.wait_ge(silu_ready, 1)
            for j, blk in enumerate(MOD_BLOCKS):
                for c in range(EC):
                    col = (j * EC + c) * NB
                    for e in range(EC):
                        nc.tensor.matmul(turned[0][:, col:col + NB],
                                         wmod_sb[:, e, blk * E + c * P:blk * E + (c + 1) * P], c_s[:, e, :],
                                         start=e == 0, stop=e == EC - 1)
            for j, blk in enumerate((2, 5)):
                for e in range(EC):
                    done = nc.tensor.matmul(turned[1][0:NB, j * E:(j + 1) * E], c_s[:, e, :],
                                            wmod_sb[:, e, blk * E:(blk + 1) * E], start=e == 0, stop=e == EC - 1)
            done.then_inc(mod_full, 1)
            pe.wait_ge(setup_loaded, 16 * 11)
            pe.wait_ge(weights_ready, 1)
            for i in range(ITEMS):
                if i == 3:
                    global_tokens()
                if i == 5:
                    global_queries()
                if i == 6:
                    global_directions()
                stage_one(0, 0, i)
            scores(0, 0)
            batches(pe, iteration)

        @block.scalar
        def _(act):
            def filled(b, k):
                act.wait_ge(stage_full, stage_count(b, k))
                return stage[k % 2]

            def modulate(b, par, half, c, k):
                bank = filled(b, k)
                act.wait_ge(mod_now_ready, b + 1)
                if positive(4 * b + 2 * half + c - 1):
                    act.wait_ge(h_lo_ready, 4 * b + 2 * half + c - 1)
                cols = slice(half * HALF, (half + 1) * HALF)
                shift, scale = mod_now[:, par, 0, c:c + 1], mod_now[:, par, 1, c:c + 1]
                nc.scalar.activation(h_full[:, c, :], bank[:], ACT.Identity, scale=scale, bias=shift)
                nc.scalar.activation(h_hi[:, c, cols], bank[:], ACT.Identity, scale=scale,
                                     bias=shift).then_inc(stage_free, 1)

            def take_keys(b, c, k):
                bank = filled(b, k)
                if positive(256 * b):
                    act.wait_ge(k_diag_loaded[c], 256 * b)
                nc.scalar.activation(k_parts[:, 0, c, :], bank[:], ACT.Identity,
                                     bias=bias_k[:, c:c + 1]).then_inc(stage_free, 1)

            def take_queries(b, c, k):
                bank = filled(b, k)
                if positive(ITEMS * b - ITEMS + 4 * c + 4):
                    act.wait_ge(score_full, ITEMS * b - ITEMS + 4 * c + 4)
                for g in range(2):
                    rows = slice(64 * g, 64 * g + 64)
                    done = nc.scalar.activation(q_stack[rows, 2 * c + g, :, 0:3:2, :],
                                                bank[rows, :].rearrange("r (p a q) -> r p a q", a=2, q=WIN),
                                                ACT.Identity, bias=bias_q[rows, c:c + 1])
                done.then_inc(stage_free, 1)

            def take_values(b, par_b, two, k):
                bank = filled(b, k)
                if isinstance(b, int) and b == 0:
                    act.wait_ge(v_zeroed, 1)
                if positive(ITEMS * b - ITEMS):
                    act.wait_ge(mix_done, ITEMS * b - ITEMS)
                for par in range(2):
                    src = bank[64 * par:64 * par + 64, :].rearrange("k (p j h d) -> k p j h d", p=2, j=H // 2, h=2)
                    for h2 in range(2):
                        dst = v_diag[64 * h2:64 * h2 + 64, par_b, 4 * two + par:4 * two + par + 3:2, :,
                                     D * h2:D * h2 + D]
                        done = nc.scalar.copy(dst, src[:, :, :, h2, :])
                done.then_inc(stage_free, 1)

            def take_global_scores(b, par, half, k):
                bank = filled(b, k)
                if known_from(b, 1):
                    act.wait_ge(small_full, small_count("flip", b - 1))
                nc.scalar.activation(g_score[:, half * HALF:(half + 1) * HALF], bank[0:H, :], ACT.Identity,
                                     bias=key_bias_now[:, par:par + 1]).then_inc(stage_free, 1)

            def global_exp(b):
                act.wait_ge(g_shift_ready, b + 1)
                nc.scalar.activation(g_score[:], g_score[:], ACT.Exp, scale=SCALE,
                                     bias=g_shift[:, 0:1]).then_inc(g_exp_done, 1)

            def exponentials(b, i):
                act.wait_ge(shifted, ITEMS * b + i + 1)
                nc.scalar.activation(prob[:, i % 4, :], prob[:, i % 4, :], ACT.Exp, scale=SCALE).then_inc(exp_done, 1)

            def copy_turned(b, i):
                act.wait_ge(turned_full, ITEMS * b + i + 1)
                if positive(ITEMS * b + i - 1):
                    act.wait_ge(mix_done, ITEMS * b + i - 1)
                nc.scalar.copy(prob_t[:, i % 2, :], turned[i % 2][:]).then_inc(turned_copied, 1)

            def take_context(b, c):
                act.wait_ge(mix_done, ITEMS * b + 4 * c + 4)
                if positive(2 * b + c):
                    act.wait_ge(ctx_lo_ready, 2 * b + c)
                if known_from(b, 1):
                    act.wait_ge(small_full, small_count("wo1", b - 1))
                nc.scalar.activation(ctx_full[:], mixed[:], ACT.Identity, bias=bias_v[:, c:c + 1])
                nc.scalar.activation(ctx_hi[:, c, :], mixed[:], ACT.Identity,
                                     bias=bias_v[:, c:c + 1]).then_inc(ctx_hi_ready, 1)

            def stage_one(b, par, i):
                if i == 2:
                    modulate(b, par, 0, 0, 1)
                    modulate(b, par, 0, 1, 2)
                if i == 3:
                    take_keys(b, 0, 3)
                if i == 4:
                    modulate(b, par, 1, 0, 4)
                    modulate(b, par, 1, 1, 5)
                if i == 5:
                    take_keys(b, 1, 6)
                    take_queries(b, 0, 7)
                if i == 6:
                    take_values(b, par, 0, 8)
                    take_global_scores(b, par, 0, 9)
                if i == 7:
                    take_global_scores(b, par, 1, 10)
                    take_values(b, par, 1, 11)

            def iteration(b, par):
                cur = known_below(b, NB)
                for i in range(ITEMS):
                    if cur:
                        if i == 0:
                            global_exp(b)
                        exponentials(b, i)
                    if (at := lagging(b, i, 2)) is not None:
                        copy_turned(*at)
                    if i == 0 and cur:
                        take_queries(b, 1, 12)
                    if i == 2 and known_from(b, 1):
                        take_context(b - 1, 1)
                    if i == 6 and cur:
                        take_context(b, 0)
                    if known_below(b, NB - 1):
                        stage_one(b + 1, 1 - par, i)

            act.wait_ge(mod_loaded, 32)
            nc.scalar.activation(c_e[:], c_t[:], ACT.Exp, scale=-1.0).then_inc(silu_exp, 1)
            act.wait_ge(setup_loaded, 16 * 11)
            for i in range(ITEMS):
                stage_one(0, 0, i)
            batches(act, iteration)

        @block.vector
        def _(dve):
            steps = {"at": 0}

            def step():
                steps["at"] = steps["at"] + 1
                return steps["at"]

            def shift_scores(b, i):
                rows = score[i % 2][:].rearrange("q (h k) -> q h k", k=WIN)
                dve.wait_ge(score_full, ITEMS * b + i + 1)
                nc.vector.reduce_max(row_max[:, i % 2, :], rows, AX).then_inc(dve_step, 1)
                dve.wait_ge(dve_step, step())
                if positive(ITEMS * b + i - 3):
                    dve.wait_ge(turned_full, ITEMS * b + i - 3)
                nc.vector.tensor_tensor(prob[:, i % 4, :].rearrange("q (h k) -> q h k", k=WIN), rows,
                                        row_max[:, i % 2, :].unsqueeze(2).broadcast_to([P, 8, WIN]),
                                        ALU.subtract).then_inc(shifted, 1)

            def invert_sums(b, i):
                dve.wait_ge(exp_done, ITEMS * b + i + 1)
                nc.vector.reduce_sum(row_sum[:, i % 2, :], prob[:, i % 4, :].rearrange("q (h k) -> q h k", k=WIN), AX).then_inc(dve_step, 1)
                dve.wait_ge(dve_step, step())
                if positive(ITEMS * b + i - 1):
                    dve.wait_ge(prob_ready, ITEMS * b + i - 1)
                nc.vector.reciprocal(row_inv[:, i % 2, :], row_sum[:, i % 2, :]).then_inc(inv_ready, 1)

            def statistics(b, tiles, half=None):
                for t in tiles:
                    dve.wait_ge(x_ln_loaded, 16 * N_ROLLED * (b + 1))
                    done = nc.vector.bn_stats(stats[:, t, :], x_ln[:, t, :])
                if half is None:
                    return
                done.then_inc(dve_step, 1)
                dve.wait_ge(dve_step, step())
                if positive(2 * b + half):
                    dve.wait_ge(rstd_ready, 2 * b + half)
                nc.vector.memset(var_eps[:, 4 * half:4 * half + 4], EPS)
                for t in range(4 * half, 4 * half + 4):
                    done = nc.vector.bn_aggr(mean_var[:, t, :], stats[:, t, :])
                done.then_inc(dve_step, 1)
                dve.wait_ge(dve_step, step())
                part = var_eps[:, 4 * half:4 * half + 4]
                nc.vector.tensor_tensor(part, part, mean_var[:, 4 * half:4 * half + 4, 1],
                                        ALU.add).then_inc(stats_ready, 1)

            def normalise(b, half):
                dve.wait_ge(rstd_ready, 2 * b + half + 1)
                if known_from(b, 1):
                    dve.wait_ge(small_full, small_count("mix", b - 1))
                for t in range(4 * half, 4 * half + 4):
                    done = nc.vector.tensor_scalar(x_n[:, t, :], x_ln[:, t, :], mean_var[:, t, 0:1],
                                                   rstd[:, t:t + 1], ALU.subtract, ALU.mult)
                done.then_inc(xn_ready, 1)

            def pick_modulation(b, par):
                src = modt[:, SA:CA + 1, :, b:b + 1] if isinstance(b, int) else modt[:, SA:CA + 1, :, bass.ds(b, 1)]
                nc.vector.tensor_copy(mod_now[:, par, :, :],
                                      src.rearrange("p j c b -> p j (c b)")).then_inc(mod_now_ready, 1)

            def pick_keys(b, par):
                at = slice(b, b + 1) if isinstance(b, int) else bass.ds(b, 1)
                nc.vector.tensor_copy(key_bias_now[:, par:par + 1], key_bias[:, at])
                nc.vector.tensor_copy(key_now[:, par, :, :, :].rearrange("p s c h -> p (s c h)"),
                                      keys[:, at, :, :, :].rearrange("p b s c h -> p (b s c h)").bitcast(F32)
                                      ).then_inc(key_now_ready, 1)

            def low_keys(b, c):
                dve.wait_ge(stage_free, stage_count(b, 3 + 3 * c))
                nc.vector.scalar_tensor_tensor(k_parts[:, 1, c, :], stage[(3 + 3 * c) % 2][:], bias_k[:, c:c + 1],
                                               k_parts[:, 0, c, :].bitcast(F32), ALU.add,
                                               ALU.subtract).then_inc(k_lo_ready, 1)

            def low_queries(b, c):
                dve.wait_ge(stage_free, stage_count(b, 7 + 5 * c))
                for g in range(2):
                    rows, other = slice(64 * g, 64 * g + 64), slice(64 - 64 * g, 128 - 64 * g)
                    for par in range(2):
                        done = nc.vector.scalar_tensor_tensor(
                            q_stack[other, 2 * c + g, :, 2 * par, :],
                            stage[(7 + 5 * c) % 2][rows, :].rearrange("r (p a q) -> r p a q", a=2, q=WIN)[:, :, par, :],
                            bias_q[rows, c:c + 1], q_stack[rows, 2 * c + g, :, 2 * par, :].bitcast(F32),
                            ALU.add, ALU.subtract)
                done.then_inc(q_lo_ready, 1)

            def global_statistics():
                dve.wait_ge(g_x_loaded, 16)
                nc.vector.bn_stats(g_stats[:], g_x).then_inc(dve_step, 1)
                dve.wait_ge(dve_step, step())
                nc.vector.bn_aggr(g_mean_var[:], g_stats[:]).then_inc(dve_step, 1)
                dve.wait_ge(dve_step, step())
                nc.vector.tensor_scalar_add(g_var_eps[:], g_mean_var[:, 1:2], EPS).then_inc(g_var_ready, 1)

            def normalise_tokens():
                dve.wait_ge(g_rstd_ready, 1)
                nc.vector.tensor_scalar(g_x_n, g_x, g_mean_var[:, 0:1], g_rstd[:], ALU.subtract,
                                        ALU.mult).then_inc(g_taken, 1)

            def modulate_tokens():
                dve.wait_ge(g_product, G_TURNED)
                turned_x = small[:, 0:EC * NB].rearrange("p (c b) -> p c b", c=EC)
                nc.vector.tensor_tensor(h_tok[:], turned_x, modt[:, CA, :, :], ALU.mult).then_inc(dve_step, 1)
                dve.wait_ge(dve_step, step())
                nc.vector.tensor_tensor(h_tok[:], h_tok[:], modt[:, SA, :, :], ALU.add).then_inc(g_taken, 1)

            def take_queries():
                dve.wait_ge(g_product, G_QUERIED)
                queries = small[:, 2 * NB:4 * NB].rearrange("p (c b) -> p c b", c=EC)
                nc.vector.tensor_tensor(q_tok[:], queries, bias_q[:].unsqueeze(2).broadcast_to([P, EC, NB]),
                                        ALU.add).then_inc(dve_step, 1)
                dve.wait_ge(dve_step, step())
                for c in range(EC):
                    done = nc.vector.tensor_tensor(q_heads[:, c, :, :],
                                                   hmask[:, c, :].unsqueeze(1).broadcast_to([P, NB, H]),
                                                   q_tok[:, c, :].unsqueeze(2).broadcast_to([P, NB, H]), ALU.mult)
                done.then_inc(g_taken, 1)

            def take_directions():
                dve.wait_ge(g_product, G_DIRECTED)
                nc.vector.tensor_copy(key_bias[:], small[0:H, 4 * NB:5 * NB])
                for e in range(EC):
                    done = nc.vector.tensor_copy(keys[:, :, 0, e, :],
                                                 mixed[:, e * P:(e + 1) * P].rearrange("p (b h) -> p b h", h=H))
                done.then_inc(dve_step, 1)
                dve.wait_ge(dve_step, step())
                for e in range(EC):
                    done = nc.vector.tensor_tensor(keys[:, :, 1, e, :],
                                                   mixed[:, e * P:(e + 1) * P].rearrange("p (b h) -> p b h", h=H),
                                                   keys[:, :, 0, e, :].bitcast(F32), ALU.subtract)
                done.then_inc(g_taken, 1)
                dve.wait_ge(g_taken, G_KEYS)

            def global_shift(b):
                dve.wait_ge(stage_free, stage_count(b, 10))
                nc.vector.reduce_max(g_max[:], g_score[:], AX).then_inc(dve_step, 1)
                dve.wait_ge(dve_step, step())
                nc.vector.tensor_scalar_mul(g_shift[:], g_max[:], -SCALE).then_inc(g_shift_ready, 1)

            def global_sum(b):
                dve.wait_ge(g_exp_done, b + 1)
                nc.vector.reduce_sum(g_sum[:], g_score[:], AX).then_inc(g_sum_ready, 1)
                dve.wait_ge(g_sum_ready, b + 1)
                nc.vector.reciprocal(g_inv[:], g_sum[:]).then_inc(dve_step, 1)
                step()

            def take_turn(b):
                dve.wait_ge(small_full, small_count("turn", b))
                nc.vector.tensor_copy(g_prob_t[:].rearrange("p t h -> p (t h)"),
                                      small[:, 0:8 * H]).then_inc(small_free, 1)

            def take_mix(b):
                dve.wait_ge(small_full, small_count("mix", b))
                nc.vector.tensor_scalar_mul(g_rows, small[0:H, 0:E], g_inv[:, 0:1]).then_inc(small_free, 1)

            def take_flip(b):
                dve.wait_ge(small_full, small_count("flip", b))
                at = slice(b, b + 1) if isinstance(b, int) else bass.ds(b, 1)
                nc.vector.tensor_copy(g_mix[:, :, at, :].rearrange("p c b h -> p c (b h)"),
                                      small[:, 0:EC * H].rearrange("p (c h) -> p c h", c=EC)).then_inc(small_free, 1)

            def modulate_mix():
                mod = g_mod.rearrange("p c (b h) -> p c b h", h=H)
                dve.wait_ge(small_free, small_count("flip", NB - 1))
                for c in range(EC):
                    done = nc.vector.tensor_tensor(mod[:, c, :, :], g_mix[:, c, :, :],
                                                   modt[:, CA, c, :].unsqueeze(2).broadcast_to([P, NB, H]), ALU.mult)
                done.then_inc(dve_step, 1)
                dve.wait_ge(dve_step, step())
                for c in range(EC):
                    done = nc.vector.tensor_tensor(mod[:, c, :, :], mod[:, c, :, :],
                                                   modt[:, SA, c, :].unsqueeze(2).broadcast_to([P, NB, H]), ALU.add)
                done.then_inc(g_taken, 1)

            def take_global_values():
                dve.wait_ge(g_product, G_VALUED)
                for c in range(EC):
                    done = nc.vector.tensor_tensor(g_all[:, c, :].rearrange("p (b h) -> p b h", h=H),
                                                   stage[0][:, c * P:(c + 1) * P].rearrange("p (b h) -> p b h", h=H),
                                                   hmask[:, c, :].unsqueeze(1).broadcast_to([P, NB, H]), ALU.mult)
                done.then_inc(dve_step, 1)
                dve.wait_ge(dve_step, step())
                nc.vector.reduce_sum(g_ctx[:], g_all.rearrange("p c (b h) -> p c b h", h=H), AX).then_inc(dve_step, 1)
                dve.wait_ge(dve_step, step())
                nc.vector.tensor_tensor(g_ctx[:], g_ctx[:], bias_v[:].unsqueeze(2).broadcast_to([P, EC, NB]),
                                        ALU.add).then_inc(dve_step, 1)
                dve.wait_ge(dve_step, step())
                nc.vector.tensor_copy(g_parts[:, 0, :, :], g_ctx[:]).then_inc(dve_step, 1)
                dve.wait_ge(dve_step, step())
                nc.vector.tensor_tensor(g_parts[:, 1, :, :], g_ctx[:], g_parts[:, 0, :, :].bitcast(F32),
                                        ALU.subtract).then_inc(g_taken, 1)

            def finish_tokens():
                dve.wait_ge(g_product, G_PROJECTED)
                dve.wait_ge(g_again_loaded, 32)
                nc.vector.tensor_tensor(g_rows[0:NB, :], stage[1][0:NB, 0:E], bias_o[0:NB, :],
                                        ALU.add).then_inc(dve_step, 1)
                dve.wait_ge(dve_step, step())
                nc.vector.tensor_tensor(g_rows[0:NB, :], g_rows[0:NB, :], g_gate, ALU.mult).then_inc(dve_step, 1)
                dve.wait_ge(dve_step, step())
                nc.vector.tensor_tensor(g_x_again, g_x_again, g_rows[0:NB, :], ALU.add).then_inc(g_taken, 1)

            def gate_out(name, b, tiles):
                dve.wait_ge(small_full, small_count(name, b))
                dve.wait_ge(gate_loaded, 16 * b + 16)
                added = 4 * b if name == "wo0" else 4 * b + 3
                if positive(added):
                    dve.wait_ge(res_added, added)
                nc.vector.tensor_tensor(attn_tmp[:, 0:tiles * E].rearrange("p (t e) -> p t e", e=E),
                                        small[:, 0:tiles * E].rearrange("p (t e) -> p t e", e=E),
                                        gate_now[:].unsqueeze(1).broadcast_to([P, tiles, E]),
                                        ALU.mult).then_inc(small_free, 1)

            def slot_steps(b, par, i):
                cur, prev, nxt = known_below(b, NB), known_from(b, 1), known_below(b, NB - 1)
                if i == 0 and nxt:
                    pick_modulation(b + 1, 1 - par)
                    pick_keys(b + 1, 1 - par)
                    statistics(b + 1, (0, 1))
                if i == 0 and cur:
                    low_queries(b, 1)
                    take_turn(b)
                if i == 1:
                    if nxt:
                        statistics(b + 1, (2, 3), 0)
                    if cur:
                        take_mix(b)
                if i == 2:
                    if nxt:
                        normalise(b + 1, 0)
                    if cur:
                        take_flip(b)
                if i == 3 and nxt:
                    statistics(b + 1, (4, 5, 6, 7), 1)
                    low_keys(b + 1, 0)
                if i == 4:
                    if nxt:
                        normalise(b + 1, 1)
                    if prev:
                        gate_out("wo0", b - 1, 2)
                if i == 5 and prev:
                    gate_out("wo1", b - 1, 2)
                if nxt:
                    if i == 5:
                        low_keys(b + 1, 1)
                        low_queries(b + 1, 0)
                    if i == 7:
                        global_shift(b + 1)

            def iteration(b, par):
                if not isinstance(b, int) or 1 <= b < NB:
                    steps["at"] = DVE_BEFORE + DVE_FIRST + DVE_STEPS * (b - 1)
                for i in range(ITEMS):
                    if known_below(b, NB):
                        shift_scores(b, i)
                        if i == 0:
                            global_sum(b)
                    if (at := lagging(b, i, 1)) is not None:
                        invert_sums(*at)
                    slot_steps(b, par, i)
                    if isinstance(b, int) and b == NB - 1:
                        if i == 4:
                            modulate_mix()
                        if i == 5:
                            take_global_values()
                        if i == 6:
                            finish_tokens()

            nc.vector.memset(q_stack[:].bitcast(F32), 0.0)
            nc.vector.memset(ones_row, 1.0)
            nc.vector.memset(neg_half[:], -0.5).then_inc(stack_zeroed, 1)
            statistics(0, (0, 1, 2, 3), 0)
            dve.wait_ge(silu_exp, 1)
            nc.vector.tensor_scalar_add(c_e[:], c_e[:], 1.0).then_inc(dve_step, 1)
            dve.wait_ge(dve_step, step())
            nc.vector.reciprocal(c_e[:], c_e[:]).then_inc(dve_step, 1)
            dve.wait_ge(dve_step, step())
            nc.vector.tensor_tensor(c_s[:], c_e[:], c_t[:], ALU.mult).then_inc(silu_ready, 1)
            statistics(0, (4, 5, 6, 7), 1)
            global_statistics()
            normalise(0, 0)
            normalise_tokens()
            dve.wait_ge(setup_loaded, 16 * 11)
            for which, src in ((WK, w_k), (WQ, w_q[:]), (WV, w_v[:]), (WO, w_o)):
                nc.vector.tensor_copy(w_hi[:, which, :, :], src).then_inc(dve_step, 1)
                dve.wait_ge(dve_step, step())
                nc.vector.tensor_tensor(w_lo[:, which, :, :], src, w_hi[:, which, :, :].bitcast(F32), ALU.subtract)
            nc.vector.tensor_copy(bias_parts[:, 0, :], bias_o[0:1, :])
            nc.vector.tensor_copy(ones_r[:], ones_row).then_inc(dve_step, 1)
            dve.wait_ge(dve_step, step())
            nc.vector.tensor_tensor(bias_parts[:, 1, :], bias_o[0:1, :], bias_parts[:, 0, :].bitcast(F32),
                                    ALU.subtract).then_inc(weights_ready, 1)
            dve.wait_ge(mod_full, 1)
            mods = turned[0][:, 0:4 * EC * NB].rearrange("p (j n) -> p j n", j=4)
            flat = modt[:].rearrange("p j c b -> p j (c b)")
            nc.vector.tensor_copy(flat[:, SA:CB:2, :], mods[:, SA:CB:2, :])
            nc.vector.tensor_scalar_add(flat[:, CA:CB + 1:2, :], mods[:, CA:CB + 1:2, :], 1.0).then_inc(dve_step, 1)
            dve.wait_ge(dve_step, step())
            pick_modulation(0, 0)
            low_keys(0, 0)
            normalise(0, 1)
            modulate_tokens()
            raw = turned[1][0:NB, :]
            nc.vector.tensor_scalar(gate_sign, raw, 0.0, 2.0, ALU.is_ge, ALU.mult)
            nc.vector.tensor_scalar_mul(gate_rows, raw, -1.0).then_inc(dve_step, 1)
            dve.wait_ge(dve_step, step())
            nc.vector.scalar_tensor_tensor(gate_rows, gate_rows, 0.25, raw, ALU.max, ALU.max).then_inc(dve_step, 1)
            dve.wait_ge(dve_step, step())
            nc.vector.scalar_tensor_tensor(gate_rows, gate_sign, 1.0, gate_rows, ALU.subtract,
                                           ALU.mult).then_inc(gates_ready, 1)
            low_keys(0, 1)
            take_queries()
            take_directions()
            pick_keys(0, 0)
            low_queries(0, 0)
            global_shift(0)
            assert steps["at"] == DVE_BEFORE, steps
            batches(dve, iteration)

        @block.gpsimd
        def _(pool):
            def power(b, half):
                pool.wait_ge(stats_ready, 2 * b + half + 1)
                if positive(2 * b - 1 + half):
                    pool.wait_ge(xn_ready, 2 * b - 1 + half)
                cols = slice(4 * half, 4 * half + 4)
                nc.gpsimd.tensor_tensor(rstd[:, cols], var_eps[:, cols], neg_half[:],
                                        ALU.pow).then_inc(rstd_ready, 1)

            def low_h(b, half, c):
                pool.wait_ge(stage_free, stage_count(b, (1 if half == 0 else 4) + c))
                cols = slice(half * HALF, (half + 1) * HALF)
                nc.gpsimd.tensor_tensor(h_lo[:, c, cols], h_full[:, c, :], h_hi[:, c, cols].bitcast(F32),
                                        ALU.subtract).then_inc(h_lo_ready, 1)

            def low_context(b, c):
                pool.wait_ge(ctx_hi_ready, 2 * b + c + 1)
                nc.gpsimd.tensor_tensor(ctx_lo[:, c, :], ctx_full[:], ctx_hi[:, c, :].bitcast(F32),
                                        ALU.subtract).then_inc(ctx_lo_ready, 1)

            def normalise_probs(b, i):
                pool.wait_ge(inv_ready, ITEMS * b + i + 1)
                rows = prob[:, i % 4, :].rearrange("q (h k) -> q h k", k=WIN)
                nc.gpsimd.tensor_tensor(rows, rows, row_inv[:, i % 2, :].unsqueeze(2).broadcast_to([P, 8, WIN]),
                                        ALU.mult).then_inc(prob_ready, 1)

            def gate_bias(b):
                pool.wait_ge(gate_loaded, 16 * b + 16)
                nc.gpsimd.tensor_tensor(gated_bias[:], bias_o[:], gate_now[:], ALU.mult).then_inc(res_added, 1)

            def add_bias(b):
                pool.wait_ge(res_added, 4 * b + 1)
                pool.wait_ge(x_res_loaded, 16 * N_ROLLED * (b + 1))
                part = x_res[:, 4:8, :]
                nc.gpsimd.tensor_tensor(part, part, gated_bias[:].unsqueeze(1).broadcast_to([P, 4, E]),
                                        ALU.add).then_inc(res_added, 1)

            def add_out(name, b, first, tiles):
                pool.wait_ge(small_free, small_count(name, b))
                pool.wait_ge(x_res_loaded, 16 * N_ROLLED * (b + 1))
                part = x_res[:, first:first + tiles, :].rearrange("p t e -> p (t e)")
                nc.gpsimd.tensor_tensor(part, part, attn_tmp[:, 0:tiles * E], ALU.add).then_inc(res_added, 1)

            def slot_steps(b, i):
                cur, prev, nxt = known_below(b, NB), known_from(b, 1), known_below(b, NB - 1)
                if i == 1 and nxt:
                    power(b + 1, 0)
                if i == 1 and prev:
                    gate_bias(b - 1)
                if i == 2 and nxt:
                    low_h(b + 1, 0, 0)
                    low_h(b + 1, 0, 1)
                if i == 2 and prev:
                    add_bias(b - 1)
                if i == 3 and prev:
                    low_context(b - 1, 1)
                if i == 3 and nxt:
                    power(b + 1, 1)
                if i == 4:
                    if nxt:
                        low_h(b + 1, 1, 0)
                        low_h(b + 1, 1, 1)
                    if prev:
                        add_out("wo0", b - 1, 0, 2)
                if i == 5:
                    if prev:
                        add_out("wo1", b - 1, 2, 2)
                if i == 7 and cur:
                    low_context(b, 0)

            def iteration(b, par):
                for i in range(ITEMS):
                    if (at := lagging(b, i, 1)) is not None:
                        normalise_probs(*at)
                    slot_steps(b, i)

            nc.gpsimd.memset(k_diag[0][:].bitcast(F32), 0.0).then_inc(zeroed, 1)
            pool.wait_ge(stack_zeroed, 1)
            power(0, 0)
            power(0, 1)
            pool.wait_ge(g_var_ready, 1)
            nc.gpsimd.tensor_tensor(g_rstd[:], g_var_eps[:], neg_half[0:NB, 0:1], ALU.pow).then_inc(g_rstd_ready, 1)
            pool.wait_ge(mod_full, 1)
            nc.gpsimd.memset(v_diag[:], 0.0).then_inc(v_zeroed, 1)
            low_h(0, 0, 0)
            low_h(0, 0, 1)
            nc.gpsimd.memset(k_diag[1][:].bitcast(F32), 0.0).then_inc(zeroed, 1)
            low_h(0, 1, 0)
            low_h(0, 1, 1)
            batches(pool, iteration)


def phase_b(nc, psum, ident, modt, neg_half, w1, w1t, b1, w2t, b2, gates, x1, out):
    units = NB * L // TOK
    DOWN_AT = (2, 4, 6, 7)
    x1_units = x1.rearrange("b (u t p) e -> (b u) p t e", p=P, t=TT)
    out_units = out.rearrange("b (u t p) e -> (b u) p t e", p=P, t=TT)

    with ExitStack() as ctx:
        def sb(name, shape, dt=F32):
            return ctx.enter_context(nc.sbuf_tensor(name, shape, dt))

        def sem(name):
            return ctx.enter_context(nc.semaphore(name))

        w1_raw = sb("w1_raw", [P, FC, E])
        w1t_raw = sb("w1t_raw", [P, EC, F])
        w2t_raw = sb("w2t_raw", [P, FC, E])
        w2_abs = sb("w2_abs", [P, FC, E])
        w1_abs = sb("w1_abs", [P, FC, E])
        w1_sign = sb("w1_sign", [P, EC, F], F32R)
        w2_sign = sb("w2_sign", [P, FC, E], F32R)
        mean_ones = sb("mean_ones", [P, P])
        w1_sum = sb("w1_sum", [P, FC])
        alpha1 = sb("alpha1", [P, FC])
        bias1 = sb("bias1", [P, FC])
        alpha2 = sb("alpha2", [P, E])
        bias2 = sb("bias2", [P, E])
        x_in = sb("x_in", [P, 2, TT, E])
        stats = sb("f_stats", [P, TT, 6])
        mean_var = sb("f_mean_var", [P, TT, 2])
        var_eps = sb("f_var_eps", [P, TT])
        rstd = sb("f_rstd", [P, TT])
        x_n = sb("f_x_n", [P, TT, E])
        mod_now = sb("f_mod_now", [P, 2, 2, EC])
        gate_now = sb("f_gate_now", [P, 2, E])
        out_scale = sb("out_scale", [P, 2, E])
        out_bias = sb("out_bias", [P, E])
        h_full = sb("f_h_full", [P, EC, TOK])
        h_hi = sb("f_h_hi", [P, 2, EC, TOK], F32R)
        h_lo = sb("f_h_lo", [P, 2, EC, TOK], F32R)
        g_full = sb("g_full", [P, 2, TOK])
        act_hi = sb("act_hi", [P, 2, FC, TOK], F32R)
        act_lo = sb("act_lo", [P, 2, FC, TOK], F32R)
        y_tmp = sb("y_tmp", [P, 2, E])
        y = sb("y", [P, 2, TT, E])

        hidden = psum[0:4]
        turned = psum[4:6]
        result = psum[6:8]

        w_loaded = sem("w_loaded")
        x_in_loaded = [sem(f"x_in_loaded{i}") for i in range(2)]
        f_gate_loaded = [sem(f"f_gate_loaded{i}") for i in range(2)]
        y_stored = [sem(f"y_stored{i}") for i in range(2)]
        signs_ready = sem("signs_ready")
        abs_ready = sem("abs_ready")
        alpha2_full = sem("alpha2_full")
        alphas_ready = sem("alphas_ready")
        f_step = sem("f_step")
        f_stats_ready = sem("f_stats_ready")
        f_rstd_ready = sem("f_rstd_ready")
        f_xn_ready = sem("f_xn_ready")
        f_mod_ready = sem("f_mod_ready")
        f_turned_full = sem("f_turned_full")
        f_h_hi_ready = sem("f_h_hi_ready")
        f_h_lo_ready = sem("f_h_lo_ready")
        hidden_full = sem("hidden_full")
        gelu_done = sem("gelu_done")
        act_lo_ready = sem("act_lo_ready")
        result_full = sem("result_full")
        scaled = sem("scaled")
        y_started = sem("y_started")
        y_ready = sem("y_ready")
        scale_ready = sem("scale_ready")
        out_bias_ready = sem("out_bias_ready")

        def moved_before(v, par):
            return 8 * (v - par)

        def over_units(engine, iteration):
            iteration(0, 0, 0)
            iteration(1, 1, 0)
            with engine.Fori(1, (units - 2) // 2) as it:
                iteration(it * 2, 0, it)
                iteration(it * 2 + 1, 1, it)
            for v in range(units - 2, units + 1):
                iteration(v, v % 2, v // 2)

        block = ctx.enter_context(nc.Block())

        @block.sync
        def _(sp):
            def load(v, par, batch):
                src = x1_units[v] if isinstance(v, int) else x1_units[bass.ds(v, 1)].rearrange(
                    "u p t e -> (u p) t e")
                row = gates[batch:batch + 1, E:2 * E] if isinstance(batch, int) else gates[bass.ds(batch, 1), E:2 * E]
                sp.dma_start(x_in[:, par, :, :], src).then_inc(x_in_loaded[par], 16)
                sp.dma_start(gate_now[:, par, :], row.broadcast_to([P, E])).then_inc(f_gate_loaded[par], 16)

            load(0, 0, 0)
            load(1, 1, 0)
            for dst, src in (
                (w1t_raw[:], w1t.rearrange("(c p) n -> p c n", p=P)),
                (w1_raw[:], w1.rearrange("(c p) n -> p c n", p=P)),
                (w2t_raw[:], w2t.rearrange("(c p) n -> p c n", p=P)),
                (bias1[:], b1),
                (bias2[:], b2.rearrange("(a n) -> a n", a=1).broadcast_to([P, E])),
            ):
                sp.dma_start(dst, src).then_inc(w_loaded, 16)

            def iteration(v, par, batch):
                if known_below(v, units - 2):
                    sp.wait_ge(y_started, v + 1)
                    load(v + 2, par, batch + 1)
                if known_from(v, 1):
                    sp.wait_ge(y_ready, TT * v)
                    dst = out_units[v - 1] if isinstance(v, int) else out_units[bass.ds(v - 1, 1)].rearrange(
                        "u p t e -> (u p) t e")
                    sp.dma_start(dst, y[:, 1 - par, :, :]).then_inc(y_stored[1 - par], 16)

            over_units(sp, iteration)
            sp.wait_ge(y_stored[0], 16 * units // 2)
            sp.wait_ge(y_stored[1], 16 * units // 2)

        @block.tensor
        def _(pe):
            def turn_x(v, c):
                pe.wait_ge(f_xn_ready, v + 1)
                if positive(2 * v + c - 1):
                    pe.wait_ge(f_h_hi_ready, 2 * v + c - 1)
                for t in range(TT):
                    done = nc.tensor.transpose(turned[c][:, t * P:(t + 1) * P], x_n[:, t, c * P:(c + 1) * P],
                                               ident[:])
                done.then_inc(f_turned_full, 1)

            def up(v, par, f):
                if f == 0:
                    pe.wait_ge(f_h_hi_ready, 2 * v + 2)
                    pe.wait_ge(f_h_lo_ready, 2 * v + 2)
                if positive(FC * v + f - 3):
                    pe.wait_ge(gelu_done, FC * v + f - 3)
                for e in range(EC):
                    for h in (h_hi, h_lo):
                        done = nc.tensor.matmul(hidden[f % 4][:], w1_sign[:, e, f * P:(f + 1) * P],
                                                h[:, par, e, :], start=e == 0 and h is h_hi,
                                                stop=e == EC - 1 and h is h_lo)
                done.then_inc(hidden_full, 1)

            def down(v, par, t):
                pe.wait_ge(act_lo_ready, FC * v + FC)
                if positive(TT * v + t - 1):
                    pe.wait_ge(scaled, TT * v + t - 1)
                for f in range(FC):
                    for a in (act_hi, act_lo):
                        done = nc.tensor.matmul(result[t % 2][:, 0:E], a[:, par, f, t * P:(t + 1) * P],
                                                w2_sign[:, f, :], start=f == 0 and a is act_hi,
                                                stop=f == FC - 1 and a is act_lo)
                done.then_inc(result_full, 1)

            def iteration(v, par, batch):
                cur, prev = known_below(v, units), known_from(v, 1)
                for f in range(FC):
                    if cur:
                        up(v, par, f)
                    if f in DOWN_AT and prev:
                        down(v - 1, 1 - par, DOWN_AT.index(f))
                    if f in (3, 4) and known_below(v, units - 1):
                        turn_x(v + 1, f - 3)

            turn_x(0, 0)
            turn_x(0, 1)
            pe.wait_ge(signs_ready, 1)
            pe.wait_ge(abs_ready, 1)
            for f in range(FC):
                done = nc.tensor.matmul(result[0][:, 0:E], mean_ones[:], w2_abs[:, f, :], start=f == 0, stop=f == FC - 1)
            done.then_inc(alpha2_full, 1)
            pe.wait_ge(alphas_ready, 1)
            over_units(pe, iteration)

        @block.scalar
        def _(act):
            def modulate(v, par, c):
                act.wait_ge(f_turned_full, 2 * v + c + 1)
                act.wait_ge(f_mod_ready, v + 1)
                if positive(2 * v + c - 1):
                    act.wait_ge(f_h_lo_ready, 2 * v + c - 1)
                shift, scale = mod_now[:, par, 0, c:c + 1], mod_now[:, par, 1, c:c + 1]
                nc.scalar.activation(h_full[:, c, :], turned[c][:], ACT.Identity, scale=scale, bias=shift)
                nc.scalar.activation(h_hi[:, par, c, :], turned[c][:], ACT.Identity, scale=scale,
                                     bias=shift).then_inc(f_h_hi_ready, 1)

            def gelu(v, par, f):
                act.wait_ge(hidden_full, FC * v + f + 1)
                if positive(FC * v + f - 1):
                    act.wait_ge(act_lo_ready, FC * v + f - 1)
                if f == 0:
                    if positive(TT * v - TT):
                        act.wait_ge(result_full, TT * v - TT)
                done = nc.scalar.activation(g_full[:, f % 2, :], hidden[f % 4][:], ACT.Gelu,
                                            scale=alpha1[:, f:f + 1], bias=bias1[:, f:f + 1])
                if f % 2 == 0:
                    done = nc.scalar.activation(act_hi[:, par, f, :], hidden[f % 4][:], ACT.Gelu,
                                                scale=alpha1[:, f:f + 1], bias=bias1[:, f:f + 1])
                done.then_inc(gelu_done, 1)

            def iteration(v, par, batch):
                for f in range(FC):
                    if known_below(v, units):
                        gelu(v, par, f)
                    if f in (3, 4) and known_below(v, units - 1):
                        modulate(v + 1, 1 - par, f - 3)

            act.wait_ge(w_loaded, 16 * 5)
            nc.scalar.activation(w1_sign[:], w1t_raw[:], ACT.Sign)
            nc.scalar.activation(w2_sign[:], w2t_raw[:], ACT.Sign).then_inc(signs_ready, 1)
            modulate(0, 0, 0)
            modulate(0, 0, 1)
            act.wait_ge(alphas_ready, 1)
            over_units(act, iteration)

        @block.vector
        def _(dve):
            steps = {"at": 0}

            def step():
                steps["at"] = steps["at"] + 1
                return steps["at"]

            def statistics(v, par):
                dve.wait_ge(x_in_loaded[par], moved_before(v, par) + 16)
                for t in range(TT):
                    done = nc.vector.bn_stats(stats[:, t, :], x_in[:, par, t, :])
                done.then_inc(f_step, 1)
                dve.wait_ge(f_step, step())
                nc.vector.memset(var_eps[:], EPS)
                for t in range(TT):
                    done = nc.vector.bn_aggr(mean_var[:, t, :], stats[:, t, :])
                done.then_inc(f_step, 1)
                dve.wait_ge(f_step, step())
                nc.vector.tensor_tensor(var_eps[:], var_eps[:], mean_var[:, :, 1], ALU.add).then_inc(f_stats_ready, 1)

            def normalise(v, par):
                dve.wait_ge(f_rstd_ready, v + 1)
                if positive(2 * v):
                    dve.wait_ge(f_turned_full, 2 * v)
                for t in range(TT):
                    done = nc.vector.tensor_scalar(x_n[:, t, :], x_in[:, par, t, :], mean_var[:, t, 0:1],
                                                   rstd[:, t:t + 1], ALU.subtract, ALU.mult)
                done.then_inc(f_xn_ready, 1)

            def pick_modulation(v, par, batch):
                src = modt[:, SB:CB + 1, :, batch:batch + 1] if isinstance(batch, int) else modt[
                    :, SB:CB + 1, :, bass.ds(batch, 1)]
                nc.vector.tensor_copy(mod_now[:, par, :, :],
                                      src.rearrange("p j c b -> p j (c b)")).then_inc(f_mod_ready, 1)

            def low_activation(v, par, f):
                dve.wait_ge(gelu_done, FC * v + f + 1)
                if f % 2 == 1:
                    nc.vector.tensor_copy(act_hi[:, par, f, :], g_full[:, f % 2, :]).then_inc(f_step, 1)
                    dve.wait_ge(f_step, step())
                nc.vector.tensor_tensor(act_lo[:, par, f, :], g_full[:, f % 2, :],
                                        act_hi[:, par, f, :].bitcast(F32), ALU.subtract).then_inc(act_lo_ready, 1)

            def scale_result(v, par, t):
                dve.wait_ge(result_full, TT * v + t + 1)
                if positive(TT * v + t - 1):
                    dve.wait_ge(y_ready, TT * v + t - 1)
                if t == 0:
                    dve.wait_ge(scale_ready, v + 1)
                nc.vector.tensor_tensor(y_tmp[:, t % 2, :], result[t % 2][:, 0:E], out_scale[:, par, :],
                                        ALU.mult).then_inc(scaled, 1)

            def iteration(v, par, batch):
                if not isinstance(v, int) or 1 <= v < units - 1:
                    steps["at"] = F_BEFORE + F_STEPS * v
                cur, prev, nxt = known_below(v, units), known_from(v, 1), known_below(v, units - 1)
                for f in range(FC):
                    if cur:
                        low_activation(v, par, f)
                    if f in DOWN_AT and prev:
                        scale_result(v - 1, 1 - par, DOWN_AT.index(f))
                    if f == 0 and nxt:
                        pick_modulation(v + 1, 1 - par, batch + 1 if par else batch)
                    if f == 1 and nxt:
                        normalise(v + 1, 1 - par)
                    if f == 6 and known_below(v, units - 2):
                        statistics(v + 2, par)

            pick_modulation(0, 0, 0)
            statistics(0, 0)
            normalise(0, 0)
            statistics(1, 1)
            nc.vector.memset(mean_ones[:], 1.0 / F)
            dve.wait_ge(w_loaded, 16 * 5)
            for dst, src in ((w2_abs, w2t_raw), (w1_abs, w1_raw)):
                done = nc.vector.scalar_tensor_tensor(dst[:], src[:], -1.0, src[:], ALU.mult, ALU.max)
                if dst is w2_abs:
                    done.then_inc(abs_ready, 1)
            done.then_inc(f_step, 1)
            dve.wait_ge(f_step, step())
            nc.vector.reduce_sum(w1_sum[:], w1_abs[:], AX).then_inc(f_step, 1)
            dve.wait_ge(f_step, step())
            nc.vector.tensor_scalar_mul(alpha1[:], w1_sum[:], 1.0 / E)
            dve.wait_ge(alpha2_full, 1)
            nc.vector.tensor_copy(alpha2[:], result[0][:, 0:E]).then_inc(alphas_ready, 1)
            assert steps["at"] == F_BEFORE, steps
            over_units(dve, iteration)

        @block.gpsimd
        def _(pool):
            def power(v):
                pool.wait_ge(f_stats_ready, v + 1)
                if positive(v):
                    pool.wait_ge(f_xn_ready, v)
                nc.gpsimd.tensor_tensor(rstd[:], var_eps[:], neg_half[:], ALU.pow).then_inc(f_rstd_ready, 1)

            def low_h(v, par, c):
                pool.wait_ge(f_h_hi_ready, 2 * v + c + 1)
                nc.gpsimd.tensor_tensor(h_lo[:, par, c, :], h_full[:, c, :], h_hi[:, par, c, :].bitcast(F32),
                                        ALU.subtract).then_inc(f_h_lo_ready, 1)

            def start_y(v, par):
                pool.wait_ge(f_gate_loaded[par], moved_before(v, par) + 16)
                pool.wait_ge(x_in_loaded[par], moved_before(v, par) + 16)
                if positive(TT * v - TT):
                    pool.wait_ge(scaled, TT * v - TT)
                nc.gpsimd.tensor_tensor(out_scale[:, par, :], alpha2[:], gate_now[:, par, :],
                                        ALU.mult).then_inc(scale_ready, 1)
                nc.gpsimd.tensor_tensor(out_bias[:], bias2[:], gate_now[:, par, :], ALU.mult).then_inc(
                    out_bias_ready, 1)
                pool.wait_ge(out_bias_ready, v + 1)
                if known_from(v, 2):
                    pool.wait_ge(y_stored[par], moved_before(v, par))
                nc.gpsimd.tensor_tensor(y[:, par, :, :], x_in[:, par, :, :],
                                        out_bias[:].unsqueeze(1).broadcast_to([P, TT, E]),
                                        ALU.add).then_inc(y_started, 1)

            def add_result(v, par, t):
                pool.wait_ge(scaled, TT * v + t + 1)
                pool.wait_ge(y_started, v + 1)
                nc.gpsimd.tensor_tensor(y[:, par, t, :], y[:, par, t, :], y_tmp[:, t % 2, :],
                                        ALU.add).then_inc(y_ready, 1)

            def iteration(v, par, batch):
                cur, prev, nxt = known_below(v, units), known_from(v, 1), known_below(v, units - 1)
                for f in range(FC):
                    if f == 7 and known_below(v, units - 2):
                        power(v + 2)
                    if f in DOWN_AT and prev:
                        add_result(v - 1, 1 - par, DOWN_AT.index(f))
                    if f in (3, 4) and nxt:
                        low_h(v + 1, 1 - par, f - 3)
                    if f == 2 and cur:
                        start_y(v, par)

            power(0)
            power(1)
            low_h(0, 0, 0)
            low_h(0, 0, 1)
            pool.wait_ge(w_loaded, 16 * 5)
            pool.wait_ge(alphas_ready, 1)
            over_units(pool, iteration)





_X = "L0_attn_hidden_states"


def kernel(**inputs):
    import numpy as np
    import concourse.bacc as bacc
    from concourse.bass_utils import run_bass_kernel_spmd

    a = {name: np.ascontiguousarray(value) for name, value in inputs.items()}
    heads = np.zeros((P, EC, H), np.float32)
    for c in range(EC):
        for p in range(P):
            heads[p, c, (c * P + p) // D] = 1.0
    def by_partition(v):
        return np.ascontiguousarray(v.reshape(-1, P).T)

    laid = {
        "x": a[_X], "wq": a["L0_attn_Wq"], "bq": by_partition(a["L0_attn_bq"]), "wk": a["L0_attn_Wk"], "bk": by_partition(a["L0_attn_bk"]),
        "wv": a["L0_attn_Wv"], "bv": by_partition(a["L0_attn_bv"]), "wo": a["L0_attn_Wo"], "bo": a["L0_attn_bo"],
        "w1": a["L0_ffn_w1"], "w1t": np.ascontiguousarray(a["L0_ffn_w1"].T), "b1": by_partition(a["L0_ffn_b1"]),
        "w2t": np.ascontiguousarray(a["L0_ffn_w2"].T), "b2": a["L0_ffn_b2"],
        "ct": np.ascontiguousarray(a["L0_c"].T), "wmod": a["L0_wmod"],
        "wkt": np.ascontiguousarray(a["L0_attn_Wk"].T), "ident": np.eye(P, dtype=np.float32), "heads": heads,
    }
    nc = bacc.Bacc("TRN2", target_bir_lowering=False, num_devices=1)
    args = [nc.dram_tensor(f"in_{n}", v.shape, F32, kind="ExternalInput").ap() for n, v in laid.items()]
    out = nc.dram_tensor("out", (NB, L, E), F32, kind="ExternalOutput").ap()
    adaln_block(nc, *args, out)
    result = run_bass_kernel_spmd(nc, [{f"in_{n}": v for n, v in laid.items()}], core_ids=[0])
    return result.results[0]["out"]
```

```python
from contextlib import ExitStack

import concourse.bass as bass
from concourse import mybir

ALU = mybir.AluOpType
ACT = mybir.ActivationFunctionType
AX = mybir.AxisListType.X
F32 = mybir.dt.float32
F32R = mybir.dt.float32r

P = 128
NB = 8
L = 1024
E = 256
EC = E // P
H = 16
D = E // H
WIN = 64
PAIRS = 4
HALF = L // 2
F = 1024
FC = F // P
ITEMS = 8
SCALE = float(D) ** -0.5
EPS = 1e-5
DVE_BEFORE, DVE_FIRST, DVE_STEPS = 22, 21, 22
F_BEFORE, F_STEPS = 2, 6
SA, CA, SB, CB = range(4)
MOD_BLOCKS = (0, 1, 3, 4)
TOK = 512
TT = TOK // P
X1_STORES = 5


def positive(value):
    return not isinstance(value, int) or value > 0


def known_below(value, limit):
    return not isinstance(value, int) or value < limit


def known_from(value, limit):
    return not isinstance(value, int) or value >= limit


def batches(engine, iteration):
    iteration(0, 0)
    with engine.Fori(0, 2) as it:
        iteration(it * 2 + 1, 1)
        iteration(it * 2 + 2, 0)
    for b in range(5, NB + 1):
        iteration(b, b % 2)


def stage_count(b, k):
    return 12 * b + k


def small_count(name, b):
    order = ("turn", "mix", "flip", "wo0", "wo1")
    n = b + 1 if name in ("wo0", "wo1") else b
    if isinstance(n, int) and n == 0:
        return 1 + order.index(name)
    at = 5 * n - 2 + 1 + order.index(name)
    if isinstance(n, int) and n == NB:
        return at - 3
    return at


def adaln_block(nc, x, wq, bq, wk, bk, wv, bv, wo, bo, w1, w1t, b1, w2t, b2, ct, wmod, wkt, ident_in, hmask_in, out):
    x1 = nc.dram_tensor("x1_between", (NB, L, E), F32).ap()
    gates = nc.dram_tensor("gates_between", (NB, 2 * E), F32).ap()

    with ExitStack() as ctx:
        def sb(name, shape, dt=F32, stack=ctx):
            return stack.enter_context(nc.sbuf_tensor(name, shape, dt))

        def sem(name, stack=ctx):
            return stack.enter_context(nc.semaphore(name))

        ident = sb("ident", [P, P])
        modt = sb("modt", [P, 4, EC, NB])
        neg_half = sb("neg_half", [P, 4])
        x_pair = sb("x_pair", [P, 8, E])
        x_res = sb("x_res", [P, 8, E])
        h_full = sb("h_full", [P, 2, 512])
        first = FirstUnit(sb, sem)
        late = sb("late", [P, 2 * FC * E], F32R)
        ffn = FfnWeights(late, sb("ffn_small", [P, 2 * E + 2 * FC]))
        x1_stored = sem("x1_stored")
        x_in_loaded = [sem(f"x_in_loaded{i}") for i in range(2)]
        psum = [ctx.enter_context(nc.psum_tensor(f"bank{i}", [P, 512], F32)) for i in range(8)]

        phase_a(nc, psum, ident, modt, neg_half, x_pair, x_res, h_full, first, late, ffn, x1_stored, x_in_loaded,
                x, wq, bq, wk, bk, wv, bv, wo, bo, w1, w1t, b1, w2t, b2, ct, wmod, wkt, ident_in, hmask_in, gates, x1)
        phase_b(nc, psum, ident, modt, neg_half, x_pair, h_full, first, ffn, x1_stored, x_in_loaded, gates, x1, out)


class FfnWeights:

    def __init__(self, late, small):
        self.w1_sign = late[:, 0:FC * E].rearrange("p (c n) -> p c n", c=EC)
        self.w2_sign = late[:, FC * E:2 * FC * E].rearrange("p (c n) -> p c n", c=FC)
        self.alpha2, self.bias2 = small[:, 0:E], small[:, E:2 * E]
        self.alpha1, self.bias1 = small[:, 2 * E:2 * E + FC], small[:, 2 * E + FC:2 * E + 2 * FC]


class FirstUnit:

    def __init__(self, sb, sem):
        self.all_stats = sb("stats", [P, 8, 6])
        self.all_mean_var = sb("mean_var", [P, 8, 2])
        self.all_var_eps = sb("var_eps", [P, 8])
        self.all_rstd = sb("rstd", [P, 8])
        self.stats, self.mean_var = self.all_stats[:, 0:TT, :], self.all_mean_var[:, 0:TT, :]
        self.var_eps, self.rstd = self.all_var_eps[:, 0:TT], self.all_rstd[:, 0:TT]
        self.stats_ready = sem("f_stats_ready")
        self.rstd_ready = sem("f_rstd_ready")
        self.xn_ready = sem("f_xn_ready")


def ffn_units(dram):
    return dram.rearrange("b (u t p) e -> (b u) p t e", p=P, t=TT)


def phase_a(nc, psum, ident, modt, neg_half, x_pair, x_res, h_full, first, late, ffn, x1_stored, x_in_loaded,
            x, wq, bq, wk, bk, wv, bv, wo, bo, w1, w1t, b1, w2t, b2, ct, wmod, wkt, ident_in, hmask_in, gates, x1):
    with ExitStack() as ctx:
        def sb(name, shape, dt=F32):
            return ctx.enter_context(nc.sbuf_tensor(name, shape, dt))

        def sem(name):
            return ctx.enter_context(nc.semaphore(name))

        WQ, WK, WV, WO = range(4)
        w_q = sb("w_q", [P, EC, E])
        w_v = sb("w_v", [P, EC, E])
        w_kt = sb("w_kt", [P, EC, E])
        w_hi = sb("w_hi", [P, 4, EC, E], F32R)
        w_lo = sb("w_lo", [P, 4, EC, E], F32R)
        bias_q = sb("bias_q", [P, EC])
        bias_k = sb("bias_k", [P, EC])
        bias_v = sb("bias_v", [P, EC])
        bias_o = sb("bias_o", [P, E])
        hmask = sb("hmask", [P, EC, H])
        c_t = sb("c_t", [P, EC, NB])

        x_ln = x_pair
        x_n = sb("x_n", [P, 8, E])
        stats, mean_var = first.all_stats, first.all_mean_var
        var_eps, rstd = first.all_var_eps, first.all_rstd
        mod_now = sb("mod_now", [P, 2, 2, EC])
        h_hi = sb("h_hi", [P, EC, L], F32R)
        h_lo = sb("h_lo", [P, EC, L], F32R)
        k_parts = sb("k_parts", [P, 2, EC, 2, PAIRS * WIN], F32R)
        k_diag = [sb("k_diag0", [P, 2, 2, 4, PAIRS * WIN], F32R),
                  late[:].rearrange("p (s g h k) -> p s g h k", s=2, g=2, h=4)]
        q_hi = sb("q_hi", [P, HALF], F32R)
        q_diag = sb("q_diag", [P, 4, 2, PAIRS, 2, WIN], F32R)
        v_diag = sb("v_diag", [P, 2, 2 * PAIRS, H // 2, 2 * D])
        prob = sb("prob", [P, 4, 512])
        row_max = sb("row_max", [P, 2, 8])
        row_sum = sb("row_sum", [P, 2, 8])
        row_inv = sb("row_inv", [P, 2, 8])
        prob_t = sb("prob_t", [P, 2, 512])
        ctx_full = sb("ctx_full", [P, HALF])
        ctx_hi = sb("ctx_hi", [P, EC, HALF], F32R)
        ctx_lo = sb("ctx_lo", [P, EC, HALF], F32R)
        attn_tmp = sb("attn_tmp", [P, 512])
        gate_now = sb("gate_now", [P, E])
        gated_bias = sb("gated_bias", [P, E])
        w1_sum = sb("w1_sum", [P, FC])
        g_stats = sb("g_stats", [NB, 6])
        g_mean_var = sb("g_mean_var", [NB, 2])
        g_var_eps = sb("g_var_eps", [NB, 1])
        g_rstd = sb("g_rstd", [NB, 1])
        h_tok = sb("h_tok", [P, EC, NB])
        q_tok = sb("q_tok", [P, EC, NB])
        keys = sb("keys", [P, NB, 2, EC, H], F32R)
        key_bias = sb("key_bias", [H, NB])
        key_now = sb("key_now", [P, 2, 2, EC, H], F32R)
        key_bias_now = sb("key_bias_now", [H, 2])
        g_score = sb("g_score", [H, L])
        g_max = sb("g_max", [H, 1])
        g_shift = sb("g_shift", [H, 1])
        g_sum = sb("g_sum", [H, 1])
        g_inv = sb("g_inv", [H, 1])
        g_prob_t = sb("g_prob_t", [P, 8, H])
        g_mix = sb("g_mix", [P, EC, NB, H])
        g_ctx = sb("g_ctx", [P, EC, NB])
        g_parts = sb("g_parts", [P, 2, EC, NB], F32R)
        ones_r = sb("ones_r", [1, P], F32R)
        bias_parts = sb("bias_parts", [1, 2, E], F32R)

        ones_row = attn_tmp[0:1, 0:P]
        gate_rows = attn_tmp[0:NB, :]
        gate_sign = ctx_full[0:NB, :]
        w2t_raw = x_n[:].rearrange("p t e -> p (t e)").rearrange("p (c n) -> p c n", c=FC)
        v_flat = v_diag[:].rearrange("p a w j d -> p (a w j d)")
        w1_raw = v_flat[:, 0:FC * E].rearrange("p (c n) -> p c n", c=FC)
        w1t_raw = v_flat[:, FC * E:2 * FC * E].rearrange("p (c n) -> p c n", c=EC)
        mean_ones = w_kt[:, 0, 0:P]
        x_n_first = h_full[:].rearrange("p h (t e) -> p (h t) e", e=E)
        wmod_sb = v_diag[:, :, :, :, :].rearrange("p a w j d -> p (a w j d)")[:, 0:EC * 6 * E].rearrange(
            "p (c n) -> p c n", c=EC)
        w_k = x_res[:, 0:2, :]
        w_o = x_res[:, 2:4, :]
        g_x = x_res[0:NB, 4, :]
        g_x_n = x_res[0:NB, 5, :]
        q_heads = g_mix
        c_e = h_tok
        c_s = q_tok
        g_rows = g_score[:, 0:E]
        g_x_again = w_q[0:NB, 0, :]
        g_gate = w_q[0:NB, 1, :]
        g_mod = w_kt[:, :, 0:P]
        g_all = w_kt[:, :, P:2 * P]

        stage = psum[0:2]
        score = psum[2:4]
        turned = psum[4:6]
        mixed = psum[6]
        small = psum[7]

        x_ln_loaded = sem("x_ln_loaded")
        x_res_loaded = sem("x_res_loaded")
        gate_loaded = sem("gate_loaded")
        w_loaded = sem("w_loaded")
        w1t_loaded = sem("w1t_loaded")
        signs_ready = sem("signs_ready")
        abs_ready = sem("abs_ready")
        alpha2_full = sem("alpha2_full")
        alpha2_ready = sem("alpha2_ready")
        setup_loaded = sem("setup_loaded")
        gates_stored = sem("gates_stored")
        gates_ready = sem("gates_ready")
        silu_exp = sem("silu_exp")
        silu_ready = sem("silu_ready")
        mod_full = sem("mod_full")
        gates_full = sem("gates_full")
        weights_ready = sem("weights_ready")
        zeroed = sem("zeroed")
        v_zeroed = sem("v_zeroed")
        dve_step = sem("dve_step")
        stats_ready = sem("stats_ready")
        rstd_ready = sem("rstd_ready")
        xn_ready = sem("xn_ready")
        mod_now_ready = sem("mod_now_ready")
        stage_full = sem("stage_full")
        stage_free = sem("stage_free")
        h_lo_ready = sem("h_lo_ready")
        k_lo_ready = sem("k_lo_ready")
        k_diag_loaded = [sem(f"k_diag_loaded{c}") for c in range(EC)]
        q_lo_ready = sem("q_lo_ready")
        score_full = sem("score_full")
        shifted = sem("shifted")
        exp_done = sem("exp_done")
        inv_ready = sem("inv_ready")
        prob_ready = sem("prob_ready")
        turned_full = sem("turned_full")
        turned_copied = sem("turned_copied")
        mix_done = sem("mix_done")
        ctx_hi_ready = sem("ctx_hi_ready")
        ctx_lo_ready = sem("ctx_lo_ready")
        small_full = sem("small_full")
        small_free = sem("small_free")
        g_shift_ready = sem("g_shift_ready")
        g_exp_done = sem("g_exp_done")
        res_added = sem("res_added")
        mod_loaded = sem("mod_loaded")
        key_now_ready = sem("key_now_ready")
        g_x_loaded = sem("g_x_loaded")
        g_var_ready = sem("g_var_ready")
        g_rstd_ready = sem("g_rstd_ready")
        g_taken = sem("g_taken")
        g_product = sem("g_product")
        g_again_loaded = sem("g_again_loaded")
        g_stored = sem("g_stored")
        constants_ready = sem("constants_ready")

        N_ROLLED = 6
        G_NORM, G_H, G_QUERY, G_KEYS, G_MOD, G_CTX, G_OUT = range(1, 8)
        G_TURNED, G_QUERIED, G_DIRECTED, G_VALUED, G_PROJECTED = range(1, 6)

        def transfers(batch, tile):
            view = batch.rearrange("(p r) e -> r p e", r=256)
            yield view[1:65, :, :], tile[0:64, 0:4, :]
            yield view[65:129, :, :], tile[0:64, 4:8, :]
            yield view[129:193, :, :], tile[64:128, 0:4, :]
            yield view[193:256, :, :], tile[64:127, 4:8, :]
            yield view[0:1, 1:4, :], tile[127:128, 4:7, :]
            yield view[0:1, 0:1, :], tile[127:128, 7:8, :]

        def lagging(b, i, lag):
            j = i - lag
            n, j = (b - 1, j + ITEMS) if j < 0 else (b + 1, j - ITEMS) if j >= ITEMS else (b, j)
            return (n, j) if known_from(n, 0) and known_below(n, NB) else None

        block = ctx.enter_context(nc.Block())

        @block.sync
        def _(sp):
            def load_x(dst, loaded, b):
                for dram, tile in transfers(x[b], dst):
                    sp.dma_start(tile, dram).then_inc(loaded, 16)

            def load_gate(b):
                row = gates[b:b + 1, 0:E] if isinstance(b, int) else gates[bass.ds(b, 1), 0:E]
                sp.dma_start(gate_now[:], row.broadcast_to([P, E])).then_inc(gate_loaded, 16)

            def spread_keys(b, c):
                if positive(ITEMS * b - ITEMS + 4 + 4 * c):
                    sp.wait_ge(score_full, ITEMS * b - ITEMS + 4 + 4 * c)
                sp.wait_ge(k_lo_ready, (b + 1) * 2 + c - 1)
                for head in range(8):
                    for par in range(2):
                        to = 64 * par + D * (head % 4)
                        sp.dma_start(k_diag[c][to:to + D, :, head // 4, head % 4, :].bitcast(F32),
                                     k_parts[D * head:D * head + D, :, c, par, :].bitcast(F32)
                                     ).then_inc(k_diag_loaded[c], 16)

            def load_ffn_weights():
                sp.wait_ge(mix_done, ITEMS * (NB - 1))
                sp.wait_ge(small_full, small_count("mix", NB - 1))
                for dst, src in (
                    (w2t_raw, w2t.rearrange("(c p) n -> p c n", p=P)),
                    (w1_raw, w1.rearrange("(c p) n -> p c n", p=P)),
                    (ffn.bias1, b1),
                    (ffn.bias2, b2.rearrange("(a n) -> a n", a=1).broadcast_to([P, E])),
                ):
                    sp.dma_start(dst, src).then_inc(w_loaded, 16)

            def load_w1t():
                sp.wait_ge(mix_done, ITEMS * NB)
                sp.dma_start(w1t_raw, w1t.rearrange("(c p) n -> p c n", p=P)).then_inc(w1t_loaded, 16)

            def finish_tokens():
                sp.wait_ge(g_taken, G_OUT)
                sp.dma_start(x1[:, 0, :], g_x_again).then_inc(g_stored, 16)
                sp.wait_ge(g_stored, 16)
                sp.wait_ge(x1_stored, 16 * X1_STORES)
                sp.wait_ge(xn_ready, 2 * NB)
                for v in range(2):
                    sp.dma_start(x_pair[:, TT * v:TT * (v + 1), :], ffn_units(x1)[v]).then_inc(x_in_loaded[v], 16)

            sp.dma_start(c_t[:], ct.rearrange("(c p) b -> p c b", p=P)).then_inc(mod_loaded, 16)
            sp.dma_start(wmod_sb, wmod.rearrange("(c p) n -> p c n", p=P)).then_inc(mod_loaded, 16)
            load_x(x_ln, x_ln_loaded, 0)
            sp.dma_start(g_x, x[:, 0, :]).then_inc(g_x_loaded, 16)
            for dst, src in (
                (ident[:], ident_in),
                (w_k, wk.rearrange("(c p) n -> p c n", p=P)),
                (w_q[:], wq.rearrange("(c p) n -> p c n", p=P)),
                (w_v[:], wv.rearrange("(c p) n -> p c n", p=P)),
                (w_o, wo.rearrange("(c p) n -> p c n", p=P)),
                (w_kt[:], wkt.rearrange("(c p) n -> p c n", p=P)),
                (hmask[:], hmask_in),
                (bias_q[:], bq),
                (bias_k[:], bk),
                (bias_v[:], bv),
                (bias_o[:], bo.rearrange("(a n) -> a n", a=1).broadcast_to([P, E])),
            ):
                sp.dma_start(dst, src).then_inc(setup_loaded, 16)
            sp.wait_ge(xn_ready, 2)
            load_x(x_ln, x_ln_loaded, 1)
            sp.wait_ge(zeroed, 1)
            spread_keys(0, 0)
            sp.wait_ge(zeroed, 2)
            spread_keys(0, 1)
            sp.wait_ge(gates_ready, 1)
            sp.dma_start(gates, gate_rows).then_inc(gates_stored, 16)
            sp.wait_ge(weights_ready, 1)
            sp.wait_ge(g_taken, G_KEYS)
            load_x(x_res, x_res_loaded, 0)
            sp.wait_ge(gates_stored, 16)
            load_gate(0)
            sp.dma_start(g_x_again, x[:, 0, :]).then_inc(g_again_loaded, 16)
            sp.dma_start(g_gate, gates[:, 0:E]).then_inc(g_again_loaded, 16)

            def iteration(b, par):
                if known_from(b, 1) and known_below(b, NB):
                    spread_keys(b, 1)
                if known_below(b, NB - 2):
                    sp.wait_ge(xn_ready, 2 * b + 4)
                    load_x(x_ln, x_ln_loaded, b + 2)
                if known_below(b, NB - 1):
                    spread_keys(b + 1, 0)
                if isinstance(b, int) and b == NB - 1:
                    load_ffn_weights()
                if isinstance(b, int) and b == NB:
                    load_w1t()
                if known_from(b, 1):
                    sp.wait_ge(res_added, 4 * b)
                    for n, (dram, tile) in enumerate(transfers(x1[b - 1], x_res)):
                        if n < X1_STORES:
                            sp.dma_start(dram, tile).then_inc(x1_stored, 16)
                    if known_below(b, NB):
                        sp.wait_ge(x1_stored, 16 * X1_STORES * b)
                        load_x(x_res, x_res_loaded, b)
                        load_gate(b)
                if isinstance(b, int) and b == NB - 1:
                    finish_tokens()

            batches(sp, iteration)

        @block.tensor
        def _(pe):
            def exact(dst, stationary, moving, fresh=True):
                n = len(stationary)
                for k in range(n):
                    (s_hi, s_lo), (m_hi, m_lo) = stationary[k], moving[k]
                    nc.tensor.matmul(dst, s_hi, m_hi, start=fresh and k == 0, stop=False)
                    nc.tensor.matmul(dst, s_hi, m_lo, start=False, stop=False)
                    done = nc.tensor.matmul(dst, s_lo, m_hi, start=False, stop=k == n - 1)
                return done

            def stage_bank(b, k):
                if positive(stage_count(b, k) - 2):
                    pe.wait_ge(stage_free, stage_count(b, k) - 2)
                if k in (7, 8):
                    pe.wait_ge(k_lo_ready, 2 * b + k - 6)
                if k == 9:
                    pe.wait_ge(q_lo_ready, 2 * b + 1)
                if k == 2 and known_from(b, 1):
                    pe.wait_ge(q_lo_ready, 2 * b)
                return stage[k % 2]

            def small_bank(name, b):
                if positive(small_count(name, b) - 1):
                    pe.wait_ge(small_free, small_count(name, b) - 1)
                return small

            def turn_x(b, half, c, k):
                if c == 0:
                    pe.wait_ge(xn_ready, 2 * b + half + 1)
                bank = stage_bank(b, k)
                for p in range(4):
                    done = nc.tensor.transpose(bank[:, p * P:(p + 1) * P],
                                               x_n[:, 4 * half + p, c * P:(c + 1) * P], ident[:])
                done.then_inc(stage_full, 1)

            def project(b, which, c, k):
                pe.wait_ge(stage_free, stage_count(b, 2))
                pe.wait_ge(h_lo_ready, 4 * b + 2)
                bank = stage_bank(b, k)
                cols = slice(c * P, (c + 1) * P)
                exact(bank[:], [(w_hi[:, which, e, cols], w_lo[:, which, e, cols]) for e in range(EC)],
                      [(h_hi[:, e, 0:HALF], h_lo[:, e, 0:HALF]) for e in range(EC)]).then_inc(stage_full, 1)

            def project_v(b, two, k):
                bank = stage_bank(b, k)
                for p in (2 * two, 2 * two + 1):
                    tok = slice(p * P, (p + 1) * P)
                    done = exact(bank[:, (p % 2) * E:(p % 2 + 1) * E],
                                 [(h_hi[:, e, tok], h_lo[:, e, tok]) for e in range(EC)],
                                 [(w_hi[:, WV, e, :], w_lo[:, WV, e, :]) for e in range(EC)])
                done.then_inc(stage_full, 1)

            def global_tokens():
                pe.wait_ge(g_taken, G_NORM)
                for c in range(EC):
                    done = nc.tensor.transpose(small[:, c * NB:(c + 1) * NB], g_x_n[:, c * P:(c + 1) * P],
                                               ident[0:NB, 0:NB])
                done.then_inc(g_product, 1)

            def global_queries():
                pe.wait_ge(g_taken, G_H)
                for c in range(EC):
                    for e in range(EC):
                        done = nc.tensor.matmul(small[:, (2 + c) * NB:(3 + c) * NB], w_q[:, e, c * P:(c + 1) * P],
                                                h_tok[:, e, :], start=e == 0, stop=e == EC - 1)
                done.then_inc(g_product, 1)

            def global_directions():
                pe.wait_ge(g_taken, G_QUERY)
                for e in range(EC):
                    for c in range(EC):
                        nc.tensor.matmul(mixed[:, e * P:(e + 1) * P], w_kt[:, c, e * P:(e + 1) * P],
                                         q_heads[:, c, :, :], start=c == 0, stop=c == EC - 1)
                for n in range(NB):
                    for c in range(EC):
                        done = nc.tensor.matmul(small[0:H, 4 * NB + n:4 * NB + n + 1], q_heads[:, c, n, :],
                                                bias_k[:, c:c + 1], start=c == 0, stop=c == EC - 1)
                done.then_inc(g_product, 1)

            def global_values():
                pe.wait_ge(stage_free, stage_count(NB - 1, 12))
                pe.wait_ge(g_taken, G_MOD)
                for c in range(EC):
                    for e in range(EC):
                        done = nc.tensor.matmul(stage[0][:, c * P:(c + 1) * P], w_v[:, e, c * P:(c + 1) * P],
                                                g_mod[:, e, :], start=e == 0, stop=e == EC - 1)
                done.then_inc(g_product, 1)

            def global_out():
                pe.wait_ge(g_taken, G_CTX)
                exact(stage[1][0:NB, 0:E], [(g_parts[:, 0, c, :], g_parts[:, 1, c, :]) for c in range(EC)],
                      [(w_hi[:, WO, c, :], w_lo[:, WO, c, :]) for c in range(EC)]).then_inc(g_product, 1)

            def global_scores(b, par, half, k):
                if half == 0:
                    pe.wait_ge(key_now_ready, b + 1)
                    pe.wait_ge(stage_free, stage_count(b, 4))
                    pe.wait_ge(h_lo_ready, 4 * b + 4)
                bank = stage_bank(b, k)
                tok = slice(half * HALF, (half + 1) * HALF)
                exact(bank[0:H, :], [(key_now[:, par, 0, e, :], key_now[:, par, 1, e, :]) for e in range(EC)],
                      [(h_hi[:, e, tok], h_lo[:, e, tok]) for e in range(EC)]).then_inc(stage_full, 1)

            def global_turn(b):
                pe.wait_ge(g_exp_done, b + 1)
                bank = small_bank("turn", b)
                nc.tensor.matmul(bank[:, 0:H], g_score[:, 0:P], ident[0:H, 0:H], start=True, stop=True)
                for t in range(1, 8):
                    done = nc.tensor.transpose(bank[:, t * H:(t + 1) * H], g_score[:, t * P:(t + 1) * P],
                                               ident[0:H, 0:H])
                done.then_inc(small_full, 1)

            def global_mix(b):
                bank = small_bank("mix", b)
                for t in range(8):
                    done = nc.tensor.matmul(bank[0:H, 0:E], g_prob_t[:, t, :], x_n[:, t, :],
                                            start=t == 0, stop=t == 7)
                done.then_inc(small_full, 1)

            def global_flip(b):
                bank = small_bank("flip", b)
                for e in range(EC):
                    done = nc.tensor.matmul(bank[:, e * H:(e + 1) * H], g_rows[:, e * P:(e + 1) * P],
                                            ident[0:H, 0:H], start=True, stop=True)
                done.then_inc(small_full, 1)

            def mean_w2():
                pe.wait_ge(abs_ready, 1)
                for f in range(FC):
                    done = nc.tensor.matmul(score[0][:, 0:E], mean_ones, w2t_raw[:, f, :], start=f == 0,
                                            stop=f == FC - 1)
                done.then_inc(alpha2_full, 1)

            def window_out(b, two):
                pe.wait_ge(ctx_hi_ready, 2 * b + 2)
                pe.wait_ge(ctx_lo_ready, 2 * b + 2)
                bank = small_bank(f"wo{two}", b)
                for p in (2 * two, 2 * two + 1):
                    tok = slice(p * P, (p + 1) * P)
                    part = bank[:, (p % 2) * E:(p % 2 + 1) * E]
                    nc.tensor.matmul(part, ones_r[:], bias_parts[:, 0, :], start=True, stop=False)
                    nc.tensor.matmul(part, ones_r[:], bias_parts[:, 1, :], start=False, stop=False)
                    done = exact(part, [(ctx_hi[:, c, tok], ctx_lo[:, c, tok]) for c in range(EC)],
                                 [(w_hi[:, WO, c, :], w_lo[:, WO, c, :]) for c in range(EC)], fresh=False)
                done.then_inc(small_full, 1)

            def scores(b, i):
                c, p = divmod(i, 4)
                if p == 0:
                    pe.wait_ge(k_diag_loaded[c], 256 * b + 256)
                    pe.wait_ge(stage_free, stage_count(b, 7 + 5 * c))
                    pe.wait_ge(q_lo_ready, 2 * b + c + 1)
                if positive(ITEMS * b + i - 1):
                    pe.wait_ge(shifted, ITEMS * b + i - 1)
                bank = score[i % 2]
                for g in range(2):
                    keys_now = [k_diag[c][:, part, g, :, p * WIN:(p + 1) * WIN] for part in range(2)]
                    queries = [q_diag[:, 2 * c + g, part, p, :, :] for part in range(2)]
                    done = exact(bank[:, g * E:(g + 1) * E], [queries], [keys_now])
                done.then_inc(score_full, 1)

            def turn_probs(b, i):
                pe.wait_ge(prob_ready, ITEMS * b + i + 1)
                if positive(ITEMS * b + i - 1):
                    pe.wait_ge(turned_copied, ITEMS * b + i - 1)
                for j in range(4):
                    done = nc.tensor.transpose(turned[i % 2][:, j * P:(j + 1) * P],
                                               prob[:, i % 4, j * P:(j + 1) * P], ident[:])
                done.then_inc(turned_full, 1)

            def mix(b, i, par_b):
                c, p = divmod(i, 4)
                pe.wait_ge(turned_copied, ITEMS * b + i + 1)
                if i == 0:
                    pe.wait_ge(stage_free, stage_count(b, 11))
                if p == 0:
                    if positive(2 * b + c):
                        pe.wait_ge(ctx_hi_ready, 2 * b + c)
                for j in range(4):
                    for par in range(2):
                        done = nc.tensor.matmul(
                            mixed[32 * j:32 * j + 32, p * P + par * WIN:p * P + (par + 1) * WIN],
                            v_diag[:, par_b, 2 * p + par, 4 * c + j, :],
                            prob_t[:, i % 2, j * P + par * WIN:j * P + (par + 1) * WIN],
                            start=True, stop=True)
                done.then_inc(mix_done, 1)

            def stage_one(b, par, i):
                if i == 2:
                    turn_x(b, 0, 0, 1)
                    turn_x(b, 0, 1, 2)
                if i == 3:
                    turn_x(b, 1, 0, 3)
                    turn_x(b, 1, 1, 4)
                if i == 4:
                    project(b, WK, 0, 5)
                if i == 5:
                    project(b, WK, 1, 6)
                    project(b, WQ, 0, 7)
                if i == 6:
                    project_v(b, 0, 8)
                    global_scores(b, par, 0, 9)
                if i == 7:
                    global_scores(b, par, 1, 10)
                    project_v(b, 1, 11)

            def rest(b, i):
                cur, prev = known_below(b, NB), known_from(b, 1)
                if i == 0 and cur:
                    project(b, WQ, 1, 12)
                    global_turn(b)
                if i == 1 and cur:
                    global_mix(b)
                if i == 2 and cur:
                    global_flip(b)
                if i == 4 and prev:
                    window_out(b - 1, 0)
                if i == 5 and prev:
                    window_out(b - 1, 1)

            def iteration(b, par):
                for i in range(ITEMS):
                    if (at := lagging(b, i, -1)) is not None:
                        scores(*at)
                    if (at := lagging(b, i, 2)) is not None:
                        turn_probs(*at)
                    if (at := lagging(b, i, 3)) is not None:
                        mix(*at, par if i >= 3 else 1 - par)
                    rest(b, i)
                    if known_below(b, NB - 1):
                        stage_one(b + 1, 1 - par, i)
                    if isinstance(b, int) and b == NB and i == 3:
                        mean_w2()
                    if isinstance(b, int) and b == NB - 1 and i == 5:
                        global_values()
                    if isinstance(b, int) and b == NB - 1 and i == 6:
                        global_out()

            def gate_products():
                for j, blk in enumerate((2, 5)):
                    for e in range(EC):
                        done = nc.tensor.matmul(turned[1][0:NB, j * E:(j + 1) * E], c_s[:, e, :],
                                                wmod_sb[:, e, blk * E:(blk + 1) * E], start=e == 0, stop=e == EC - 1)
                done.then_inc(gates_full, 1)

            pe.wait_ge(mod_loaded, 32)
            pe.wait_ge(silu_ready, 1)
            for j, blk in enumerate(MOD_BLOCKS):
                for c in range(EC):
                    col = (j * EC + c) * NB
                    for e in range(EC):
                        done = nc.tensor.matmul(turned[0][:, col:col + NB],
                                                wmod_sb[:, e, blk * E + c * P:blk * E + (c + 1) * P], c_s[:, e, :],
                                                start=e == 0, stop=e == EC - 1)
            done.then_inc(mod_full, 1)
            pe.wait_ge(setup_loaded, 16 * 11)
            for i in range(ITEMS):
                if i == 3:
                    global_tokens()
                if i == 4:
                    gate_products()
                    pe.wait_ge(weights_ready, 1)
                if i == 5:
                    global_queries()
                if i == 6:
                    global_directions()
                stage_one(0, 0, i)
            scores(0, 0)
            batches(pe, iteration)

        @block.scalar
        def _(act):
            def filled(b, k):
                act.wait_ge(stage_full, stage_count(b, k))
                return stage[k % 2]

            def modulate(b, par, half, c, k):
                bank = filled(b, k)
                act.wait_ge(mod_now_ready, b + 1)
                if positive(4 * b + 2 * half + c - 1):
                    act.wait_ge(h_lo_ready, 4 * b + 2 * half + c - 1)
                cols = slice(half * HALF, (half + 1) * HALF)
                shift, scale = mod_now[:, par, 0, c:c + 1], mod_now[:, par, 1, c:c + 1]
                nc.scalar.activation(h_full[:, c, :], bank[:], ACT.Identity, scale=scale, bias=shift)
                nc.scalar.activation(h_hi[:, c, cols], bank[:], ACT.Identity, scale=scale,
                                     bias=shift).then_inc(stage_free, 1)

            def take_keys(b, c, k):
                bank = filled(b, k)
                if positive(256 * b):
                    act.wait_ge(k_diag_loaded[c], 256 * b)
                nc.scalar.activation(k_parts[:, 0, c, :, :].rearrange("r a (p k) -> r a p k", k=WIN),
                                     bank[:].rearrange("r (p a k) -> r a p k", a=2, k=WIN), ACT.Identity,
                                     bias=bias_k[:, c:c + 1]).then_inc(stage_free, 1)

            def take_queries(b, c, k):
                bank = filled(b, k)
                if positive(2 * b + c):
                    act.wait_ge(q_lo_ready, 2 * b + c)
                nc.scalar.activation(q_hi[:], bank[:], ACT.Identity, bias=bias_q[:, c:c + 1])
                if positive(ITEMS * b - ITEMS + 4 * c + 4):
                    act.wait_ge(score_full, ITEMS * b - ITEMS + 4 * c + 4)
                for g in range(2):
                    rows = slice(64 * g, 64 * g + 64)
                    for par in range(2):
                        done = nc.scalar.activation(
                            q_diag[64 * par:64 * par + 64, 2 * c + g, 0, :, par, :],
                            bank[rows, :].rearrange("r (p a q) -> r p a q", a=2, q=WIN)[:, :, par, :],
                            ACT.Identity, bias=bias_q[rows, c:c + 1])
                done.then_inc(stage_free, 1)

            def take_values(b, par_b, two, k):
                bank = filled(b, k)
                if isinstance(b, int) and b == 0:
                    act.wait_ge(v_zeroed, 1)
                if positive(ITEMS * b - ITEMS):
                    act.wait_ge(mix_done, ITEMS * b - ITEMS)
                for par in range(2):
                    src = bank[64 * par:64 * par + 64, :].rearrange("k (p j h d) -> k p j h d", p=2, j=H // 2, h=2)
                    for h2 in range(2):
                        dst = v_diag[64 * h2:64 * h2 + 64, par_b, 4 * two + par:4 * two + par + 3:2, :,
                                     D * h2:D * h2 + D]
                        done = nc.scalar.copy(dst, src[:, :, :, h2, :])
                done.then_inc(stage_free, 1)

            def take_global_scores(b, par, half, k):
                bank = filled(b, k)
                if known_from(b, 1):
                    act.wait_ge(small_full, small_count("flip", b - 1))
                nc.scalar.activation(g_score[:, half * HALF:(half + 1) * HALF], bank[0:H, :], ACT.Identity,
                                     bias=key_bias_now[:, par:par + 1]).then_inc(stage_free, 1)

            def global_exp(b):
                act.wait_ge(g_shift_ready, b + 1)
                nc.scalar.activation(g_score[:], g_score[:], ACT.Exp, scale=SCALE, bias=g_shift[:, 0:1],
                                     accum_out=g_sum[:, 0:1]).then_inc(g_exp_done, 1)

            def exponentials(b, i):
                act.wait_ge(shifted, ITEMS * b + i + 1)
                nc.scalar.activation(prob[:, i % 4, :], prob[:, i % 4, :], ACT.Exp, scale=SCALE).then_inc(exp_done, 1)

            def copy_turned(b, i):
                act.wait_ge(turned_full, ITEMS * b + i + 1)
                if positive(ITEMS * b + i - 1):
                    act.wait_ge(mix_done, ITEMS * b + i - 1)
                nc.scalar.copy(prob_t[:, i % 2, :], turned[i % 2][:]).then_inc(turned_copied, 1)

            def signs():
                act.wait_ge(w_loaded, 16 * 4)
                act.wait_ge(score_full, ITEMS * NB)
                nc.scalar.activation(ffn.w2_sign, w2t_raw, ACT.Sign).then_inc(signs_ready, 1)

            def take_context(b, c):
                act.wait_ge(mix_done, ITEMS * b + 4 * c + 4)
                if positive(2 * b + c):
                    act.wait_ge(ctx_lo_ready, 2 * b + c)
                if known_from(b, 1):
                    act.wait_ge(small_full, small_count("wo1", b - 1))
                nc.scalar.activation(ctx_full[:], mixed[:], ACT.Identity, bias=bias_v[:, c:c + 1])
                nc.scalar.activation(ctx_hi[:, c, :], mixed[:], ACT.Identity,
                                     bias=bias_v[:, c:c + 1]).then_inc(ctx_hi_ready, 1)

            def stage_one(b, par, i):
                if i == 2:
                    modulate(b, par, 0, 0, 1)
                    modulate(b, par, 0, 1, 2)
                if i == 3:
                    modulate(b, par, 1, 0, 3)
                    modulate(b, par, 1, 1, 4)
                if i == 4:
                    take_keys(b, 0, 5)
                if i == 5:
                    take_keys(b, 1, 6)
                    take_queries(b, 0, 7)
                if i == 6:
                    take_values(b, par, 0, 8)
                    take_global_scores(b, par, 0, 9)
                if i == 7:
                    take_global_scores(b, par, 1, 10)
                    take_values(b, par, 1, 11)

            def iteration(b, par):
                cur = known_below(b, NB)
                for i in range(ITEMS):
                    if cur:
                        if i == 0:
                            global_exp(b)
                        exponentials(b, i)
                    if (at := lagging(b, i, 2)) is not None:
                        copy_turned(*at)
                    if i == 0 and cur:
                        take_queries(b, 1, 12)
                    if i == 2 and known_from(b, 1):
                        take_context(b - 1, 1)
                    if i == 6 and cur:
                        take_context(b, 0)
                    if isinstance(b, int) and b == NB and i == 0:
                        signs()
                    if isinstance(b, int) and b == NB and i == 3:
                        act.wait_ge(w1t_loaded, 16)
                        nc.scalar.activation(ffn.w1_sign, w1t_raw, ACT.Sign)
                    if known_below(b, NB - 1):
                        stage_one(b + 1, 1 - par, i)

            act.wait_ge(mod_loaded, 32)
            nc.scalar.activation(c_e[:], c_t[:], ACT.Exp, scale=-1.0).then_inc(silu_exp, 1)
            act.wait_ge(setup_loaded, 16 * 11)
            for i in range(ITEMS):
                stage_one(0, 0, i)
            batches(act, iteration)

        @block.vector
        def _(dve):
            steps = {"at": 0}

            def step():
                steps["at"] = steps["at"] + 1
                return steps["at"]

            def shift_scores(b, i):
                rows = score[i % 2][:].rearrange("q (h k) -> q h k", k=WIN)
                dve.wait_ge(score_full, ITEMS * b + i + 1)
                nc.vector.reduce_max(row_max[:, i % 2, :], rows, AX).then_inc(dve_step, 1)
                dve.wait_ge(dve_step, step())
                if positive(ITEMS * b + i - 3):
                    dve.wait_ge(turned_full, ITEMS * b + i - 3)
                nc.vector.tensor_tensor(prob[:, i % 4, :].rearrange("q (h k) -> q h k", k=WIN), rows,
                                        row_max[:, i % 2, :].unsqueeze(2).broadcast_to([P, 8, WIN]),
                                        ALU.subtract).then_inc(shifted, 1)

            def invert_sums(b, i):
                dve.wait_ge(exp_done, ITEMS * b + i + 1)
                nc.vector.reduce_sum(row_sum[:, i % 2, :], prob[:, i % 4, :].rearrange("q (h k) -> q h k", k=WIN),
                                     AX).then_inc(dve_step, 1)
                dve.wait_ge(dve_step, step())
                if positive(ITEMS * b + i - 1):
                    dve.wait_ge(prob_ready, ITEMS * b + i - 1)
                nc.vector.reciprocal(row_inv[:, i % 2, :], row_sum[:, i % 2, :]).then_inc(inv_ready, 1)

            def statistics(b, half):
                dve.wait_ge(x_ln_loaded, 16 * N_ROLLED * (b + 1))
                for t in range(4 * half, 4 * half + 4):
                    done = nc.vector.bn_stats(stats[:, t, :], x_ln[:, t, :])
                done.then_inc(dve_step, 1)
                dve.wait_ge(dve_step, step())
                if positive(2 * b + half):
                    dve.wait_ge(rstd_ready, 2 * b + half)
                nc.vector.memset(var_eps[:, 4 * half:4 * half + 4], EPS)
                for t in range(4 * half, 4 * half + 4):
                    done = nc.vector.bn_aggr(mean_var[:, t, :], stats[:, t, :])
                done.then_inc(dve_step, 1)
                dve.wait_ge(dve_step, step())
                part = var_eps[:, 4 * half:4 * half + 4]
                nc.vector.tensor_tensor(part, part, mean_var[:, 4 * half:4 * half + 4, 1],
                                        ALU.add).then_inc(stats_ready, 1)

            def normalise(b, half):
                dve.wait_ge(rstd_ready, 2 * b + half + 1)
                if known_from(b, 1):
                    dve.wait_ge(small_full, small_count("mix", b - 1))
                for t in range(4 * half, 4 * half + 4):
                    done = nc.vector.tensor_scalar(x_n[:, t, :], x_ln[:, t, :], mean_var[:, t, 0:1],
                                                   rstd[:, t:t + 1], ALU.subtract, ALU.mult)
                done.then_inc(xn_ready, 1)

            def pick_modulation(b, par):
                src = modt[:, SA:CA + 1, :, b:b + 1] if isinstance(b, int) else modt[:, SA:CA + 1, :, bass.ds(b, 1)]
                nc.vector.tensor_copy(mod_now[:, par, :, :],
                                      src.rearrange("p j c b -> p j (c b)")).then_inc(mod_now_ready, 1)

            def pick_keys(b, par):
                at = slice(b, b + 1) if isinstance(b, int) else bass.ds(b, 1)
                nc.vector.tensor_copy(key_bias_now[:, par:par + 1], key_bias[:, at])
                nc.vector.tensor_copy(key_now[:, par, :, :, :].rearrange("p s c h -> p (s c h)"),
                                      keys[:, at, :, :, :].rearrange("p b s c h -> p (b s c h)").bitcast(F32)
                                      ).then_inc(key_now_ready, 1)

            def low_keys(b, c):
                dve.wait_ge(stage_free, stage_count(b, 5 + c))
                bank = stage[(5 + c) % 2][:].rearrange("r (p a k) -> r p a k", a=2, k=WIN)
                for par in range(2):
                    parts = k_parts[:, :, c, par, :].rearrange("r s (p k) -> r s p k", k=WIN)
                    done = nc.vector.scalar_tensor_tensor(parts[:, 1, :, :], bank[:, :, par, :], bias_k[:, c:c + 1],
                                                          parts[:, 0, :, :].bitcast(F32), ALU.add, ALU.subtract)
                done.then_inc(k_lo_ready, 1)

            def low_queries(b, c):
                dve.wait_ge(stage_free, stage_count(b, 7 + 5 * c))
                bank = stage[(7 + 5 * c) % 2][:].rearrange("r (p a q) -> r p a q", a=2, q=WIN)
                hi = q_hi[:].rearrange("r (p a q) -> r p a q", a=2, q=WIN)
                for g in range(2):
                    rows = slice(64 * g, 64 * g + 64)
                    for par in range(2):
                        done = nc.vector.scalar_tensor_tensor(
                            q_diag[64 * par:64 * par + 64, 2 * c + g, 1, :, par, :], bank[rows, :, par, :],
                            bias_q[rows, c:c + 1], hi[rows, :, par, :].bitcast(F32), ALU.add, ALU.subtract)
                done.then_inc(q_lo_ready, 1)

            def global_statistics():
                dve.wait_ge(g_x_loaded, 16)
                nc.vector.bn_stats(g_stats[:], g_x).then_inc(dve_step, 1)
                dve.wait_ge(dve_step, step())
                nc.vector.bn_aggr(g_mean_var[:], g_stats[:]).then_inc(dve_step, 1)
                dve.wait_ge(dve_step, step())
                nc.vector.tensor_scalar_add(g_var_eps[:], g_mean_var[:, 1:2], EPS).then_inc(g_var_ready, 1)

            def normalise_tokens():
                dve.wait_ge(g_rstd_ready, 1)
                nc.vector.tensor_scalar(g_x_n, g_x, g_mean_var[:, 0:1], g_rstd[:], ALU.subtract,
                                        ALU.mult).then_inc(g_taken, 1)

            def modulate_tokens():
                dve.wait_ge(g_product, G_TURNED)
                turned_x = small[:, 0:EC * NB].rearrange("p (c b) -> p c b", c=EC)
                nc.vector.tensor_tensor(h_tok[:], turned_x, modt[:, CA, :, :], ALU.mult).then_inc(dve_step, 1)
                dve.wait_ge(dve_step, step())
                nc.vector.tensor_tensor(h_tok[:], h_tok[:], modt[:, SA, :, :], ALU.add).then_inc(g_taken, 1)

            def take_queries():
                dve.wait_ge(g_product, G_QUERIED)
                queries = small[:, 2 * NB:4 * NB].rearrange("p (c b) -> p c b", c=EC)
                nc.vector.tensor_tensor(q_tok[:], queries, bias_q[:].unsqueeze(2).broadcast_to([P, EC, NB]),
                                        ALU.add).then_inc(dve_step, 1)
                dve.wait_ge(dve_step, step())
                for c in range(EC):
                    done = nc.vector.tensor_tensor(q_heads[:, c, :, :],
                                                   hmask[:, c, :].unsqueeze(1).broadcast_to([P, NB, H]),
                                                   q_tok[:, c, :].unsqueeze(2).broadcast_to([P, NB, H]), ALU.mult)
                done.then_inc(g_taken, 1)

            def take_directions():
                dve.wait_ge(g_product, G_DIRECTED)
                nc.vector.tensor_copy(key_bias[:], small[0:H, 4 * NB:5 * NB])
                for e in range(EC):
                    done = nc.vector.tensor_copy(keys[:, :, 0, e, :],
                                                 mixed[:, e * P:(e + 1) * P].rearrange("p (b h) -> p b h", h=H))
                done.then_inc(dve_step, 1)
                dve.wait_ge(dve_step, step())
                for e in range(EC):
                    done = nc.vector.tensor_tensor(keys[:, :, 1, e, :],
                                                   mixed[:, e * P:(e + 1) * P].rearrange("p (b h) -> p b h", h=H),
                                                   keys[:, :, 0, e, :].bitcast(F32), ALU.subtract)
                done.then_inc(g_taken, 1)
                dve.wait_ge(g_taken, G_KEYS)

            def global_shift(b):
                dve.wait_ge(stage_free, stage_count(b, 10))
                nc.vector.reduce_max(g_max[:], g_score[:], AX).then_inc(dve_step, 1)
                dve.wait_ge(dve_step, step())
                nc.vector.tensor_scalar_mul(g_shift[:], g_max[:], -SCALE).then_inc(g_shift_ready, 1)

            def global_inverse(b):
                dve.wait_ge(g_exp_done, b + 1)
                nc.vector.reciprocal(g_inv[:], g_sum[:]).then_inc(dve_step, 1)
                step()

            def take_turn(b):
                dve.wait_ge(small_full, small_count("turn", b))
                nc.vector.tensor_copy(g_prob_t[:].rearrange("p t h -> p (t h)"),
                                      small[:, 0:8 * H]).then_inc(small_free, 1)

            def take_mix(b):
                dve.wait_ge(small_full, small_count("mix", b))
                nc.vector.tensor_scalar_mul(g_rows, small[0:H, 0:E], g_inv[:, 0:1]).then_inc(small_free, 1)

            def take_flip(b):
                dve.wait_ge(small_full, small_count("flip", b))
                at = slice(b, b + 1) if isinstance(b, int) else bass.ds(b, 1)
                nc.vector.tensor_copy(g_mix[:, :, at, :].rearrange("p c b h -> p c (b h)"),
                                      small[:, 0:EC * H].rearrange("p (c h) -> p c h", c=EC)).then_inc(small_free, 1)

            def modulate_mix():
                mod = g_mod.rearrange("p c (b h) -> p c b h", h=H)
                dve.wait_ge(small_free, small_count("flip", NB - 1))
                for c in range(EC):
                    done = nc.vector.tensor_tensor(mod[:, c, :, :], g_mix[:, c, :, :],
                                                   modt[:, CA, c, :].unsqueeze(2).broadcast_to([P, NB, H]), ALU.mult)
                done.then_inc(dve_step, 1)
                dve.wait_ge(dve_step, step())
                for c in range(EC):
                    done = nc.vector.tensor_tensor(mod[:, c, :, :], mod[:, c, :, :],
                                                   modt[:, SA, c, :].unsqueeze(2).broadcast_to([P, NB, H]), ALU.add)
                done.then_inc(g_taken, 1)

            def take_global_values():
                dve.wait_ge(g_product, G_VALUED)
                for c in range(EC):
                    done = nc.vector.tensor_tensor(g_all[:, c, :].rearrange("p (b h) -> p b h", h=H),
                                                   stage[0][:, c * P:(c + 1) * P].rearrange("p (b h) -> p b h", h=H),
                                                   hmask[:, c, :].unsqueeze(1).broadcast_to([P, NB, H]), ALU.mult)
                done.then_inc(dve_step, 1)
                dve.wait_ge(dve_step, step())
                nc.vector.reduce_sum(g_ctx[:], g_all.rearrange("p c (b h) -> p c b h", h=H), AX).then_inc(dve_step, 1)
                dve.wait_ge(dve_step, step())
                nc.vector.tensor_tensor(g_ctx[:], g_ctx[:], bias_v[:].unsqueeze(2).broadcast_to([P, EC, NB]),
                                        ALU.add).then_inc(dve_step, 1)
                dve.wait_ge(dve_step, step())
                nc.vector.tensor_copy(g_parts[:, 0, :, :], g_ctx[:]).then_inc(dve_step, 1)
                dve.wait_ge(dve_step, step())
                nc.vector.tensor_tensor(g_parts[:, 1, :, :], g_ctx[:], g_parts[:, 0, :, :].bitcast(F32),
                                        ALU.subtract).then_inc(g_taken, 1)

            def finish_tokens():
                dve.wait_ge(g_product, G_PROJECTED)
                dve.wait_ge(g_again_loaded, 32)
                nc.vector.tensor_tensor(g_rows[0:NB, :], stage[1][0:NB, 0:E], bias_o[0:NB, :],
                                        ALU.add).then_inc(dve_step, 1)
                dve.wait_ge(dve_step, step())
                nc.vector.tensor_tensor(g_rows[0:NB, :], g_rows[0:NB, :], g_gate, ALU.mult).then_inc(dve_step, 1)
                dve.wait_ge(dve_step, step())
                nc.vector.tensor_tensor(g_x_again, g_x_again, g_rows[0:NB, :], ALU.add).then_inc(g_taken, 1)

            def magnitudes():
                dve.wait_ge(w_loaded, 16 * 4)
                nc.vector.memset(mean_ones, 1.0 / F)
                nc.vector.scalar_tensor_tensor(w1_raw, w1_raw, -1.0, w1_raw, ALU.mult, ALU.max).then_inc(dve_step, 1)
                dve.wait_ge(signs_ready, 1)
                nc.vector.scalar_tensor_tensor(w2t_raw, w2t_raw, -1.0, w2t_raw, ALU.mult,
                                               ALU.max).then_inc(abs_ready, 1)
                dve.wait_ge(dve_step, step())

            def first_unit_statistics():
                dve.wait_ge(x_in_loaded[0], 16)
                for t in range(TT):
                    done = nc.vector.bn_stats(first.stats[:, t, :], x_pair[:, t, :])
                done.then_inc(dve_step, 1)
                dve.wait_ge(dve_step, step())
                for t in range(TT):
                    done = nc.vector.bn_aggr(first.mean_var[:, t, :], first.stats[:, t, :])
                done.then_inc(dve_step, 1)
                dve.wait_ge(dve_step, step())
                nc.vector.tensor_scalar_add(first.var_eps, first.mean_var[:, :, 1], EPS).then_inc(first.stats_ready, 1)

            def normalise_first_unit():
                dve.wait_ge(first.rstd_ready, 1)
                for t in range(TT):
                    done = nc.vector.tensor_scalar(x_n_first[:, t, :], x_pair[:, t, :], first.mean_var[:, t, 0:1],
                                                   first.rstd[:, t:t + 1], ALU.subtract, ALU.mult)
                done.then_inc(first.xn_ready, 1)

            def mean_w1():
                nc.vector.reduce_sum(w1_sum[:], w1_raw, AX).then_inc(dve_step, 1)
                dve.wait_ge(dve_step, step())
                nc.vector.tensor_scalar_mul(ffn.alpha1, w1_sum[:], 1.0 / E)

            def gate_out(name, b, tiles):
                dve.wait_ge(small_full, small_count(name, b))
                dve.wait_ge(gate_loaded, 16 * b + 16)
                dve.wait_ge(res_added, 4 * b + (1 if name == "wo0" else 3))
                nc.vector.tensor_tensor(attn_tmp[:, 0:tiles * E].rearrange("p (t e) -> p t e", e=E),
                                        small[:, 0:tiles * E].rearrange("p (t e) -> p t e", e=E),
                                        gate_now[:].unsqueeze(1).broadcast_to([P, tiles, E]),
                                        ALU.mult).then_inc(small_free, 1)

            def slot_steps(b, par, i):
                cur, prev, nxt = known_below(b, NB), known_from(b, 1), known_below(b, NB - 1)
                if i == 0 and nxt:
                    pick_modulation(b + 1, 1 - par)
                    pick_keys(b + 1, 1 - par)
                if i == 0 and cur:
                    take_turn(b)
                if i == 1:
                    if cur:
                        low_queries(b, 1)
                    if nxt:
                        statistics(b + 1, 1)
                    if cur:
                        take_mix(b)
                if i == 2:
                    if nxt:
                        normalise(b + 1, 0)
                    if cur:
                        take_flip(b)
                if i == 3 and nxt:
                    normalise(b + 1, 1)
                if i == 4:
                    if nxt:
                        low_keys(b + 1, 0)
                    if prev:
                        gate_out("wo0", b - 1, 2)
                if i == 5 and prev:
                    gate_out("wo1", b - 1, 2)
                if i == 5 and nxt:
                    low_keys(b + 1, 1)
                if i == 7 and nxt:
                    global_shift(b + 1)
                if i == 6 and nxt:
                    low_queries(b + 1, 0)
                if i == 6 and known_below(b, NB - 2):
                    statistics(b + 2, 0)

            def iteration(b, par):
                if not isinstance(b, int) or 1 <= b < NB - 1:
                    steps["at"] = DVE_BEFORE + DVE_FIRST + DVE_STEPS * (b - 1)
                for i in range(ITEMS):
                    if known_below(b, NB):
                        shift_scores(b, i)
                        if i == 0:
                            global_inverse(b)
                    if (at := lagging(b, i, 1)) is not None:
                        invert_sums(*at)
                    slot_steps(b, par, i)
                    if isinstance(b, int) and b == NB:
                        if i == 1:
                            magnitudes()
                        if i == 2:
                            mean_w1()
                            first_unit_statistics()
                        if i == 4:
                            normalise_first_unit()
                        if i == 5:
                            dve.wait_ge(alpha2_full, 1)
                            nc.vector.tensor_copy(ffn.alpha2, score[0][:, 0:E]).then_inc(alpha2_ready, 1)
                    if isinstance(b, int) and b == NB - 1:
                        if i == 4:
                            modulate_mix()
                        if i == 5:
                            take_global_values()
                        if i == 6:
                            finish_tokens()

            nc.vector.memset(q_diag[:].bitcast(F32), 0.0)
            nc.vector.memset(ones_row, 1.0)
            nc.vector.memset(neg_half[:], -0.5).then_inc(constants_ready, 1)
            statistics(0, 0)
            dve.wait_ge(silu_exp, 1)
            nc.vector.tensor_scalar_add(c_e[:], c_e[:], 1.0).then_inc(dve_step, 1)
            dve.wait_ge(dve_step, step())
            nc.vector.reciprocal(c_e[:], c_e[:]).then_inc(dve_step, 1)
            dve.wait_ge(dve_step, step())
            nc.vector.tensor_tensor(c_s[:], c_e[:], c_t[:], ALU.mult).then_inc(silu_ready, 1)
            statistics(0, 1)
            global_statistics()
            normalise(0, 0)
            dve.wait_ge(mod_full, 1)
            mods = turned[0][:, 0:4 * EC * NB].rearrange("p (j n) -> p j n", j=4)
            flat = modt[:].rearrange("p j c b -> p j (c b)")
            nc.vector.tensor_copy(flat[:, SA:CB:2, :], mods[:, SA:CB:2, :])
            nc.vector.tensor_scalar_add(flat[:, CA:CB + 1:2, :], mods[:, CA:CB + 1:2, :], 1.0).then_inc(dve_step, 1)
            dve.wait_ge(dve_step, step())
            pick_modulation(0, 0)
            normalise(0, 1)
            normalise_tokens()
            dve.wait_ge(setup_loaded, 16 * 11)
            for which, src in ((WK, w_k), (WQ, w_q[:]), (WV, w_v[:]), (WO, w_o)):
                nc.vector.tensor_copy(w_hi[:, which, :, :], src).then_inc(dve_step, 1)
                dve.wait_ge(dve_step, step())
                nc.vector.tensor_tensor(w_lo[:, which, :, :], src, w_hi[:, which, :, :].bitcast(F32), ALU.subtract)
            nc.vector.tensor_copy(bias_parts[:, 0, :], bias_o[0:1, :])
            nc.vector.tensor_copy(ones_r[:], ones_row).then_inc(dve_step, 1)
            dve.wait_ge(dve_step, step())
            nc.vector.tensor_tensor(bias_parts[:, 1, :], bias_o[0:1, :], bias_parts[:, 0, :].bitcast(F32),
                                    ALU.subtract).then_inc(weights_ready, 1)
            modulate_tokens()
            dve.wait_ge(gates_full, 1)
            raw = turned[1][0:NB, :]
            nc.vector.tensor_scalar(gate_sign, raw, 0.0, 2.0, ALU.is_ge, ALU.mult)
            nc.vector.tensor_scalar_mul(gate_rows, raw, -1.0).then_inc(dve_step, 1)
            dve.wait_ge(dve_step, step())
            nc.vector.scalar_tensor_tensor(gate_rows, gate_rows, 0.25, raw, ALU.max, ALU.max).then_inc(dve_step, 1)
            dve.wait_ge(dve_step, step())
            nc.vector.scalar_tensor_tensor(gate_rows, gate_sign, 1.0, gate_rows, ALU.subtract,
                                           ALU.mult).then_inc(gates_ready, 1)
            low_keys(0, 0)
            low_keys(0, 1)
            take_queries()
            take_directions()
            pick_keys(0, 0)
            low_queries(0, 0)
            global_shift(0)
            statistics(1, 0)
            assert steps["at"] == DVE_BEFORE, steps
            batches(dve, iteration)

        @block.gpsimd
        def _(pool):
            def power(b, half):
                pool.wait_ge(stats_ready, 2 * b + half + 1)
                if positive(2 * b - 1 + half):
                    pool.wait_ge(xn_ready, 2 * b - 1 + half)
                cols = slice(4 * half, 4 * half + 4)
                nc.gpsimd.tensor_tensor(rstd[:, cols], var_eps[:, cols], neg_half[:],
                                        ALU.pow).then_inc(rstd_ready, 1)

            def low_h(b, half, c):
                pool.wait_ge(stage_free, stage_count(b, 1 + 2 * half + c))
                cols = slice(half * HALF, (half + 1) * HALF)
                nc.gpsimd.tensor_tensor(h_lo[:, c, cols], h_full[:, c, :], h_hi[:, c, cols].bitcast(F32),
                                        ALU.subtract).then_inc(h_lo_ready, 1)

            def low_context(b, c):
                pool.wait_ge(ctx_hi_ready, 2 * b + c + 1)
                nc.gpsimd.tensor_tensor(ctx_lo[:, c, :], ctx_full[:], ctx_hi[:, c, :].bitcast(F32),
                                        ALU.subtract).then_inc(ctx_lo_ready, 1)

            def normalise_probs(b, i):
                pool.wait_ge(inv_ready, ITEMS * b + i + 1)
                rows = prob[:, i % 4, :].rearrange("q (h k) -> q h k", k=WIN)
                nc.gpsimd.tensor_tensor(rows, rows, row_inv[:, i % 2, :].unsqueeze(2).broadcast_to([P, 8, WIN]),
                                        ALU.mult).then_inc(prob_ready, 1)

            def gate_bias(b):
                pool.wait_ge(gate_loaded, 16 * b + 16)
                nc.gpsimd.tensor_tensor(gated_bias[:], bias_o[:], gate_now[:], ALU.mult).then_inc(res_added, 1)

            def add_bias(b):
                pool.wait_ge(res_added, 4 * b + 1)
                pool.wait_ge(x_res_loaded, 16 * N_ROLLED * (b + 1))
                part = x_res[:, 4:8, :]
                nc.gpsimd.tensor_tensor(part, part, gated_bias[:].unsqueeze(1).broadcast_to([P, 4, E]),
                                        ALU.add).then_inc(res_added, 1)

            def add_out(name, b, first, tiles):
                pool.wait_ge(small_free, small_count(name, b))
                pool.wait_ge(x_res_loaded, 16 * N_ROLLED * (b + 1))
                part = x_res[:, first:first + tiles, :].rearrange("p t e -> p (t e)")
                nc.gpsimd.tensor_tensor(part, part, attn_tmp[:, 0:tiles * E], ALU.add).then_inc(res_added, 1)

            def slot_steps(b, i):
                cur, prev, nxt = known_below(b, NB), known_from(b, 1), known_below(b, NB - 1)
                if i == 1 and nxt:
                    power(b + 1, 1)
                if i == 1 and prev:
                    gate_bias(b - 1)
                if i == 2 and prev:
                    low_context(b - 1, 1)
                if i in (2, 3) and nxt:
                    low_h(b + 1, i - 2, 0)
                    low_h(b + 1, i - 2, 1)
                if i == 3 and prev:
                    add_bias(b - 1)
                if isinstance(b, int) and b == NB and i == 4:
                    pool.wait_ge(first.stats_ready, 1)
                    nc.gpsimd.tensor_tensor(first.rstd, first.var_eps, neg_half[:],
                                            ALU.pow).then_inc(first.rstd_ready, 1)
                if i == 4 and prev:
                    add_out("wo0", b - 1, 0, 2)
                if i == 5 and prev:
                    add_out("wo1", b - 1, 2, 2)
                if i == 6 and known_below(b, NB - 2):
                    power(b + 2, 0)
                if i == 7 and cur:
                    low_context(b, 0)

            def iteration(b, par):
                for i in range(ITEMS):
                    if (at := lagging(b, i, 1)) is not None:
                        normalise_probs(*at)
                    slot_steps(b, i)

            nc.gpsimd.memset(k_diag[0][:].bitcast(F32), 0.0).then_inc(zeroed, 1)
            pool.wait_ge(constants_ready, 1)
            power(0, 0)
            power(0, 1)
            pool.wait_ge(g_var_ready, 1)
            nc.gpsimd.tensor_tensor(g_rstd[:], g_var_eps[:], neg_half[0:NB, 0:1], ALU.pow).then_inc(g_rstd_ready, 1)
            nc.gpsimd.memset(late[:].bitcast(F32), 0.0).then_inc(zeroed, 1)
            low_h(0, 0, 0)
            low_h(0, 0, 1)
            low_h(0, 1, 0)
            low_h(0, 1, 1)
            pool.wait_ge(gates_full, 1)
            nc.gpsimd.memset(v_diag[:], 0.0).then_inc(v_zeroed, 1)
            power(1, 0)
            batches(pool, iteration)


def phase_b(nc, psum, ident, modt, neg_half, x_pair, h_full, first, ffn, x1_stored, x_in_loaded, gates, x1, out):
    units = NB * L // TOK
    DOWN_AT = (2, 4, 6, 7)
    x1_units, out_units = ffn_units(x1), ffn_units(out)

    with ExitStack() as ctx:
        def sb(name, shape, dt=F32):
            return ctx.enter_context(nc.sbuf_tensor(name, shape, dt))

        def sem(name):
            return ctx.enter_context(nc.semaphore(name))

        x_in = x_pair[:].rearrange("p (u t) e -> p u t e", u=2)
        alpha1, bias1, alpha2, bias2 = ffn.alpha1, ffn.bias1, ffn.alpha2, ffn.bias2
        w1_sign, w2_sign = ffn.w1_sign, ffn.w2_sign
        stats, mean_var, var_eps, rstd = first.stats, first.mean_var, first.var_eps, first.rstd
        f_stats_ready, f_rstd_ready, f_xn_ready = first.stats_ready, first.rstd_ready, first.xn_ready
        x_n = h_full[:].rearrange("p h (t e) -> p (h t) e", e=E)
        mod_now = sb("f_mod_now", [P, 2, 2, EC])
        gate_now = sb("f_gate_now", [P, 2, E])
        out_scale = sb("out_scale", [P, 2, E])
        out_bias = sb("out_bias", [P, E])
        h_new = sb("f_h_new", [P, EC, TOK])
        h_hi = sb("f_h_hi", [P, 2, EC, TOK], F32R)
        h_lo = sb("f_h_lo", [P, 2, EC, TOK], F32R)
        g_full = sb("g_full", [P, 2, TOK])
        act_hi = sb("act_hi", [P, 2, FC, TOK], F32R)
        act_lo = sb("act_lo", [P, 2, FC, TOK], F32R)
        y_tmp = sb("y_tmp", [P, 2, E])
        y = sb("y", [P, 2, TT, E])

        hidden = psum[0:4]
        turned = psum[4:6]
        result = psum[6:8]

        f_gate_loaded = [sem(f"f_gate_loaded{i}") for i in range(2)]
        y_stored = [sem(f"y_stored{i}") for i in range(2)]
        f_step = sem("f_step")
        f_mod_ready = sem("f_mod_ready")
        f_turned_full = sem("f_turned_full")
        f_h_hi_ready = sem("f_h_hi_ready")
        f_h_lo_ready = sem("f_h_lo_ready")
        hidden_full = sem("hidden_full")
        gelu_done = sem("gelu_done")
        act_lo_ready = sem("act_lo_ready")
        result_full = sem("result_full")
        scaled = sem("scaled")
        y_started = sem("y_started")
        y_ready = sem("y_ready")
        scale_ready = sem("scale_ready")
        out_bias_ready = sem("out_bias_ready")

        def moved_before(v, par):
            return 8 * (v - par)

        def over_units(engine, iteration):
            iteration(0, 0, 0)
            iteration(1, 1, 0)
            with engine.Fori(1, (units - 2) // 2) as it:
                iteration(it * 2, 0, it)
                iteration(it * 2 + 1, 1, it)
            for v in range(units - 2, units + 1):
                iteration(v, v % 2, v // 2)

        block = ctx.enter_context(nc.Block())

        @block.sync
        def _(sp):
            def load(v, par, batch):
                src = x1_units[v] if isinstance(v, int) else x1_units[bass.ds(v, 1)].rearrange(
                    "u p t e -> (u p) t e")
                sp.dma_start(x_in[:, par, :, :], src).then_inc(x_in_loaded[par], 16)
                load_gate(par, batch)

            def load_gate(par, batch):
                row = gates[batch:batch + 1, E:2 * E] if isinstance(batch, int) else gates[bass.ds(batch, 1), E:2 * E]
                sp.dma_start(gate_now[:, par, :], row.broadcast_to([P, E])).then_inc(f_gate_loaded[par], 16)

            for v in range(2):
                load_gate(v, 0)
            sp.wait_ge(x1_stored, 16 * X1_STORES * NB)

            def iteration(v, par, batch):
                if known_below(v, units - 2):
                    sp.wait_ge(y_started, v + 1)
                    load(v + 2, par, batch + 1)
                if isinstance(v, int) and v == units:
                    for lo, hi in ((0, TT - 1), (TT - 1, TT)):
                        sp.wait_ge(y_ready, TT * (v - 1) + hi)
                        sp.dma_start(out_units[v - 1][:, lo:hi, :], y[:, 1 - par, lo:hi, :]).then_inc(
                            y_stored[1 - par], 16)
                elif known_from(v, 1):
                    sp.wait_ge(y_ready, TT * v)
                    dst = out_units[v - 1] if isinstance(v, int) else out_units[bass.ds(v - 1, 1)].rearrange(
                        "u p t e -> (u p) t e")
                    sp.dma_start(dst, y[:, 1 - par, :, :]).then_inc(y_stored[1 - par], 16)

            over_units(sp, iteration)
            sp.wait_ge(y_stored[0], 16 * units // 2)
            sp.wait_ge(y_stored[1], 16 * (units // 2 + 1))

        @block.tensor
        def _(pe):
            def turn_x(v, c):
                pe.wait_ge(f_xn_ready, v + 1)
                if positive(2 * v + c - 1):
                    pe.wait_ge(f_h_hi_ready, 2 * v + c - 1)
                for t in range(TT):
                    done = nc.tensor.transpose(turned[c][:, t * P:(t + 1) * P], x_n[:, t, c * P:(c + 1) * P],
                                               ident[:])
                done.then_inc(f_turned_full, 1)

            def up(v, par, f):
                if f == 0:
                    pe.wait_ge(f_h_hi_ready, 2 * v + 2)
                    pe.wait_ge(f_h_lo_ready, 2 * v + 2)
                if positive(FC * v + f - 3):
                    pe.wait_ge(gelu_done, FC * v + f - 3)
                for e in range(EC):
                    for h in (h_hi, h_lo):
                        done = nc.tensor.matmul(hidden[f % 4][:], w1_sign[:, e, f * P:(f + 1) * P],
                                                h[:, par, e, :], start=e == 0 and h is h_hi,
                                                stop=e == EC - 1 and h is h_lo)
                done.then_inc(hidden_full, 1)

            def down(v, par, t):
                pe.wait_ge(act_lo_ready, FC * v + FC)
                if positive(TT * v + t - 1):
                    pe.wait_ge(scaled, TT * v + t - 1)
                for f in range(FC):
                    for a in (act_hi, act_lo):
                        done = nc.tensor.matmul(result[t % 2][:, 0:E], a[:, par, f, t * P:(t + 1) * P],
                                                w2_sign[:, f, :], start=f == 0 and a is act_hi,
                                                stop=f == FC - 1 and a is act_lo)
                done.then_inc(result_full, 1)

            def iteration(v, par, batch):
                cur, prev = known_below(v, units), known_from(v, 1)
                for f in range(FC):
                    if cur:
                        up(v, par, f)
                    if f in DOWN_AT and prev:
                        down(v - 1, 1 - par, DOWN_AT.index(f))
                    if f in (3, 4) and known_below(v, units - 1):
                        turn_x(v + 1, f - 3)

            turn_x(0, 0)
            turn_x(0, 1)
            over_units(pe, iteration)

        @block.scalar
        def _(act):
            def modulate(v, par, c):
                act.wait_ge(f_turned_full, 2 * v + c + 1)
                act.wait_ge(f_mod_ready, v + 1)
                if positive(2 * v + c - 1):
                    act.wait_ge(f_h_lo_ready, 2 * v + c - 1)
                shift, scale = mod_now[:, par, 0, c:c + 1], mod_now[:, par, 1, c:c + 1]
                nc.scalar.activation(h_new[:, c, :], turned[c][:], ACT.Identity, scale=scale, bias=shift)
                nc.scalar.activation(h_hi[:, par, c, :], turned[c][:], ACT.Identity, scale=scale,
                                     bias=shift).then_inc(f_h_hi_ready, 1)

            def gelu(v, par, f):
                act.wait_ge(hidden_full, FC * v + f + 1)
                if positive(FC * v + f - 1):
                    act.wait_ge(act_lo_ready, FC * v + f - 1)
                if f == 0:
                    if positive(TT * v - TT):
                        act.wait_ge(result_full, TT * v - TT)
                done = nc.scalar.activation(g_full[:, f % 2, :], hidden[f % 4][:], ACT.Gelu,
                                            scale=alpha1[:, f:f + 1], bias=bias1[:, f:f + 1])
                if f % 2 == 0:
                    done = nc.scalar.activation(act_hi[:, par, f, :], hidden[f % 4][:], ACT.Gelu,
                                                scale=alpha1[:, f:f + 1], bias=bias1[:, f:f + 1])
                done.then_inc(gelu_done, 1)

            def iteration(v, par, batch):
                for f in range(FC):
                    if known_below(v, units):
                        gelu(v, par, f)
                    if f in (3, 4) and known_below(v, units - 1):
                        modulate(v + 1, 1 - par, f - 3)

            modulate(0, 0, 0)
            modulate(0, 0, 1)
            over_units(act, iteration)

        @block.vector
        def _(dve):
            steps = {"at": 0}

            def step():
                steps["at"] = steps["at"] + 1
                return steps["at"]

            def statistics(v, par):
                dve.wait_ge(x_in_loaded[par], moved_before(v, par) + 16)
                for t in range(TT):
                    done = nc.vector.bn_stats(stats[:, t, :], x_in[:, par, t, :])
                done.then_inc(f_step, 1)
                dve.wait_ge(f_step, step())
                nc.vector.memset(var_eps, EPS)
                for t in range(TT):
                    done = nc.vector.bn_aggr(mean_var[:, t, :], stats[:, t, :])
                done.then_inc(f_step, 1)
                dve.wait_ge(f_step, step())
                nc.vector.tensor_tensor(var_eps, var_eps, mean_var[:, :, 1], ALU.add).then_inc(f_stats_ready, 1)

            def normalise(v, par):
                dve.wait_ge(f_rstd_ready, v + 1)
                if positive(2 * v):
                    dve.wait_ge(f_turned_full, 2 * v)
                for t in range(TT):
                    done = nc.vector.tensor_scalar(x_n[:, t, :], x_in[:, par, t, :], mean_var[:, t, 0:1],
                                                   rstd[:, t:t + 1], ALU.subtract, ALU.mult)
                done.then_inc(f_xn_ready, 1)

            def pick_modulation(v, par, batch):
                src = modt[:, SB:CB + 1, :, batch:batch + 1] if isinstance(batch, int) else modt[
                    :, SB:CB + 1, :, bass.ds(batch, 1)]
                nc.vector.tensor_copy(mod_now[:, par, :, :],
                                      src.rearrange("p j c b -> p j (c b)")).then_inc(f_mod_ready, 1)

            def low_activation(v, par, f):
                dve.wait_ge(gelu_done, FC * v + f + 1)
                if f % 2 == 1:
                    nc.vector.tensor_copy(act_hi[:, par, f, :], g_full[:, f % 2, :]).then_inc(f_step, 1)
                    dve.wait_ge(f_step, step())
                nc.vector.tensor_tensor(act_lo[:, par, f, :], g_full[:, f % 2, :],
                                        act_hi[:, par, f, :].bitcast(F32), ALU.subtract).then_inc(act_lo_ready, 1)

            def scale_result(v, par, t):
                dve.wait_ge(result_full, TT * v + t + 1)
                if positive(TT * v + t - 1):
                    dve.wait_ge(y_ready, TT * v + t - 1)
                if t == 0:
                    dve.wait_ge(scale_ready, v + 1)
                nc.vector.tensor_tensor(y_tmp[:, t % 2, :], result[t % 2][:, 0:E], out_scale[:, par, :],
                                        ALU.mult).then_inc(scaled, 1)

            def iteration(v, par, batch):
                if not isinstance(v, int) or 1 <= v < units - 1:
                    steps["at"] = F_BEFORE + F_STEPS * v
                cur, prev, nxt = known_below(v, units), known_from(v, 1), known_below(v, units - 1)
                for f in range(FC):
                    if cur:
                        low_activation(v, par, f)
                    if f in DOWN_AT and prev:
                        scale_result(v - 1, 1 - par, DOWN_AT.index(f))
                    if f == 0 and nxt:
                        pick_modulation(v + 1, 1 - par, batch + 1 if par else batch)
                    if f == 1 and nxt:
                        normalise(v + 1, 1 - par)
                    if f == 6 and known_below(v, units - 2):
                        statistics(v + 2, par)

            pick_modulation(0, 0, 0)
            statistics(1, 1)
            assert steps["at"] == F_BEFORE, steps
            over_units(dve, iteration)

        @block.gpsimd
        def _(pool):
            def power(v):
                pool.wait_ge(f_stats_ready, v + 1)
                if positive(v):
                    pool.wait_ge(f_xn_ready, v)
                nc.gpsimd.tensor_tensor(rstd, var_eps, neg_half[:], ALU.pow).then_inc(f_rstd_ready, 1)

            def low_h(v, par, c):
                pool.wait_ge(f_h_hi_ready, 2 * v + c + 1)
                nc.gpsimd.tensor_tensor(h_lo[:, par, c, :], h_new[:, c, :], h_hi[:, par, c, :].bitcast(F32),
                                        ALU.subtract).then_inc(f_h_lo_ready, 1)

            def start_y(v, par):
                pool.wait_ge(f_gate_loaded[par], moved_before(v, par) + 16)
                pool.wait_ge(x_in_loaded[par], moved_before(v, par) + 16)
                if positive(TT * v - TT):
                    pool.wait_ge(scaled, TT * v - TT)
                nc.gpsimd.tensor_tensor(out_scale[:, par, :], alpha2, gate_now[:, par, :],
                                        ALU.mult).then_inc(scale_ready, 1)
                nc.gpsimd.tensor_tensor(out_bias[:], bias2, gate_now[:, par, :], ALU.mult).then_inc(
                    out_bias_ready, 1)
                pool.wait_ge(out_bias_ready, v + 1)
                if known_from(v, 2):
                    pool.wait_ge(y_stored[par], moved_before(v, par))
                nc.gpsimd.tensor_tensor(y[:, par, :, :], x_in[:, par, :, :],
                                        out_bias[:].unsqueeze(1).broadcast_to([P, TT, E]),
                                        ALU.add).then_inc(y_started, 1)

            def add_result(v, par, t):
                pool.wait_ge(scaled, TT * v + t + 1)
                pool.wait_ge(y_started, v + 1)
                nc.gpsimd.tensor_tensor(y[:, par, t, :], y[:, par, t, :], y_tmp[:, t % 2, :],
                                        ALU.add).then_inc(y_ready, 1)

            def iteration(v, par, batch):
                cur, prev, nxt = known_below(v, units), known_from(v, 1), known_below(v, units - 1)
                for f in range(FC):
                    if f == 7 and known_below(v, units - 2):
                        power(v + 2)
                    if f in DOWN_AT and prev:
                        add_result(v - 1, 1 - par, DOWN_AT.index(f))
                    if f in (3, 4) and nxt:
                        low_h(v + 1, 1 - par, f - 3)
                    if f == 2 and cur:
                        start_y(v, par)

            low_h(0, 0, 0)
            low_h(0, 0, 1)
            power(1)
            over_units(pool, iteration)



_X = "L0_attn_hidden_states"


def kernel(**inputs):
    import numpy as np
    import concourse.bacc as bacc
    from concourse.bass_utils import run_bass_kernel_spmd

    a = {name: np.ascontiguousarray(value) for name, value in inputs.items()}
    heads = np.zeros((P, EC, H), np.float32)
    for c in range(EC):
        for p in range(P):
            heads[p, c, (c * P + p) // D] = 1.0
    def by_partition(v):
        return np.ascontiguousarray(v.reshape(-1, P).T)

    laid = {
        "x": a[_X],
        "wq": a["L0_attn_Wq"], "bq": by_partition(a["L0_attn_bq"]),
        "wk": a["L0_attn_Wk"], "bk": by_partition(a["L0_attn_bk"]),
        "wv": a["L0_attn_Wv"], "bv": by_partition(a["L0_attn_bv"]), "wo": a["L0_attn_Wo"], "bo": a["L0_attn_bo"],
        "w1": a["L0_ffn_w1"], "w1t": np.ascontiguousarray(a["L0_ffn_w1"].T), "b1": by_partition(a["L0_ffn_b1"]),
        "w2t": np.ascontiguousarray(a["L0_ffn_w2"].T), "b2": a["L0_ffn_b2"],
        "ct": np.ascontiguousarray(a["L0_c"].T), "wmod": a["L0_wmod"],
        "wkt": np.ascontiguousarray(a["L0_attn_Wk"].T), "ident": np.eye(P, dtype=np.float32), "heads": heads,
    }
    nc = bacc.Bacc("TRN2", target_bir_lowering=False, num_devices=1)
    args = [nc.dram_tensor(f"in_{n}", v.shape, F32, kind="ExternalInput").ap() for n, v in laid.items()]
    out = nc.dram_tensor("out", (NB, L, E), F32, kind="ExternalOutput").ap()
    adaln_block(nc, *args, out)
    result = run_bass_kernel_spmd(nc, [{f"in_{n}": v for n, v in laid.items()}], core_ids=[0])
    return result.results[0]["out"]
```
